# Optimizing a Trainium2 kernel written in Bass

```python
import numpy as np
import jax
import jax.numpy as jnp

def _softmax(x, axis=-1):
    return jax.nn.softmax(x, axis=axis)

def _gelu(x):
    return jax.nn.gelu(x, approximate=True)

def _silu(x):
    return jax.nn.silu(x)

def _sigmoid(x):
    return jax.nn.sigmoid(x)

def _layernorm(x, axis=-1, eps=1e-05):
    m = jnp.mean(x, axis=axis, keepdims=True)
    v = jnp.var(x, axis=axis, keepdims=True)
    return (x - m) / jnp.sqrt(v + eps)

def _scatter_add(tgt, idx, src, axis=0):
    return tgt.at[idx].add(src)

def _segment_sum(src, seg, n):
    return jax.ops.segment_sum(src, seg, n)
kernel_name = 'mk_xattn_ffn_d2_seqx_r4_a6fc45'

def setup_inputs(seed: int=0):
    np.random.seed(seed)
    _w = jnp.asarray

    def _rec_inputs():
        import jax
        import jax.numpy as jnp
        _rk = jax.random.key(seed)
        x = 7.22e-05 + 1 * jax.random.normal(jax.random.fold_in(_rk, 1), (16, 112, 256), jnp.float32)
        _lenS = 112 - jax.random.randint(jax.random.fold_in(_rk, 7), (16,), 0, max(1, 112 // 4) + 1, jnp.int32)
        _lenS2 = 375 - jax.random.randint(jax.random.fold_in(_rk, 8), (16,), 0, max(1, 375 // 4) + 1, jnp.int32)
        _ctx_1024P = jax.random.normal(jax.random.fold_in(_rk, 11), (16, 16, 256), jnp.float32)
        _ctx_1024c = jax.random.dirichlet(jax.random.fold_in(_rk, 511), 0.3 * jnp.ones((16,), jnp.float32), (16, 375))
        _ctx_1024t = jnp.einsum('bsk,bkd->bsd', _ctx_1024c, _ctx_1024P)
        _ctx_1024t = _ctx_1024t * jax.lax.rsqrt(jnp.mean(jnp.square(_ctx_1024t)) + 1e-12) * 0.953939
        ctx_1024 = 4.13588e-05 + 0.999923 * (_ctx_1024t + 0.3 * jax.random.normal(jax.random.fold_in(_rk, 611), (16, 375, 256), jnp.float32))
        _validS = jnp.arange(112)[None, :] < _lenS[:, None]
        _validS2 = jnp.arange(375)[None, :] < _lenS2[:, None]
        _causal = jnp.tril(jnp.ones((112, 112), dtype=bool))
        mask_BxSxS2_bk1 = jnp.broadcast_to(_validS2[:, None, :], (16, 112, 375))
        return (x, ctx_1024, mask_BxSxS2_bk1)
    x, ctx_1024, mask_BxSxS2_bk1 = _rec_inputs()

    def _L0_xattn_setup():
        import jax, jax.numpy as jnp
        import numpy as np
        B, S, D, H = (4, 512, 256, 16)
        DK = D // H
        key = jax.random.key(seed)
        ks = jax.random.split(key, 12)
        sc = 0.02
        return {'q': jax.random.normal(ks[0], (B, S, D), jnp.float32), 'k': jax.random.normal(ks[1], (B, S, D), jnp.float32), 'v': jax.random.normal(ks[2], (B, S, D), jnp.float32), 'mask': jax.random.randint(ks[3], (B, S, S), 0, 2).astype(bool), 'Wq': jax.random.normal(ks[4], (H, D, DK), jnp.float32) * sc, 'bq': jax.random.normal(ks[5], (H, DK), jnp.float32) * sc, 'Wk': jax.random.normal(ks[6], (H, D, DK), jnp.float32) * sc, 'bk': jax.random.normal(ks[7], (H, DK), jnp.float32) * sc, 'Wv': jax.random.normal(ks[8], (H, D, DK), jnp.float32) * sc, 'bv': jax.random.normal(ks[9], (H, DK), jnp.float32) * sc, 'Wo': jax.random.normal(ks[10], (D, D), jnp.float32) * sc, 'bo': jax.random.normal(ks[11], (D,), jnp.float32) * sc}
    _L0_xattn_all = _L0_xattn_setup()
    _L0_xattn_in = {k: v for k, v in _L0_xattn_all.items() if k in ('Wq', 'bq', 'Wk', 'bk', 'Wv', 'bv', 'Wo', 'bo')}
    del _L0_xattn_all

    def _L0_ffn_setup():
        import jax, jax.numpy as jnp
        import numpy as np
        D_MODEL = 256
        D_FF = 1024
        N_EXPERTS = 8
        D_EXPERT = D_FF // N_EXPERTS
        TOP_K = 2
        LB_WEIGHT = 0.01
        B, S = (4, 512)

        def _top_k_softmax(logits, k):
            vals, _ = jax.lax.top_k(logits, k)
            thresh = vals[..., -1:]
            masked = jnp.where(logits >= thresh, logits, -jnp.inf)
            return jax.nn.softmax(masked, axis=-1)
        key = jax.random.key(seed)
        ks = jax.random.split(key, 8)
        x = jax.random.normal(ks[0], (B, S, D_MODEL), dtype=jnp.float32)
        w1 = jax.random.normal(ks[1], (N_EXPERTS, D_MODEL, D_EXPERT), dtype=jnp.float32) * (1.0 / np.sqrt(D_MODEL))
        b1 = jnp.zeros((N_EXPERTS, D_EXPERT), dtype=jnp.float32)
        w2 = jax.random.normal(ks[2], (N_EXPERTS, D_EXPERT, D_MODEL), dtype=jnp.float32) * (1.0 / np.sqrt(D_EXPERT))
        b2 = jnp.zeros((N_EXPERTS, D_MODEL), dtype=jnp.float32)
        centroids = jax.random.normal(ks[3], (N_EXPERTS, D_MODEL), dtype=jnp.float32) * 0.02
        w_route = jax.random.normal(ks[4], (N_EXPERTS, D_MODEL), dtype=jnp.float32) * (1.0 / np.sqrt(D_MODEL))
        return {'x': x, 'w1': w1, 'b1': b1, 'w2': w2, 'b2': b2, 'centroids': centroids, 'w_route': w_route}
    _L0_ffn_all = _L0_ffn_setup()
    _L0_ffn_in = {k: v for k, v in _L0_ffn_all.items() if k in ('w1', 'b1', 'w2', 'b2', 'centroids', 'w_route')}
    del _L0_ffn_all

    def _L1_xattn_setup():
        import jax, jax.numpy as jnp
        import numpy as np
        D = 256
        NUM_ITERS = 3
        EPS = 1e-06
        SCALE = D ** (-0.5)

        def rmsnorm(x, w, eps=EPS):
            return x * jax.lax.rsqrt(jnp.mean(x * x, axis=-1, keepdims=True) + eps) * w

        def gru_cell(x, h, wih, whh, bih, bhh):
            gx = x @ wih.T + bih
            gh = h @ whh.T + bhh
            xr, xz, xn = jnp.split(gx, 3, axis=-1)
            hr, hz, hn = jnp.split(gh, 3, axis=-1)
            r = jax.nn.sigmoid(xr + hr)
            z = jax.nn.sigmoid(xz + hz)
            n = jnp.tanh(xn + r * hn)
            return (1.0 - z) * n + z * h
        key = jax.random.key(seed)
        ks = jax.random.split(key, 8)
        B, K, M, d = (8, 64, 1024, D)
        w_std = d ** (-0.5)
        return {'slots': jax.random.normal(ks[0], (B, K, d), jnp.float32), 'P': jax.random.normal(ks[1], (B, M, d), jnp.float32), 'Wq': jax.random.normal(ks[2], (d, d), jnp.float32) * w_std, 'Wk': jax.random.normal(ks[3], (d, d), jnp.float32) * w_std, 'Wv': jax.random.normal(ks[4], (d, d), jnp.float32) * w_std, 'gru_wih': jax.random.normal(ks[5], (3 * d, d), jnp.float32) * w_std, 'gru_whh': jax.random.normal(ks[6], (3 * d, d), jnp.float32) * w_std, 'gru_bih': jnp.zeros((3 * d,), jnp.float32), 'gru_bhh': jnp.zeros((3 * d,), jnp.float32), 'slot_norm_w': jnp.ones((d,), jnp.float32), 'input_norm_w': jnp.ones((d,), jnp.float32)}
    _L1_xattn_all = _L1_xattn_setup()
    _L1_xattn_in = {k: v for k, v in _L1_xattn_all.items() if k in ('Wq', 'Wk', 'Wv', 'gru_wih', 'gru_whh', 'gru_bih', 'gru_bhh', 'slot_norm_w', 'input_norm_w')}
    del _L1_xattn_all

    def _L1_ffn_setup():
        import jax, jax.numpy as jnp
        import numpy as np
        EPS = 1e-06
        N_EXPERTS = 8

        def _rms_norm(x, scale, eps=EPS):
            mean_sq = jnp.mean(x.astype(jnp.float32) ** 2, axis=-1, keepdims=True)
            s = scale.astype(jnp.float32) * jax.lax.rsqrt(mean_sq + eps)
            return x * s.astype(x.dtype)

        def _dist2(x, y):
            nx = jnp.sum(x ** 2, axis=-1)[..., :, None]
            ny = jnp.sum(y ** 2, axis=-1)[..., None, :]
            return nx + ny - 2.0 * (x @ y.T)
        key = jax.random.key(seed)
        ks = jax.random.split(key, 5)
        dim, hidden, E = (256, 512, N_EXPERTS)
        x = jax.random.normal(ks[0], (4, 512, dim), dtype=jnp.float32)
        scale = jnp.ones((dim,), dtype=jnp.float32)
        centroids = jax.random.normal(ks[1], (E, dim), dtype=jnp.float32)
        up_w = jax.random.normal(ks[2], (E, dim, hidden * 2), dtype=jnp.float32) * dim ** (-0.5)
        down_w = jax.random.normal(ks[3], (E, hidden, dim), dtype=jnp.float32) * hidden ** (-0.5)
        return {'x': x, 'scale': scale, 'centroids': centroids, 'up_w': up_w, 'down_w': down_w}
    _L1_ffn_all = _L1_ffn_setup()
    _L1_ffn_in = {k: v for k, v in _L1_ffn_all.items() if k in ('scale', 'centroids', 'up_w', 'down_w')}
    del _L1_ffn_all
    return {'x': x, 'ctx_1024': ctx_1024, 'mask_BxSxS2_bk1': mask_BxSxS2_bk1, 'L0_xattn_Wq': _L0_xattn_in['Wq'], 'L0_xattn_bq': _L0_xattn_in['bq'], 'L0_xattn_Wk': _L0_xattn_in['Wk'], 'L0_xattn_bk': _L0_xattn_in['bk'], 'L0_xattn_Wv': _L0_xattn_in['Wv'], 'L0_xattn_bv': _L0_xattn_in['bv'], 'L0_xattn_Wo': _L0_xattn_in['Wo'], 'L0_xattn_bo': _L0_xattn_in['bo'], 'L0_ffn_w1': _L0_ffn_in['w1'], 'L0_ffn_b1': _L0_ffn_in['b1'], 'L0_ffn_w2': _L0_ffn_in['w2'], 'L0_ffn_b2': _L0_ffn_in['b2'], 'L0_ffn_centroids': _L0_ffn_in['centroids'], 'L0_ffn_w_route': _L0_ffn_in['w_route'], 'L1_xattn_Wq': _L1_xattn_in['Wq'], 'L1_xattn_Wk': _L1_xattn_in['Wk'], 'L1_xattn_Wv': _L1_xattn_in['Wv'], 'L1_xattn_gru_wih': _L1_xattn_in['gru_wih'], 'L1_xattn_gru_whh': _L1_xattn_in['gru_whh'], 'L1_xattn_gru_bih': _L1_xattn_in['gru_bih'], 'L1_xattn_gru_bhh': _L1_xattn_in['gru_bhh'], 'L1_xattn_slot_norm_w': _L1_xattn_in['slot_norm_w'], 'L1_xattn_input_norm_w': _L1_xattn_in['input_norm_w'], 'L1_ffn_scale': _L1_ffn_in['scale'], 'L1_ffn_centroids': _L1_ffn_in['centroids'], 'L1_ffn_up_w': _L1_ffn_in['up_w'], 'L1_ffn_down_w': _L1_ffn_in['down_w']}

def reference(x, ctx_1024, mask_BxSxS2_bk1, L0_xattn_Wq, L0_xattn_bq, L0_xattn_Wk, L0_xattn_bk, L0_xattn_Wv, L0_xattn_bv, L0_xattn_Wo, L0_xattn_bo, L0_ffn_w1, L0_ffn_b1, L0_ffn_w2, L0_ffn_b2, L0_ffn_centroids, L0_ffn_w_route, L1_xattn_Wq, L1_xattn_Wk, L1_xattn_Wv, L1_xattn_gru_wih, L1_xattn_gru_whh, L1_xattn_gru_bih, L1_xattn_gru_bhh, L1_xattn_slot_norm_w, L1_xattn_input_norm_w, L1_ffn_scale, L1_ffn_centroids, L1_ffn_up_w, L1_ffn_down_w):
    import jax
    import jax.numpy as jnp

    def _L0_xattn_ref(q, k, v, mask, Wq, bq, Wk, bk, Wv, bv, Wo, bo):
        import jax, jax.numpy as jnp
        import numpy as np
        B, S, D, H = (4, 512, 256, 16)
        DK = D // H
        qh = jnp.einsum('bsd,hdk->bhsk', q, Wq) + bq[None, :, None, :]
        kh = jnp.einsum('bsd,hdk->bhsk', k, Wk) + bk[None, :, None, :]
        vh = jnp.einsum('bsd,hdk->bhsk', v, Wv) + bv[None, :, None, :]
        dk = qh.shape[-1]
        scores = jnp.einsum('bhsk,bhtk->bhst', qh, kh) / dk ** 0.5
        scores = jnp.where(mask[:, None, :, :], scores, jnp.float32(-1e-06))
        attn = jax.nn.softmax(scores, axis=-1)
        out = jnp.einsum('bhst,bhtk->bhsk', attn, vh)
        b, h, s, _ = out.shape
        out = out.transpose(0, 2, 1, 3).reshape(b, s, h * dk)
        return out @ Wo + bo

    def _L0_ffn_ref(x, w1, b1, w2, b2, centroids, w_route):
        import jax, jax.numpy as jnp
        import numpy as np
        D_MODEL = 256
        D_FF = 1024
        N_EXPERTS = 8
        D_EXPERT = D_FF // N_EXPERTS
        TOP_K = 2
        LB_WEIGHT = 0.01
        B, S = (4, 512)

        def _top_k_softmax(logits, k):
            vals, _ = jax.lax.top_k(logits, k)
            thresh = vals[..., -1:]
            masked = jnp.where(logits >= thresh, logits, -jnp.inf)
            return jax.nn.softmax(masked, axis=-1)
        eps = 1e-12
        x_norm = x / jnp.maximum(jnp.linalg.norm(x, axis=-1, keepdims=True), eps)
        c_norm = centroids / jnp.maximum(jnp.linalg.norm(centroids, axis=-1, keepdims=True), eps)
        cos_scores = jnp.einsum('bsd,ed->bse', x_norm, c_norm)
        route_scores = jnp.einsum('bsd,ed->bse', x, w_route)
        logits = cos_scores + route_scores
        gates = _top_k_softmax(logits, TOP_K)
        h = jax.nn.gelu(jnp.einsum('bsd,edh->bseh', x, w1) + b1, approximate=False)
        expert_out = jnp.einsum('bseh,ehd->bsed', h, w2) + b2
        out = jnp.einsum('bse,bsed->bsd', gates, expert_out)
        return out

    def _L1_xattn_ref(slots, P, Wq, Wk, Wv, gru_wih, gru_whh, gru_bih, gru_bhh, slot_norm_w, input_norm_w):
        import jax, jax.numpy as jnp
        import numpy as np
        D = 256
        NUM_ITERS = 3
        EPS = 1e-06
        SCALE = D ** (-0.5)

        def rmsnorm(x, w, eps=EPS):
            return x * jax.lax.rsqrt(jnp.mean(x * x, axis=-1, keepdims=True) + eps) * w

        def gru_cell(x, h, wih, whh, bih, bhh):
            gx = x @ wih.T + bih
            gh = h @ whh.T + bhh
            xr, xz, xn = jnp.split(gx, 3, axis=-1)
            hr, hz, hn = jnp.split(gh, 3, axis=-1)
            r = jax.nn.sigmoid(xr + hr)
            z = jax.nn.sigmoid(xz + hz)
            n = jnp.tanh(xn + r * hn)
            return (1.0 - z) * n + z * h
        Pn = rmsnorm(P, input_norm_w)
        k_proj = Pn @ Wk.T
        v_proj = Pn @ Wv.T
        for _ in range(NUM_ITERS):
            sn = rmsnorm(slots, slot_norm_w)
            q_proj = sn @ Wq.T
            scores = jnp.einsum('bkd,bmd->bkm', q_proj, k_proj) * SCALE
            attn = jax.nn.softmax(scores, axis=-2)
            attn = attn / (jnp.sum(attn, axis=-1, keepdims=True) + EPS)
            updates = jnp.einsum('bkm,bmd->bkd', attn, v_proj)
            slots = gru_cell(updates, slots, gru_wih, gru_whh, gru_bih, gru_bhh)
        return slots

    def _L1_ffn_ref(x, scale, centroids, up_w, down_w):
        import jax, jax.numpy as jnp
        import numpy as np
        EPS = 1e-06
        N_EXPERTS = 8

        def _rms_norm(x, scale, eps=EPS):
            mean_sq = jnp.mean(x.astype(jnp.float32) ** 2, axis=-1, keepdims=True)
            s = scale.astype(jnp.float32) * jax.lax.rsqrt(mean_sq + eps)
            return x * s.astype(x.dtype)

        def _dist2(x, y):
            nx = jnp.sum(x ** 2, axis=-1)[..., :, None]
            ny = jnp.sum(y ** 2, axis=-1)[..., None, :]
            return nx + ny - 2.0 * (x @ y.T)
        skip = x
        xn = _rms_norm(x, scale)
        ids = jnp.argmin(_dist2(xn, centroids), axis=-1)
        out = jnp.zeros_like(x)
        for e in range(N_EXPERTS):
            h = jnp.einsum('bsd,dh->bsh', xn, up_w[e])
            a, g = jnp.split(h, 2, axis=-1)
            y = jnp.einsum('bsh,hd->bsd', a * jax.nn.silu(g), down_w[e])
            out = jnp.where((ids == e)[..., None], y, out)
        return out + skip
    x = x + _L0_xattn_ref(_layernorm(x, axis=-1), ctx_1024, ctx_1024, mask_BxSxS2_bk1, L0_xattn_Wq, L0_xattn_bq, L0_xattn_Wk, L0_xattn_bk, L0_xattn_Wv, L0_xattn_bv, L0_xattn_Wo, L0_xattn_bo)
    x = x + _L0_ffn_ref(_layernorm(x, axis=-1), L0_ffn_w1, L0_ffn_b1, L0_ffn_w2, L0_ffn_b2, L0_ffn_centroids, L0_ffn_w_route)
    x = x + _L1_xattn_ref(_layernorm(x, axis=-1), ctx_1024, L1_xattn_Wq, L1_xattn_Wk, L1_xattn_Wv, L1_xattn_gru_wih, L1_xattn_gru_whh, L1_xattn_gru_bih, L1_xattn_gru_bhh, L1_xattn_slot_norm_w, L1_xattn_input_norm_w)
    x = x + _L1_ffn_ref(_layernorm(x, axis=-1), L1_ffn_scale, L1_ffn_centroids, L1_ffn_up_w, L1_ffn_down_w)
    return x

_drawn_inputs = setup_inputs


def setup_inputs(seed=0):
    import zlib

    import numpy as np

    out = dict(_drawn_inputs(seed))
    spreads = {'L0_ffn_b1': (0.0, 0.1),
     'L0_ffn_b2': (0.0, 0.1),
     'L1_xattn_gru_bih': (0.0, 0.1),
     'L1_xattn_gru_bhh': (0.0, 0.1),
     'L1_xattn_slot_norm_w': (1.0, 0.2),
     'L1_xattn_input_norm_w': (1.0, 0.2),
     'L1_ffn_scale': (1.0, 0.2)}
    factors = {'L0_xattn_Wq': 3.172, 'L0_xattn_bq': 23.009, 'L0_xattn_Wk': 3.16, 'L0_xattn_bk': 62.27}
    for name, (base, spread) in spreads.items():
        noise = np.random.default_rng([zlib.crc32(name.encode()), seed]).standard_normal(out[name].shape)
        drawn = base * np.exp(spread * noise) if base else spread * noise
        out[name] = jnp.asarray(drawn.astype(out[name].dtype))
    for name, factor in factors.items():
        out[name] = (out[name] * factor).astype(out[name].dtype)
    return out
```

```python
from contextlib import ExitStack

import concourse.bass as bass
from concourse import mybir

F32 = mybir.dt.float32
BF16 = mybir.dt.bfloat16
U8 = mybir.dt.uint8
U32 = mybir.dt.uint32
I32 = mybir.dt.int32
ALU = mybir.AluOpType
ACT = mybir.ActivationFunctionType
AX = mybir.AxisListType

B, S, D, KEYS = 16, 112, 256, 375
P = 128
DC = D // P
H, DK = 16, 16
HC = P // DK
KT = 3
KP = KEYS // KT
HP = 32
HG = H // 4
E0, F0 = 8, 128
E1, F1 = 8, 512
GB = 4
NG = B // GB
GN = GB * S
LN_EPS, RMS_EPS, SLOT_EPS = 1e-5, 1e-6, 1e-6
NORM_EPS = 1e-12
ROUNDS = 3
MASKED = -1e-6
MT = (B * S) // P + E1 - 1


class Sig:

    def __init__(self, sem, per=1):
        self.sem, self.per = sem, per

    def __call__(self, i, k):
        return self.sem, i * self.per + k


def phase_1(nc, ctx, a, t):
    def sb(name, shape, dt=F32):
        return ctx.enter_context(nc.sbuf_tensor(name, shape, dt))

    def psum(name, shape):
        return ctx.enter_context(nc.psum_tensor(name, shape, F32))

    def sem(name, per=1):
        return Sig(ctx.enter_context(nc.semaphore(name)), per)

    x_all, ident, xnT_all, gates_all = t["x_all"], t["ident"], t["xnT_all"], t["gates"]
    R = 4

    wq = sb("wq", [P, DC, D])
    wk = sb("wk", [P, DC, D])
    wv = sb("wv", [P, DC, D])
    wo = sb("wo", [P, HG, D])
    bq = sb("bq", [P, DC])
    bk = sb("bk", [P, DC])
    bv = sb("bv", [P, HG])
    bo = sb("bo", [1, D])
    bvb = sb("bvb", [P, HG, P])
    bvo = sb("bvo", [P, D])
    b2 = sb("b2", [E0, D])
    cent = sb("cent", [E0, D])
    csq = sb("csq", [E0, D])
    cn = sb("cn", [E0, 3])
    cr = sb("cr", [P, DC, 2 * E0])
    hmask = sb("hmask", [P, HC])
    ones = sb("ones", [P, P])
    mhalf = sb("mhalf", [P, 1])
    ctxT = [sb(f"ctxT{i}", [P, DC, KEYS]) for i in range(2)]
    mask8 = [sb(f"mask8_{i}", [S, KEYS], U8) for i in range(2)]
    maskf = [sb(f"maskf{i}", [S, KEYS]) for i in range(2)]
    kT = [sb(f"kT{i}", [P, DC, KEYS]) for i in range(2)]
    v = [sb(f"v{i}", [KP, KT, H, HP]) for i in range(2)]
    qm = [sb(f"qm{i}", [P, H, S]) for i in range(2)]
    nmax = [sb(f"nmax{i}", [S, H]) for i in range(2)]
    esum = [sb(f"esum{i}", [S, H]) for i in range(2)]
    st, mv, rstd = sb("st", [S, 6]), sb("mv", [S, 2]), sb("rstd", [S, 2])
    xn, xnT, qT = sb("xn", [S, D]), sb("xnT", [P, DC, S]), sb("qT", [P, DC, S])
    rec, recx = sb("rec", [S, H]), sb("recx", [S, H, HP])
    oT, oTn = sb("oT", [P, HG, S]), sb("oTn", [P, HG, S])
    st2, mv2, rs2 = sb("st2", [S, 6]), sb("mv2", [S, 2]), sb("rs2", [S, 6])
    xn2, xnT2 = sb("xn2", [S, D]), sb("xnT2", [P, DC, S])
    lg, lgt, top, keep = sb("lg", [S, 2 * E0]), sb("lgt", [S, E0]), sb("top", [S, 8]), sb("keep", [S, E0])
    ntop, eg, ek = sb("ntop", [S, 1]), sb("eg", [S, E0]), sb("ek", [S, E0])
    gs, gr, gate, gT = sb("gs", [S, 1]), sb("gr", [S, 1]), sb("gate", [S, E0]), sb("gT", [E0, S])
    sm = sb("sm", [S, R, KEYS])
    ex = sb("ex", [S, R, KEYS])
    eT = sb("eT", [KP, R, KT, S])

    ps = psum("ps", [P, 2, 512])
    pt = psum("pt", [P, 2, 512])
    po = psum("po", [P, 2, 512])
    pf = psum("pf", [P, 2, 512])

    NW = 11
    NF, NT = 6, 6
    w_in, x_in, w2_in = sem("w_in"), sem("x_in"), sem("w2_in")
    apart = sem("apart")
    made = sem("made")
    su_d, su_p, su_pe = sem("su_d"), sem("su_p"), sem("su_pe")
    loaded = [sem("loaded0", 32), sem("loaded1", 32)]
    conv = sem("conv")
    scored = sem("scored", H)
    masked = sem("masked", H)
    maxed = sem("maxed", H)
    exped = sem("exped", H)
    turned = sem("turned", H)
    eT_up = sem("eT_up", H)
    times_v = sem("times_v", H)
    f_pe, f_ev = sem("f_pe", NF), sem("f_ev", NF)
    t_pe, t_ev = sem("t_pe", NT), sem("t_ev", NT)
    f_d, f_p = sem("f_d", 3), sem("f_p", 3)
    qm_up = sem("qm_up", DC)
    t_d, t_p = sem("t_d", 13), sem("t_p", 9)
    t_a = sem("t_a", 1)
    oT_up = sem("oT_up", 1)

    PF = [("f", 0, 2), ("t", 0, 3), ("f", 1, 4), ("t", 1, 5), ("f", 2, 6), ("f", 3, 7), ("t", 2, 8),
          ("f", 4, 9), ("t", 3, 10), ("f", 5, 11), ("t", 4, 14), ("t", 5, 15)]
    BANK = {(k, n): i % 2 for i, (k, n, _) in enumerate(PF)}

    def last_use(k, n, b, prev, nxt):
        i = [u[:2] for u in PF].index((k, n))
        here = [u for j, u in enumerate(PF[:i]) if j % 2 == i % 2 and (nxt if u[0] == "f" else prev)]
        if here:
            kk, m, _ = here[-1]
            return f_ev(b + 1, m + 1) if kk == "f" else t_ev(b - 1, m + 1)
        static = isinstance(b, int)
        before = [u for j, u in enumerate(PF) if j % 2 == i % 2 and (u[0] == "f" or not (static and b <= 1))]
        kk, m, _ = before[-1]
        return f_ev(b, m + 1) if kk == "f" else t_ev(b - 2, m + 1)

    def fbank(k, n):
        return pf[:, BANK[(k, n)], :]

    def bodies(eng, body):
        body(0, 0, False, True)
        body(1, 1, True, True)
        with eng.Fori(1, B // 2 - 1) as j:
            body(2 * j, 0, True, True)
            body(2 * j + 1, 1, True, True)
        body(B - 2, 0, True, True)
        body(B - 1, 1, True, False)

    block = ctx.enter_context(nc.Block())

    @block.sync
    def _(sp):
        def load(b, par):
            sp.dma_start(ctxT[par][:], a["ctxT"][b].rearrange("(c p) m -> p c m", p=P)).then_inc(loaded[par].sem, 16)
            sp.dma_start(mask8[par][:], a["mask"][b]).then_inc(loaded[par].sem, 16)

        sp.dma_start(x_all[:], a["x"].rearrange("b s d -> s b d")).then_inc(x_in.sem, 16)
        load(0, 0)
        for dst, src in ((wq[:], a["wq"].rearrange("(c p) n -> p c n", p=P)),
                         (wk[:], a["wk"].rearrange("(c p) n -> p c n", p=P)),
                         (wv[:], a["wv"].rearrange("(c p) n -> p c n", p=P)),
                         (bq[:], a["bq"]),
                         (bk[:], a["bk"]),
                         (cent[:], a["cent"]),
                         (cr[:, :, E0:2 * E0], a["w_routeT"].rearrange("(c p) e -> p c e", p=P)),
                         (wo[:], a["wo"].rearrange("(c p) n -> p c n", p=P)),
                         (bv[:], a["bv"]),
                         (bo[:], a["bo"].rearrange("(o n) -> o n", o=1)),
                         (b2[:], a["b2"])):
            sp.dma_start(dst, src).then_inc(w_in.sem, 16)
        load(1, 1)
        sp.dma_start(t["w1"][:], a["w1"].rearrange("(c p) n -> p c n", p=P)).then_inc(w2_in.sem, 16)
        sp.dma_start(t["w2"][:], a["w2"].rearrange("e p n -> p e n")).then_inc(w2_in.sem, 16)
        sp.dma_start(t["b1"][:], a["b1"]).then_inc(w2_in.sem, 16)

        with sp.Fori(0, B // 2 - 1) as j:
            for par in range(2):
                sp.wait_ge(*f_pe(2 * j + par, NF))
                sp.sem_inc(apart.sem, 1)
                sp.wait_ge(*conv(2 * j + par, 1))
                sp.sem_inc(apart.sem, 1)
                load(2 * j + par + 2, par)
        sp.wait_ge(w2_in.sem, 48)

    @block.tensor
    def _(pe):
        def front(b, n, par):
            out = fbank("f", n)
            if n == 0:
                pe.wait_ge(*f_d(b, 3))
                for c in range(DC):
                    m = pe.transpose(out[:, c * S:(c + 1) * S], xn[:, c * P:(c + 1) * P], ident[:S, :S])
            elif n == 1:
                pe.wait_ge(*f_ev(b, 1))
                for o in range(DC):
                    for c in range(DC):
                        m = pe.matmul(out[:, o * S:(o + 1) * S], wq[:, c, o * P:(o + 1) * P], xnT[:, c, :],
                                      start=(c == 0), stop=(c == DC - 1))
            elif n in (2, 3):
                o = n - 2
                if n == 2:
                    pe.wait_ge(loaded[par].sem, 16 * (b - par) + 32)
                for c in range(DC):
                    m = pe.matmul(out[:, 0:KEYS], wk[:, c, o * P:(o + 1) * P], ctxT[par][:, c, :],
                                  start=(c == 0), stop=(c == DC - 1))
            else:
                for kt in ((0, 1) if n == 4 else (2,)):
                    for c in range(DC):
                        m = pe.matmul(out[:KP, kt % 2 * D:(kt % 2 + 1) * D], ctxT[par][:, c, kt * KP:(kt + 1) * KP],
                                      wv[:, c, :], start=(c == 0), stop=(c == DC - 1))
            m.then_inc(f_pe.sem, 1)

        def tail(b, n):
            out = fbank("t", n)
            if n == 0:
                pe.wait_ge(*t_p(b, 1))
                for g in range(HG):
                    m = pe.transpose(out[:, g * S:(g + 1) * S],
                                     recx[:, 4 * g:4 * g + 4, :].rearrange("s h p -> s (h p)"), ident[:S, :S])
            elif n == 1:
                pe.wait_ge(*t_ev(b, 1))
                for g in range(HG):
                    m = pe.matmul(out[:S, 0:D], oTn[:, g, :], wo[:, g, :], start=(g == 0), stop=(g == HG - 1))
            elif n == 2:
                pe.wait_ge(*t_d(b, 4))
                for c in range(DC):
                    m = pe.transpose(out[:, c * S:(c + 1) * S], xn2[:, c * P:(c + 1) * P], ident[:S, :S])
            elif n == 3:
                pe.wait_ge(*t_ev(b, 3))
                for c in range(DC):
                    m = pe.matmul(out[:S, 0:2 * E0], xnT2[:, c, :], cr[:, c, :], start=(c == 0), stop=(c == DC - 1))
            elif n == 4:
                pe.wait_ge(*t_d(b, 13))
                m = pe.transpose(out[:E0, 0:S], gate[:, :], ident[:S, :S])
            else:
                pe.wait_ge(*t_ev(b, 5))
                m = pe.matmul(out[:S, 0:D], gT[:, :], b2[:, :], start=True, stop=True)
            m.then_inc(t_pe.sem, 1)

        def score(b, s, par, ring_full):
            if ring_full:
                pe.wait_ge(*masked(b, s - 1))
            pe.matmul(ps[:S, s % 2, 0:KEYS], qm[par][:, s, :], kT[par][:, s // HC, :],
                      start=True, stop=True).then_inc(scored.sem, 1)

        def turn(b, s, ring_full):
            pe.wait_ge(*exped(b, s + 1))
            if ring_full:
                pe.wait_ge(*eT_up(b, s - 1))
            for kt in range(KT):
                m = pe.transpose(pt[:KP, s % 2, kt * S:(kt + 1) * S], ex[:, s % R, kt * KP:(kt + 1) * KP], ident[:S, :S])
            m.then_inc(turned.sem, 1)

        def attend(b, s, par, wait_out):
            hh = s % H
            g, j = hh // 4, hh % 4
            pe.wait_ge(*eT_up(b, s + 1))
            if wait_out:
                pe.wait_ge(*oT_up(b - 2, 1))
            for kt in range(KT):
                m = pe.matmul(po[j * HP:(j + 1) * HP, par, g * S:(g + 1) * S], v[par][:, kt, hh, :],
                              eT[:, s % R, kt, :], start=(kt == 0), stop=(kt == KT - 1))
            m.then_inc(times_v.sem, 1)

        def body(b, par, prev, nxt):
            pe.wait_ge(*qm_up(b, DC))
            pe.wait_ge(*f_ev(b, NF))
            for s in range(H):
                score(b, s, par, prev or s >= 2)
                if prev or s >= 2:
                    turn(b, s - 2, prev or s >= 4)
                if prev or s >= 3:
                    mine = s >= 3
                    attend(b, s - 3, par if mine else 1 - par, s == 3 and not (isinstance(b, int) and b < 2))
                for k, n, at in PF:
                    if at == s and (nxt if k == "f" else prev):
                        pe.wait_ge(*last_use(k, n, b, prev, nxt))
                        if k == "f":
                            front(b + 1, n, 1 - par)
                        else:
                            tail(b - 1, n)

        pe.wait_ge(made.sem, 6)
        pe.wait_ge(w_in.sem, 16 * NW)
        pe.wait_ge(su_d.sem, 2)
        for g in range(HG):
            pe.matmul(pf[:, 0, 0:D], bvb[:, g, :], wo[:, g, :], start=(g == 0), stop=False)
        pe.matmul(pf[:, 0, 0:D], ones[0:1, :], bo[:, :], start=False, stop=True)
        pe.wait_ge(su_d.sem, 3)
        for c in range(DC):
            m = pe.transpose(pf[:, 1, c * E0:(c + 1) * E0], csq[:, c * P:(c + 1) * P], ident[:E0, :E0])
        m.then_inc(su_pe.sem, 1)
        pe.wait_ge(su_d.sem, 5)
        pe.wait_ge(made.sem, 8)
        for n in range(NF):
            if n == 3:
                pe.wait_ge(*f_ev(0, 2))
            elif n == 2:
                pass
            elif n == 4:
                pe.wait_ge(*f_ev(0, 3))
            elif n == 5:
                pe.wait_ge(*f_ev(0, 4))
            if n:
                pe.wait_ge(*f_ev(0, n))
            front(0, n, 0)
        bodies(pe, body)
        last = B - 1
        for s in (H - 2, H - 1):
            turn(last, s, True)
            attend(last, s - 1, 1, False)
        attend(last, H - 1, 1, False)
        for n in range(NT):
            pe.wait_ge(*(t_ev(last, n) if n else t_ev(last - 1, NT)))
            tail(last, n)

    @block.scalar
    def _(act):
        def exp(b, s, par, ring_full):
            act.wait_ge(*maxed(b, s + 1))
            if ring_full:
                act.wait_ge(*turned(b, s - R + 1))
            act.activation(ex[:, s % R, :], sm[:, s % R, :], ACT.Exp, bias=nmax[par][:, s % H:s % H + 1],
                           accum_out=esum[par][:, s % H:s % H + 1]).then_inc(exped.sem, 1)

        def up(b, s, ring_full):
            act.wait_ge(*turned(b, s + 1))
            if ring_full:
                act.wait_ge(*times_v(b, s - R + 1))
            act.activation(eT[:, s % R, :, :].rearrange("p t s -> p (t s)"), pt[:KP, s % 2, 0:KT * S],
                           ACT.Copy).then_inc(eT_up.sem, 1)

        def o_up(b, par, first):
            act.wait_ge(*times_v(b, H))
            if not first:
                act.wait_ge(*t_ev(b - 1, 1))
            act.activation(oT[:, :, :].rearrange("p g s -> p (g s)"), po[:, par, 0:HG * S], ACT.Copy).then_inc(oT_up.sem, 1)

        def gate_exp(b):
            act.wait_ge(*t_d(b, 9))
            act.activation(eg[:], lgt[:], ACT.Exp, bias=ntop[:]).then_inc(t_a.sem, 1)

        def body(b, par, prev, nxt):
            for s in range(H):
                if prev or s >= 1:
                    exp(b, s - 1, par if s >= 1 else 1 - par, prev or s >= R + 1)
                if prev or s >= 2:
                    up(b, s - 2, prev or s >= R + 2)
                if prev and s == 3:
                    o_up(b - 1, 1 - par, isinstance(b, int) and b == 1)
                if prev and s == 12:
                    gate_exp(b - 1)

        bodies(act, body)
        last = B - 1
        exp(last, H - 1, 1, True)
        up(last, H - 2, True)
        up(last, H - 1, True)
        o_up(last, 1, False)
        gate_exp(last)

    @block.vector
    def _(dve):
        def mask_max(b, s, par, ring_full):
            if s == 0:
                dve.wait_ge(*conv(b, 1))
            dve.wait_ge(*scored(b, s + 1))
            if ring_full:
                dve.wait_ge(*exped(b, s - R + 1))
            dve.scalar_tensor_tensor(out=sm[:, s % R, :], in0=ps[:S, s % 2, 0:KEYS], scalar=-MASKED,
                                     in1=maskf[par][:], op0=ALU.add, op1=ALU.mult).then_inc(masked.sem, 1)
            dve.wait_ge(*masked(b, s + 1))
            dve.tensor_reduce(nmax[par][:, s:s + 1], sm[:, s % R, :], AX.X, ALU.max, negate=True).then_inc(maxed.sem, 1)

        def stats(b):
            dve.sem_inc(apart.sem, 1)
            dve.bn_stats(st[:], x_all[:, b, :]).then_inc(f_d.sem, 1)
            dve.wait_ge(*f_d(b, 1))
            dve.sem_inc(apart.sem, 1)
            dve.bn_aggr(mv[:], st[:]).then_inc(f_d.sem, 1)

        def normalise(b, first):
            dve.wait_ge(*f_p(b, 2))
            if not first:
                dve.wait_ge(*f_pe(b - 1, 1))
            dve.tensor_scalar(xn[:], x_all[:, b, :], mv[:, 0:1], rstd[:, 1:2], ALU.subtract, ALU.mult).then_inc(f_d.sem, 1)

        def front(b, n, par, first):
            src = fbank("f", n)
            dve.wait_ge(*f_pe(b, n + 1))
            if n == 0:
                m = dve.tensor_copy(xnT[:, :, :].rearrange("p c s -> p (c s)"), src[:, 0:DC * S])
            elif n == 1:
                if not first:
                    dve.wait_ge(*qm_up(b - 1, DC))
                for c in range(DC):
                    m = dve.tensor_scalar(qT[:, c, :], src[:, c * S:(c + 1) * S], bq[:, c:c + 1], DK ** -0.5,
                                          ALU.add, ALU.mult)
            elif n in (2, 3):
                m = dve.tensor_scalar(kT[par][:, n - 2, :], src[:, 0:KEYS], bk[:, n - 2:n - 1], None, ALU.add)
            elif n == 4:
                m = dve.tensor_copy(v[par][:, 0:2, :, 0:DK], src[:KP, 0:2 * D].rearrange("p (t h d) -> p t h d", t=2, h=H))
            else:
                m = dve.tensor_copy(v[par][:, 2, :, 0:DK], src[:KP, 0:D].rearrange("p (h d) -> p h d", h=H))
            m.then_inc(f_ev.sem, 1)

        def recip(b, par, first):
            dve.wait_ge(*exped(b, H))
            if not first:
                dve.wait_ge(*t_p(b - 1, 1))
            dve.reciprocal(rec[:], esum[par][:]).then_inc(t_d.sem, 1)

        def tail(b, n, first):
            src = fbank("t", n)
            dve.wait_ge(*t_pe(b, n + 1))
            if n == 0:
                dve.wait_ge(*oT_up(b, 1))
                if not first:
                    dve.wait_ge(*t_pe(b - 1, 2))
                dve.tensor_tensor(oTn[:, :, :].rearrange("p g s -> p (g s)"), src[:, 0:HG * S],
                                  oT[:, :, :].rearrange("p g s -> p (g s)"), ALU.mult).then_inc(t_ev.sem, 1)
            elif n == 1:
                dve.wait_ge(*f_p(b, 3))
                dve.tensor_tensor(x_all[:, b, :], src[:S, 0:D], x_all[:, b, :], ALU.add).then_inc(t_ev.sem, 1)
                dve.wait_ge(*t_ev(b, 2))
                dve.sem_inc(apart.sem, 1)
                dve.bn_stats(st2[:], x_all[:, b, :]).then_inc(t_d.sem, 1)
                dve.wait_ge(*t_d(b, 2))
                if not first:
                    dve.wait_ge(*t_p(b - 1, 7))
                dve.sem_inc(apart.sem, 1)
                dve.bn_aggr(mv2[:], st2[:]).then_inc(t_d.sem, 1)
            elif n == 2:
                if not first:
                    dve.wait_ge(*t_p(b - 1, 8))
                dve.tensor_copy(xnT2[:, :, :].rearrange("p c s -> p (c s)"), src[:, 0:DC * S]).then_inc(t_ev.sem, 1)
            elif n == 3:
                dve.tensor_copy(lg[:], src[:S, 0:2 * E0]).then_inc(t_ev.sem, 1)
                dve.wait_ge(*t_ev(b, 4))
                dve.wait_ge(*t_p(b, 7))
                dve.scalar_tensor_tensor(out=lgt[:], in0=lg[:, 0:E0], scalar=rs2[:, 5:6], in1=lg[:, E0:2 * E0],
                                         op0=ALU.mult, op1=ALU.add).then_inc(t_d.sem, 1)
                dve.wait_ge(*t_d(b, 5))
                dve.sem_inc(apart.sem, 1)
                dve.max(top[:], lgt[:]).then_inc(t_d.sem, 1)
                dve.wait_ge(*t_d(b, 6))
                dve.tensor_scalar(keep[:], lgt[:], top[:, 1:2], None, ALU.is_ge).then_inc(t_d.sem, 1)
                dve.tensor_scalar(ntop[:], top[:, 0:1], -1.0, None, ALU.mult).then_inc(t_d.sem, 1)
                dve.engine_nop().then_inc(t_d.sem, 1)
            elif n == 4:
                dve.tensor_copy(gT[:], src[:E0, 0:S]).then_inc(t_ev.sem, 1)
            else:
                dve.tensor_tensor(x_all[:, b, :], src[:S, 0:D], x_all[:, b, :], ALU.add).then_inc(t_ev.sem, 1)

        def normalise2(b):
            dve.wait_ge(*t_p(b, 3))
            dve.tensor_scalar(xn2[:], x_all[:, b, :], mv2[:, 0:1], rs2[:, 1:2], ALU.subtract, ALU.mult).then_inc(t_d.sem, 1)

        def gates(b, first):
            dve.wait_ge(*t_a(b, 1))
            dve.wait_ge(*t_d(b, 9))
            dve.tensor_tensor(ek[:], eg[:], keep[:], ALU.mult).then_inc(t_d.sem, 1)
            dve.wait_ge(*t_d(b, 10))
            dve.tensor_reduce(gs[:], ek[:], AX.X, ALU.add).then_inc(t_d.sem, 1)
            dve.wait_ge(*t_d(b, 11))
            dve.reciprocal(gr[:], gs[:]).then_inc(t_d.sem, 1)
            dve.wait_ge(*t_d(b, 12))
            if not first:
                dve.wait_ge(*t_p(b - 1, 9))
            dve.tensor_scalar(gate[:], ek[:], gr[:], None, ALU.mult).then_inc(t_d.sem, 1)

        def body(b, par, prev, nxt):
            first_t = isinstance(b, int) and b == 1
            for s in range(H):
                mask_max(b, s, par, prev or s >= R)
                if nxt and s == 0:
                    stats(b + 1)
                if nxt and s == 1:
                    normalise(b + 1, False)
                if prev and s == 1:
                    recip(b - 1, 1 - par, first_t)
                for k, n, at in PF:
                    if at != s - 1 or not (nxt if k == "f" else prev):
                        continue
                    if k == "f":
                        front(b + 1, n, 1 - par, False)
                    else:
                        tail(b - 1, n, first_t)
                if prev and s == 7:
                    normalise2(b - 1)
                if prev and s == 13:
                    gates(b - 1, first_t)
            if prev:
                tail(b - 1, 5, first_t)

        dve.wait_ge(w_in.sem, 16 * NW)
        dve.tensor_copy(bvb[:], bv[:, :].unsqueeze(2).to_broadcast([P, HG, P])).then_inc(su_d.sem, 1)
        dve.tensor_tensor_reduce(csq[:], cent[:], cent[:], 1.0, 0.0, ALU.mult, ALU.add, cn[:, 0:1]).then_inc(su_d.sem, 1)
        dve.wait_ge(su_p.sem, 2)
        dve.tensor_scalar(csq[:], cent[:], cn[:, 2:3], None, ALU.mult).then_inc(su_d.sem, 1)
        dve.wait_ge(su_pe.sem, 1)
        dve.tensor_copy(bvo[:], pf[:, 0, 0:D]).then_inc(su_d.sem, 1)
        dve.tensor_copy(cr[:, :, 0:E0], pf[:, 1, 0:DC * E0].rearrange("p (c e) -> p c e", c=DC)).then_inc(su_d.sem, 1)
        dve.wait_ge(x_in.sem, 16)
        stats(0)
        normalise(0, True)
        dve.wait_ge(made.sem, 8)
        for n in range(NF):
            front(0, n, 0, True)
        bodies(dve, body)
        last = B - 1
        recip(last, 1, False)
        for n in range(NT):
            tail(last, n, False)
            if n == 1:
                normalise2(last)
            if n == 3:
                gates(last, False)

    @block.gpsimd
    def _(pool):
        def root(b, sig, k, var, tmp, out):
            pool.sem_inc(apart.sem, 1)
            pool.tensor_scalar(tmp, var, LN_EPS, None, ALU.add).then_inc(sig.sem, 1)
            pool.wait_ge(*sig(b, k))
            pool.tensor_tensor(out, tmp, mhalf[:S, :], ALU.pow).then_inc(sig.sem, 1)

        def front(b, par, early):
            pool.wait_ge(*f_d(b, 2))
            root(b, f_p, 1, mv[:, 1:2], rstd[:, 0:1], rstd[:, 1:2])
            pool.wait_ge(loaded[par].sem, 16 * (b - par) + 32)
            if not early:
                pool.wait_ge(*masked(b - 2, H))
            pool.sem_inc(apart.sem, 1)
            pool.tensor_copy(maskf[par][:], mask8[par][:]).then_inc(conv.sem, 1)
            pool.wait_ge(*f_d(b, 3))
            pool.tensor_tensor(x_all[:, b, :], x_all[:, b, :], bvo[:S, :], ALU.add).then_inc(f_p.sem, 1)

        def mask_q(b, par, early):
            pool.wait_ge(*f_ev(b, 2))
            if not early:
                pool.wait_ge(*scored(b - 2, H))
            for c in range(DC):
                pool.tensor_tensor(qm[par][:, c * HC:(c + 1) * HC, :],
                                   qT[:, c, :].unsqueeze(1).to_broadcast([P, HC, S]),
                                   hmask[:, :].unsqueeze(2).to_broadcast([P, HC, S]), ALU.mult).then_inc(qm_up.sem, 1)

        def tail_1(b, first):
            pool.wait_ge(*t_d(b, 1))
            if not first:
                pool.wait_ge(*t_pe(b - 1, 1))
            pool.sem_inc(apart.sem, 1)
            pool.tensor_copy(recx[:], rec[:, :].unsqueeze(2).to_broadcast([S, H, HP])).then_inc(t_p.sem, 1)

        def tail_2(b):
            pool.wait_ge(*t_d(b, 3))
            root(b, t_p, 2, mv2[:, 1:2], rs2[:, 0:1], rs2[:, 1:2])
            pool.wait_ge(*t_p(b, 3))
            pool.tensor_tensor(rs2[:, 2:3], mv2[:, 1:2], rs2[:, 1:2], ALU.mult).then_inc(t_p.sem, 1)
            pool.wait_ge(*t_p(b, 4))
            pool.tensor_tensor(rs2[:, 3:4], rs2[:, 2:3], rs2[:, 1:2], ALU.mult).then_inc(t_p.sem, 1)
            pool.wait_ge(*t_p(b, 5))
            pool.sem_inc(apart.sem, 1)
            pool.tensor_scalar(rs2[:, 4:5], rs2[:, 3:4], float(D), NORM_EPS ** 2, ALU.mult, ALU.max).then_inc(t_p.sem, 1)
            pool.wait_ge(*t_p(b, 6))
            pool.tensor_tensor(rs2[:, 5:6], rs2[:, 4:5], mhalf[:S, :], ALU.pow).then_inc(t_p.sem, 1)

        def tail_3(b):
            pool.wait_ge(*t_ev(b, 3))
            pool.sem_inc(apart.sem, 1)
            pool.tensor_copy(xnT_all[:, :, bass.ts(b, S)], xnT2[:]).then_inc(t_p.sem, 1)
            pool.wait_ge(*t_d(b, 13))
            pool.sem_inc(apart.sem, 1)
            pool.tensor_copy(gates_all[:, b, :], gate[:]).then_inc(t_p.sem, 1)

        def body(b, par, prev, nxt):
            static = isinstance(b, int)
            if nxt:
                front(b + 1, 1 - par, static and b == 0)
            if prev:
                tail_1(b - 1, static and b == 1)
            if nxt:
                mask_q(b + 1, 1 - par, static and b == 0)
            if prev:
                tail_2(b - 1)
                tail_3(b - 1)

        pool.memset(ident[:], 0.0).then_inc(made.sem, 1)
        pool.memset(hmask[:], 1.0).then_inc(made.sem, 1)
        pool.memset(ones[:], 1.0).then_inc(made.sem, 1)
        pool.memset(mhalf[:], -0.5).then_inc(made.sem, 1)
        pool.wait_ge(made.sem, 4)
        pool.affine_select(out=ident[:], in_=ident[:], compare_op=ALU.not_equal, fill=1.0, base=0,
                           pattern=[[-1, P]], channel_multiplier=1).then_inc(made.sem, 1)
        pool.affine_select(out=hmask[:], in_=hmask[:], compare_op=ALU.is_ge, fill=0.0, base=0,
                           pattern=[[-DK, HC]], channel_multiplier=1).then_inc(made.sem, 1)
        pool.wait_ge(made.sem, 6)
        pool.affine_select(out=hmask[:], in_=hmask[:], compare_op=ALU.is_ge, fill=0.0, base=DK - 1,
                           pattern=[[DK, HC]], channel_multiplier=-1).then_inc(made.sem, 1)
        for par in range(2):
            m = pool.memset(v[par][:], 0.0)
        m.then_inc(made.sem, 1)
        pool.wait_ge(su_d.sem, 2)
        pool.sem_inc(apart.sem, 1)
        pool.tensor_scalar(cn[:, 1:2], cn[:, 0:1], NORM_EPS ** 2, None, ALU.max).then_inc(su_p.sem, 1)
        pool.wait_ge(su_p.sem, 1)
        pool.tensor_tensor(cn[:, 2:3], cn[:, 1:2], mhalf[:E0, :], ALU.pow).then_inc(su_p.sem, 1)
        pool.wait_ge(su_d.sem, 4)
        pool.wait_ge(made.sem, 8)
        front(0, 0, True)
        mask_q(0, 0, True)
        bodies(pool, body)
        last = B - 1
        tail_1(last, False)
        tail_2(last)
        tail_3(last)



def phase_2(nc, ctx, a, t):
    def sb(name, shape, dt=F32):
        return ctx.enter_context(nc.sbuf_tensor(name, shape, dt))

    def sem(name, per=1):
        return Sig(ctx.enter_context(nc.semaphore(name)), per)

    x_all, xnT_all, gates_all, w1, b1, w2 = (t[k] for k in ("x_all", "xnT_all", "gates", "w1", "b1", "w2"))
    hid = sb("hid", [P, 2, GN])
    ph = ctx.enter_context(nc.psum_tensor("ph", [P, 2, 512], F32))
    py = ctx.enter_context(nc.psum_tensor("py", [P, 2, GB, D], F32))
    hidden = sem("hidden", E0)
    gelud = sem("gelud", E0)
    expert = sem("expert", E0)
    added = sem("added", E0 * GB)
    block = ctx.enter_context(nc.Block())

    def groups(eng, body):
        body(0, True)
        with eng.Fori(1, NG) as g:
            body(g, False)

    @block.tensor
    def _(pe):
        def second(g, e, first):
            pe.wait_ge(*gelud(g, e + 1))
            if not first:
                pe.wait_ge(*added(g, (e - 1) * GB))
            for i in range(GB):
                m = pe.matmul(py[:S, e % 2, i, :], hid[:, e % 2, i * S:(i + 1) * S], w2[:, e % E0, :],
                              start=True, stop=True)
            m.then_inc(expert.sem, 1)

        def body(g, first):
            for e in range(E0):
                if not (first and e < 2):
                    pe.wait_ge(*gelud(g, e - 1))
                for c in range(DC):
                    m = pe.matmul(ph[:, e % 2, 0:GN], w1[:, c, e * F0:(e + 1) * F0], xnT_all[:, c, bass.ts(g, GN)],
                                  start=(c == 0), stop=(c == DC - 1))
                m.then_inc(hidden.sem, 1)
                if not (first and e < 1):
                    second(g, e - 1, first and e < 3)
        groups(pe, body)
        second(NG - 1, E0 - 1, False)

    @block.scalar
    def _(act):
        def body(g, first):
            for e in range(E0):
                act.wait_ge(*hidden(g, e + 1))
                if not (first and e < 2):
                    act.wait_ge(*expert(g, e - 1))
                act.activation(hid[:, e % 2, :], ph[:, e % 2, 0:GN], ACT.Gelu, bias=b1[:, e:e + 1]).then_inc(gelud.sem, 1)
        groups(act, body)

    @block.vector
    def _(dve):
        def body(g, first):
            for e in range(E0):
                dve.wait_ge(*expert(g, e + 1))
                for i in range(GB):
                    if e:
                        dve.wait_ge(*added(g, (e - 1) * GB + i + 1))
                    x = x_all[:, g * GB + i, :]
                    dve.scalar_tensor_tensor(out=x, in0=py[:S, e % 2, i, :], scalar=gates_all[:, g * GB + i, e:e + 1],
                                             in1=x, op0=ALU.mult, op1=ALU.add).then_inc(added.sem, 1)
        groups(dve, body)



def phase_3(nc, ctx, a, t):
    def sb(name, shape, dt=F32):
        return ctx.enter_context(nc.sbuf_tensor(name, shape, dt))

    def psum(name, shape):
        return ctx.enter_context(nc.psum_tensor(name, shape, F32))

    sigs = {}

    def sem(name, per, owner):
        s = Sig(ctx.enter_context(nc.semaphore("r_" + name)), per)
        sigs.setdefault(owner, []).append(s)
        return s

    def at(s, K, k):
        return s.sem, (K + 1) * s.per + k

    def prime(eng, owner):
        for s in sigs[owner]:
            eng.sem_inc(s.sem, s.per)

    x_all, ident = t["x_all"], t["ident"]
    UNITS = 2 * ROUNDS
    G3 = 3 * D
    SCALE = D ** -0.5

    wq, wk, wv = sb("xwq", [P, DC, D]), sb("xwk", [P, DC, D]), sb("xwv", [P, DC, D])
    wih, whh = sb("wihT", [P, DC, G3]), sb("whhT", [P, DC, G3])
    bih, bhh = sb("bih", [P, 6]), sb("bhh", [P, 6])
    slot_w, in_w, in_row = sb("slot_w", [P, DC]), sb("in_w", [P, DC]), sb("in_row", [P, D])
    wqk, wg = sb("wqk", [P, DC, D]), sb("wg", [P, DC, G3])
    brz = sb("brz", [P, 4])
    in_row2 = sb("in_row2", [P, DC, D])
    ones = sb("ones3", [P, 1])
    mhalf = sb("mhalf3", [P, 1])
    cx = [sb(f"cx{g}", [KP, GB, KT, D + 1]) for g in range(2)]
    cT = [sb(f"cT{g}", [P, GB, DC, KEYS]) for g in range(2)]
    hT = [[sb(f"hT{g}{r}", [P, DC, GN]) for r in range(2)] for g in range(2)]
    uT = [sb(f"uT{g}", [P, DC, GN]) for g in range(2)]
    kr = [sb(f"kr{g}", [KP, 3, GB * KT]) for g in range(2)]
    ks = [sb(f"ks{g}", [KP, GB * KT]) for g in range(2)]
    st, mv, lr = sb("st3", [S, GB, 6]), sb("mv3", [S, GB, 2]), sb("lr3", [S, 2, GB])
    sl = sb("sl", [S, 2, D])
    sqr = sb("sqr3", [KP, D])
    hsq = sb("hsq", [P, DC, GN])
    ms, rinv = sb("ms", [S, GB]), sb("rinv", [S, GB])
    qs, qT = sb("qs", [S, 2, D]), sb("qT3", [P, 2, DC, S])
    nm, nb = sb("nm3", [KP, GB, KT]), sb("nb3", [KP, GB, KT])
    e = sb("e3", [KP, GB, KT, S])
    es, er = sb("es3", [KP, GB, KT]), sb("er3", [KP, GB, KT])
    uk, un = sb("uk", [S, 2, 2]), sb("un", [S, 2, D])
    tr, tz = sb("tr", [P, DC, GN]), sb("tz", [P, DC, GN])
    hh, na, nn = sb("hh", [P, DC, GN]), sb("na", [P, DC, GN]), sb("nn", [P, DC, GN])
    df = sb("df", [P, DC, GN])

    pa, pg, pc, pu = (psum(n, [P, 2, 512]) for n in ("pa", "pg", "pc", "pu"))

    w_in, made, su = (Sig(ctx.enter_context(nc.semaphore(n))) for n in ("xw_in", "x_made", "x_su"))
    apart = Sig(ctx.enter_context(nc.semaphore("x_apart")))
    c_in = [sem(f"c_in{g}", 16 * (KT + 1) * GB, "sp") for g in range(2)]
    U4 = UNITS * GB
    pe_i = sem("pe_i", 2 * GB, "pe")
    pe_ss = sem("pe_ss", UNITS, "pe")
    pe_q = sem("pe_q", U4, "pe")
    pe_t = sem("pe_t", U4, "pe")
    pe_s = sem("pe_s", U4, "pe")
    pe_u = sem("pe_u", U4, "pe")
    pe_x = sem("pe_x", U4, "pe")
    pe_g = sem("pe_g", UNITS * 8, "pe")
    pe_f = sem("pe_f", 2 * GB, "pe")
    a_sq = sem("a_sq", 2 * GB * KT, "act")
    a_i = sem("a_i", 2 * GB, "act")
    a_q = sem("a_q", U4, "act")
    a_e = sem("a_e", U4, "act")
    a_g = sem("a_g", UNITS * 6, "act")
    d_l = sem("d_l", 2 * (2 * GB), "dve")
    d_n = sem("d_n", 2 * GB, "dve")
    d_ss = sem("d_ss", UNITS, "dve")
    d_t = sem("d_t3", U4, "dve")
    d_m = sem("d_m3", 2 * U4, "dve")
    d_e = sem("d_e", 2 * U4, "dve")
    d_u = sem("d_u", 3 * U4, "dve")
    d_x = sem("d_x", U4, "dve")
    d_g = sem("d_g", UNITS * 8, "dve")
    d_h = sem("d_h", UNITS * 2, "dve")
    d_f = sem("d_f3", 2 * GB, "dve")
    p_k = sem("p_k", 2 * (3 + GB), "pool")
    p_l = sem("p_l", 2 * 2, "pool")
    p_q = sem("p_q", UNITS * 2, "pool")
    p_r = sem("p_r", UNITS, "pool")
    p_d = sem("p_d", UNITS * 2, "pool")

    ATT = [("SS", 0), ("q", 0), ("q", 1), "g", ("T", 0), ("T", 1), ("q", 2), ("q", 3), "g", ("T", 2), ("S", 0),
           ("T", 3), ("S", 1), "g", ("S", 2), ("N", 0), "g", ("S", 3), ("N", 1), ("U", 0), "g", ("N", 2), ("U", 1),
           ("X", 0), "g", ("N", 3), ("U", 2), ("X", 1), "g", ("U", 3), ("X", 2), "g", ("X", 3)]
    GRU = [("g", 0), ("g", 1), ("g", 2), ("g", 3), ("g", 4), ("g", 5), ("g", 6), ("g", 7)]
    STEP = [("r", 0), ("hn", 0), ("r", 1), ("hn", 1), ("xn", 0), ("z", 0), ("xn", 1), ("z", 1)]
    AT_A = {("r", 0): 1, ("r", 1): 2, ("xn", 0): 3, ("z", 0): 4, ("xn", 1): 5, ("z", 1): 6}

    def schedule():
        out = [("init", g, g) for g in range(2)]
        for n in range(UNITS + 1):
            gru = [(w, i, n - 1) for w, i in GRU] if n else []
            for s in (ATT if n < UNITS else ["g"] * 8):
                if s == "g":
                    if gru:
                        out.append(gru.pop(0))
                else:
                    out.append((*s, n))
            if n >= UNITS - 1:
                out.append(("fin", (n - 1) % 2, n - 1))
        return out
    SCHEDULE = schedule()

    def iterations(eng, owner, do):
        prime(eng, owner)
        with eng.Fori(0, NG // 2) as K:
            for what, i, n in SCHEDULE:
                do(what, i, n, K)

    block = ctx.enter_context(nc.Block())

    @block.sync
    def _(sp):
        prime(sp, "sp")
        for dst, src in ((wq[:], a["xwq"].rearrange("(c p) n -> p c n", p=P)),
                         (wk[:], a["xwk"].rearrange("(c p) n -> p c n", p=P)),
                         (wv[:], a["xwv"].rearrange("(c p) n -> p c n", p=P)),
                         (wih[:], a["wihT"].rearrange("(c p) n -> p c n", p=P)),
                         (whh[:], a["whhT"].rearrange("(c p) n -> p c n", p=P)),
                         (bih[:], a["bih"]), (bhh[:], a["bhh"]), (slot_w[:], a["slot_w"]), (in_w[:], a["in_w"]),
                         (in_row[:], a["in_w_row"].to_broadcast([P, D]))):
            sp.dma_start(dst, src).then_inc(w_in.sem, 16)
        with sp.Fori(0, NG // 2) as K:
            for g in range(2):
                sp.wait_ge(*at(pe_u, K, -(1 - g) * GB))
                sp.sem_inc(apart.sem, 1)
                for i in range(GB):
                    b = (2 * K + g) * GB + i
                    for kt in range(KT):
                        sp.dma_start(cx[g][:, i, kt, 0:D], a["ctx"][b, kt * KP:(kt + 1) * KP, :]).then_inc(c_in[g].sem, 16)
                    sp.dma_start(cT[g][:, i], a["ctxT"][b].rearrange("(c p) m -> p c m", p=P)).then_inc(c_in[g].sem, 16)

    @block.tensor
    def _(pe):
        def do(what, i, n, K):
            g, r = n % 2, n // 2
            k = n * GB + i + 1
            old, new = hT[g][r % 2], hT[g][(r + 1) % 2]
            if what == "init":
                for j in range(GB):
                    b = g * GB + j
                    pe.wait_ge(*at(d_n, K, b + 1))
                    if b >= 2:
                        pe.wait_ge(*at(a_i, K, b - 1))
                    else:
                        pe.wait_ge(*at(d_f, K, 0))
                    for c in range(DC):
                        m = pe.transpose(pu[:, b % 2, c * S:(c + 1) * S], sl[:, b % 2, c * P:(c + 1) * P], ident[:S, :S])
                    m.then_inc(pe_i.sem, 1)
            elif what == "SS":
                pe.wait_ge(*at(p_q, K, 2 * n + 2))
                pe.wait_ge(*at(d_t, K, n * GB))
                for j in range(GB):
                    for c in range(DC):
                        m = pe.matmul(pa[:S, 0, j:j + 1], hsq[:, c, j * S:(j + 1) * S], ones[:, 0:1],
                                      start=(c == 0), stop=(c == DC - 1))
                m.then_inc(pe_ss.sem, 1)
            elif what == "q":
                if i == 0:
                    pe.wait_ge(*at(d_ss, K, n + 1))
                    if r == 0:
                        pe.wait_ge(*at(a_i, K, (g + 1) * GB))
                    else:
                        pe.wait_ge(*at(d_h, K, 2 * (n - 1)))
                elif i == 1:
                    pe.wait_ge(*at(d_t, K, n * GB))
                else:
                    pe.wait_ge(*at(d_t, K, k - 2))
                for c in range(DC):
                    m = pe.matmul(pa[:S, i % 2, 0:D], old[:, c, i * S:(i + 1) * S], wqk[:, c, :],
                                  start=(c == 0), stop=(c == DC - 1))
                m.then_inc(pe_q.sem, 1)
            elif what == "T":
                pe.wait_ge(*at(a_q, K, k))
                for c in range(DC):
                    m = pe.transpose(pa[:, i % 2, D + c * S:D + (c + 1) * S], qs[:, i % 2, c * P:(c + 1) * P], ident[:S, :S])
                m.then_inc(pe_t.sem, 1)
            elif what == "S":
                if i == 0 and r == 0:
                    pe.wait_ge(*at(c_in[g], K, c_in[g].per))
                pe.wait_ge(*at(d_t, K, k))
                pe.wait_ge(*at(a_e, K, k - 2))
                for kt in range(KT):
                    for c in range(DC):
                        m = pe.matmul(pc[:KP, i % 2, kt * S:(kt + 1) * S], cT[g][:, i, c, kt * KP:(kt + 1) * KP],
                                      qT[:, i % 2, c, :], start=(c == 0), stop=(c == DC - 1))
                m.then_inc(pe_s.sem, 1)
            elif what == "U":
                pe.wait_ge(*at(d_e, K, 2 * k))
                if i == 0 and r == 0:
                    pe.wait_ge(*at(p_k, K, (g + 1) * (3 + GB)))
                if n == 0 and i == 0:
                    pe.wait_ge(*at(a_i, K, 2 * GB))
                pe.wait_ge(*at(d_x, K, k - 2))
                for kt in range(KT):
                    m = pe.matmul(pu[:S, i % 2, 0:D + 1], e[:, i, kt, :], cx[g][:, i, kt, :],
                                  start=(kt == 0), stop=(kt == KT - 1))
                m.then_inc(pe_u.sem, 1)
            elif what == "X":
                pe.wait_ge(*at(d_u, K, 3 * k))
                for c in range(DC):
                    m = pe.transpose(pu[:, i % 2, c * S:(c + 1) * S],
                                     un[:, i % 2, c * P:(c + 1) * P], ident[:S, :S])
                m.then_inc(pe_x.sem, 1)
            elif what == "g":
                kind, c = STEP[i]
                out = pg[:, i % 2, 0:GN]
                if i < 2:
                    pe.wait_ge(*at(a_g, K, 6 * n))
                    pe.wait_ge(*at(d_g, K, 8 * n))
                    pe.wait_ge(*at(d_x, K, (n + 1) * GB))
                elif i == 2:
                    pe.wait_ge(*at(a_g, K, 6 * n + 1))
                elif i == 3:
                    pe.wait_ge(*at(d_g, K, 8 * n + 1))
                elif i == 4:
                    pe.wait_ge(*at(a_g, K, 6 * n + 2))
                elif i == 5:
                    pe.wait_ge(*at(d_g, K, 8 * n + 3))
                elif i == 6:
                    pe.wait_ge(*at(d_g, K, 8 * n + 5))
                else:
                    pe.wait_ge(*at(a_g, K, 6 * n + 4))
                col = {"r": 0, "z": D, "hn": 2 * D, "xn": 2 * D}[kind] + c * P
                parts = ([(wg, uT[g])] if kind != "hn" else []) + ([(whh, old)] if kind != "xn" else [])
                terms = [(w, s, q) for w, s in parts for q in range(DC)]
                for j, (w, s, q) in enumerate(terms):
                    m = pe.matmul(out, w[:, q, col:col + P], s[:, q, :], start=(j == 0), stop=(j == len(terms) - 1))
                m.then_inc(pe_g.sem, 1)
            elif what == "fin":
                for j in range(GB):
                    b = g * GB + j
                    pe.wait_ge(*at(d_h, K, 2 * (n + 1)))
                    if b < 2:
                        pe.wait_ge(*at(a_e, K, U4))
                    else:
                        pe.wait_ge(*at(d_f, K, b - 1))
                    if g == 0 and j < 2:
                        pe.wait_ge(*at(d_u, K, 3 * U4))
                        pe.wait_ge(*at(d_x, K, U4))
                    for c in range(DC):
                        m = pe.transpose(pu[:S, b % 2, c * P:(c + 1) * P], new[:, c, j * S:(j + 1) * S], ident[:, :])
                    m.then_inc(pe_f.sem, 1)

        pe.wait_ge(w_in.sem, 160)
        for c in range(DC):
            for o in range(DC):
                m = pe.matmul(pa[:, c, 0:D], wq[:, o, c * P:(c + 1) * P], wk[:, o, :], start=(o == 0), stop=(o == DC - 1))
        m.then_inc(su.sem, 1)
        for c in range(DC):
            for lo in (0, 512):
                n = min(512, G3 - lo)
                dst = (pg if lo == 0 else pc)[:, c, 0:n]
                for o in range(DC):
                    m = pe.matmul(dst, wv[:, o, c * P:(c + 1) * P], wih[:, o, lo:lo + n], start=(o == 0), stop=(o == DC - 1))
        m.then_inc(su.sem, 1)
        pe.wait_ge(su.sem, 3)
        pe.wait_ge(made.sem, 4)
        iterations(pe, "pe", do)

    @block.scalar
    def _(act):
        def do(what, i, n, K):
            g, r = n % 2, n // 2
            k = n * GB + i + 1
            if what == "init":
                for j in range(GB):
                    act.wait_ge(*at(pe_i, K, g * GB + j + 1))
                    act.wait_ge(*at(pe_f, K, 0))
                    act.activation(hT[g][0][:, :, j * S:(j + 1) * S],
                                   pu[:, j % 2, 0:DC * S].rearrange("p (c s) -> p c s", c=DC), ACT.Copy).then_inc(a_i.sem, 1)
                act.wait_ge(*at(c_in[g], K, c_in[g].per))
                act.wait_ge(*at(p_k, K, -(1 - g) * (3 + GB)))
                for j in range(GB * KT):
                    act.activation(sqr[:], cx[g][:, j // KT, j % KT, 0:D], ACT.Square,
                                   accum_out=kr[g][:, 0, j:j + 1]).then_inc(a_sq.sem, 1)
                    act.wait_ge(*at(a_sq, K, g * GB * KT + j + 1))
            elif what == "q":
                act.wait_ge(*at(pe_q, K, k))
                act.wait_ge(*at(p_r, K, n + 1))
                act.wait_ge(*at(pe_t, K, k - 2))
                act.activation(qs[:, i % 2, :], pa[:S, i % 2, 0:D], ACT.Copy, scale=rinv[:, i:i + 1]).then_inc(a_q.sem, 1)
            elif what == "S":
                act.wait_ge(*at(d_m, K, 2 * k))
                act.wait_ge(*at(pe_u, K, k - GB))
                for kt in range(KT):
                    m = act.activation(e[:, i, kt, :], pc[:KP, i % 2, kt * S:(kt + 1) * S], ACT.Exp,
                                       scale=ks[g][:, i * KT + kt:i * KT + kt + 1], bias=nb[:, i, kt:kt + 1],
                                       accum_out=es[:, i, kt:kt + 1])
                m.then_inc(a_e.sem, 1)
            elif what == "g" and STEP[i] in AT_A:
                kind, c = STEP[i]
                ps = pg[:, i % 2, 0:GN]
                if kind == "xn":
                    act.wait_ge(*at(d_g, K, 8 * n + 5 + c))
                    act.wait_ge(*at(d_h, K, 2 * n))
                    act.activation(nn[:, c, :], na[:, c, :], ACT.Tanh, bias=bih[:, 4 + c:5 + c]).then_inc(a_g.sem, 1)
                else:
                    act.wait_ge(*at(pe_g, K, 8 * n + i + 1))
                    dst, col = (tr, c) if kind == "r" else (tz, 2 + c)
                    act.wait_ge(*at(d_h, K, 2 * n))
                    act.activation(dst[:, c, :], ps, ACT.Tanh, scale=0.5, bias=brz[:, col:col + 1]).then_inc(a_g.sem, 1)

        iterations(act, "act", do)

    @block.vector
    def _(dve):
        def do(what, i, n, K):
            g, r = n % 2, n // 2
            k = n * GB + i + 1
            old, new = hT[g][r % 2], hT[g][(r + 1) % 2]
            if what == "init":
                for j in range(GB):
                    x = x_all[:, (2 * K + g) * GB + j, :]
                    dve.wait_ge(*at(d_n, K, g * GB))
                    dve.sem_inc(apart.sem, 1)
                    dve.bn_stats(st[:, j, :], x).then_inc(d_l.sem, 1)
                for j in range(GB):
                    dve.wait_ge(*at(d_l, K, g * 2 * GB + j + 1))
                    dve.sem_inc(apart.sem, 1)
                    dve.bn_aggr(mv[:, j, :], st[:, j, :]).then_inc(d_l.sem, 1)
                for j in range(GB):
                    b = g * GB + j
                    x = x_all[:, (2 * K + g) * GB + j, :]
                    dve.wait_ge(*at(p_l, K, 2 * g + 2))
                    dve.wait_ge(*at(pe_i, K, b - 1))
                    dve.tensor_scalar(sl[:, b % 2, :], x, mv[:, j, 0:1], lr[:, 1, j:j + 1],
                                      ALU.subtract, ALU.mult).then_inc(d_n.sem, 1)
            elif what == "SS":
                dve.wait_ge(*at(pe_ss, K, n + 1))
                dve.wait_ge(*at(p_r, K, n))
                dve.tensor_scalar(ms[:], pa[:S, 0, 0:GB], 1.0 / D, RMS_EPS, ALU.mult, ALU.add).then_inc(d_ss.sem, 1)
            elif what == "T":
                dve.wait_ge(*at(pe_t, K, k))
                dve.wait_ge(*at(pe_s, K, k - 2))
                dve.tensor_copy(qT[:, i % 2].rearrange("p c s -> p (c s)"), pa[:, i % 2, D:D + DC * S]).then_inc(d_t.sem, 1)
            elif what == "S":
                dve.wait_ge(*at(pe_s, K, k))
                if i == 0 and r == 0:
                    dve.wait_ge(*at(p_k, K, g * (3 + GB) + 3))
                dve.wait_ge(*at(a_e, K, k - GB))
                dve.tensor_reduce(nm[:, i, :], pc[:KP, i % 2, 0:KT * S].rearrange("p (t s) -> p t s", t=KT),
                                  AX.X, ALU.max, negate=True).then_inc(d_m.sem, 1)
                dve.wait_ge(*at(d_m, K, 2 * k - 1))
                dve.tensor_tensor(nb[:, i, :], nm[:, i, :], ks[g][:, i * KT:(i + 1) * KT], ALU.mult).then_inc(d_m.sem, 1)
            elif what == "N":
                dve.wait_ge(*at(a_e, K, k))
                dve.reciprocal(er[:, i, :], es[:, i, :]).then_inc(d_e.sem, 1)
                dve.wait_ge(*at(d_e, K, 2 * k - 1))
                dve.tensor_tensor(e[:, i], e[:, i], er[:, i, :].unsqueeze(2).to_broadcast([KP, KT, S]),
                                  ALU.mult).then_inc(d_e.sem, 1)
            elif what == "U":
                dve.wait_ge(*at(pe_u, K, k))
                dve.tensor_scalar(uk[:, i % 2, 0:1], pu[:S, i % 2, D:D + 1], SLOT_EPS, None, ALU.add).then_inc(d_u.sem, 1)
                dve.wait_ge(*at(d_u, K, 3 * k - 2))
                dve.reciprocal(uk[:, i % 2, 1:2], uk[:, i % 2, 0:1]).then_inc(d_u.sem, 1)
                dve.wait_ge(*at(d_u, K, 3 * k - 1))
                dve.wait_ge(*at(pe_x, K, k - 2))
                dve.tensor_scalar(un[:, i % 2, :], pu[:S, i % 2, 0:D], uk[:, i % 2, 1:2], None, ALU.mult).then_inc(d_u.sem, 1)
            elif what == "X":
                dve.wait_ge(*at(pe_x, K, k))
                if i == 0:
                    dve.wait_ge(*at(pe_g, K, 8 * (n - 1)))
                dve.tensor_copy(uT[g][:, :, i * S:(i + 1) * S],
                                pu[:, i % 2, 0:DC * S].rearrange("p (c s) -> p c s", c=DC)).then_inc(d_x.sem, 1)
            elif what == "g":
                kind, c = STEP[i]
                ps = pg[:, i % 2, 0:GN]
                if kind == "hn":
                    dve.wait_ge(*at(pe_g, K, 8 * n + i + 1))
                    dve.tensor_scalar(hh[:, c, :], ps, bhh[:, 4 + c:5 + c], 0.5, ALU.add, ALU.mult).then_inc(d_g.sem, 1)
                    dve.wait_ge(*at(d_g, K, 8 * n + 2 * c + 1))
                    dve.wait_ge(*at(a_g, K, 6 * n + 1 + c))
                    dve.scalar_tensor_tensor(out=hh[:, c, :], in0=tr[:, c, :], scalar=1.0, in1=hh[:, c, :],
                                             op0=ALU.add, op1=ALU.mult).then_inc(d_g.sem, 1)
                elif kind == "xn":
                    dve.wait_ge(*at(pe_g, K, 8 * n + i + 1))
                    dve.wait_ge(*at(d_g, K, 8 * n + 2 * c + 2))
                    dve.wait_ge(*at(a_g, K, 6 * n))
                    dve.tensor_tensor(na[:, c, :], ps, hh[:, c, :], ALU.add).then_inc(d_g.sem, 1)
                if i == 6:
                    state(n, 0, K, old, new)
                elif i == 7:
                    state(n, 1, K, old, new)
            elif what == "fin":
                for j in range(GB):
                    x = x_all[:, (2 * K + g) * GB + j, :]
                    dve.wait_ge(*at(pe_f, K, g * GB + j + 1))
                    dve.tensor_tensor(x, pu[:S, j % 2, 0:D], x, ALU.add).then_inc(d_f.sem, 1)

        def state(n, c, K, old, new):
            dve.wait_ge(*at(p_d, K, 2 * n + c + 1))
            dve.wait_ge(*at(a_g, K, 6 * n + 4 + 2 * c))
            dve.scalar_tensor_tensor(out=tz[:, c, :], in0=tz[:, c, :], scalar=1.0, in1=df[:, c, :],
                                     op0=ALU.add, op1=ALU.mult).then_inc(d_g.sem, 1)
            dve.wait_ge(*at(d_g, K, 8 * n + 7 + c))
            dve.scalar_tensor_tensor(out=new[:, c, :], in0=tz[:, c, :], scalar=0.5, in1=nn[:, c, :],
                                     op0=ALU.mult, op1=ALU.add).then_inc(d_h.sem, 1)

        dve.wait_ge(w_in.sem, 160)
        for c in range(DC):
            m = dve.tensor_scalar(in_row2[:, c, :], in_row[:], slot_w[:, c:c + 1], None, ALU.mult)
        m.then_inc(made.sem, 1)
        dve.tensor_tensor(brz[:], bih[:, 0:4], bhh[:, 0:4], ALU.add).then_inc(made.sem, 1)
        dve.wait_ge(su.sem, 2)
        dve.wait_ge(made.sem, 2 + 2)
        dve.tensor_scalar(brz[:], brz[:], 0.5, None, ALU.mult)
        for c in range(DC):
            dve.tensor_tensor(wqk[:, c, :], pa[:, c, 0:D], in_row2[:, c, :], ALU.mult)
            dve.tensor_scalar(wg[:, c, 0:512], pg[:, c, :], in_w[:, c:c + 1], None, ALU.mult)
            m = dve.tensor_scalar(wg[:, c, 512:G3], pc[:, c, 0:G3 - 512], in_w[:, c:c + 1], None, ALU.mult)
        m.then_inc(su.sem, 1)
        iterations(dve, "dve", do)

    @block.gpsimd
    def _(pool):
        def do(what, i, n, K):
            g, r = n % 2, n // 2
            old = hT[g][r % 2]
            if what == "init":
                pool.wait_ge(*at(d_l, K, (g + 1) * 2 * GB))
                pool.sem_inc(apart.sem, 1)
                pool.tensor_scalar(lr[:, 0, :], mv[:, :, 1], LN_EPS, None, ALU.add).then_inc(p_l.sem, 1)
                pool.wait_ge(*at(p_l, K, 2 * g + 1))
                pool.tensor_tensor(lr[:, 1, :], lr[:, 0, :], mhalf[:S, 0:1].to_broadcast([S, GB]), ALU.pow).then_inc(p_l.sem, 1)
                k0 = g * (3 + GB)
                pool.wait_ge(*at(a_sq, K, (g + 1) * GB * KT))
                pool.sem_inc(apart.sem, 1)
                pool.tensor_scalar(kr[g][:, 1, :], kr[g][:, 0, :], 1.0 / D, RMS_EPS, ALU.mult, ALU.add).then_inc(p_k.sem, 1)
                pool.wait_ge(*at(p_k, K, k0 + 1))
                pool.tensor_tensor(kr[g][:, 2, :], kr[g][:, 1, :], mhalf[:KP, 0:1].to_broadcast([KP, GB * KT]),
                                   ALU.pow).then_inc(p_k.sem, 1)
                pool.wait_ge(*at(p_k, K, k0 + 2))
                pool.sem_inc(apart.sem, 1)
                pool.tensor_scalar(ks[g][:], kr[g][:, 2, :], SCALE, None, ALU.mult).then_inc(p_k.sem, 1)
                for j in range(GB):
                    pool.tensor_tensor(cx[g][:, j, :, 0:D], cx[g][:, j, :, 0:D],
                                       kr[g][:, 2, j * KT:(j + 1) * KT].unsqueeze(2).to_broadcast([KP, KT, D]),
                                       ALU.mult).then_inc(p_k.sem, 1)
                if g == 1:
                    squares(0, K)
            elif what == "SS":
                pool.wait_ge(*at(d_ss, K, n + 1))
                pool.wait_ge(*at(a_q, K, n * GB))
                pool.tensor_tensor(rinv[:], ms[:], mhalf[:S, 0:1].to_broadcast([S, GB]), ALU.pow).then_inc(p_r.sem, 1)
                if n == 0:
                    squares(1, K)
            elif what == "g" and i in (5, 7):
                c = (i - 5) // 2
                pool.wait_ge(*at(a_g, K, 6 * n + 3 + 2 * c))
                pool.wait_ge(*at(d_g, K, 8 * n - 1 + c))
                pool.tensor_tensor(df[:, c, :], old[:, c, :], nn[:, c, :], ALU.subtract).then_inc(p_d.sem, 1)
                if i == 7 and n + 2 < UNITS:
                    squares(n + 2, K)

        def squares(n, K):
            g, r = n % 2, n // 2
            for c in range(DC):
                if r == 0:
                    pool.wait_ge(*at(a_i, K, (g + 1) * GB))
                else:
                    pool.wait_ge(*at(d_h, K, 2 * (n - 2) + c + 1))
                pool.wait_ge(*at(pe_ss, K, n))
                pool.tensor_tensor(hsq[:, c, :], hT[g][r % 2][:, c, :], hT[g][r % 2][:, c, :], ALU.mult).then_inc(p_q.sem, 1)

        pool.memset(ones[:], 1.0)
        pool.memset(mhalf[:], -0.5).then_inc(made.sem, 1)
        for g in range(2):
            m = pool.memset(cx[g][:, :, :, D:D + 1], 1.0)
        m.then_inc(made.sem, 1)
        pool.wait_ge(made.sem, 4)
        iterations(pool, "pool", do)



def phase_4(nc, ctx, a, t, out):
    def sb(name, shape, dt=F32):
        return ctx.enter_context(nc.sbuf_tensor("e_" + name, shape, dt))

    def psum(name, shape):
        return ctx.enter_context(nc.psum_tensor("e_" + name, shape, F32))

    def sem(name, per=1):
        return Sig(ctx.enter_context(nc.semaphore("e_" + name)), per)

    x_all, ident = t["x_all"], t["ident"]
    HID2 = 2 * F1
    FC = F1 // P
    BE = B * E1

    up = sb("up", [P, E1, DC, HID2])
    down = sb("down", [P, E1, FC, D])
    scale = sb("scale4", [S, D])
    cT1 = sb("cT1", [P, DC, E1])
    ny, csq = sb("ny", [S, E1]), sb("csq4", [P, DC, E1])
    zeros = sb("zeros", [P, D])
    onesf, onesb = sb("onesf", [P, S]), sb("onesb", [S, S], BF16)
    before = sb("before", [S, S], BF16)
    mhalf = sb("mhalf4", [P, 1])
    rank_e = sb("rank_e", [S, E1])
    less = sb("less", [S, E1, E1])
    kk = sb("kk", [S, E1, B * S // P])
    tj = sb("tj", [S, MT, E1])
    st, mv = sb("st4", [S, B, 6]), sb("mv4", [S, B, 2])
    rt = sb("rt", [S, 6, B])
    xl, xn = sb("xl", [S, 2, D]), sb("xn4", [S, 2, D])
    xn_all = sb("xn_all", [S, B, D])
    sq = sb("sq4", [S, D])
    nx = sb("nx", [S, B])
    xnT = sb("xnT4", [P, 2, DC, S])
    dots = sb("dots", [S, B, E1])
    dist, cand, oh = sb("dist", [S, B, E1]), sb("cand", [S, B, E1]), sb("oh", [S, B, E1])
    best = sb("best", [S, 2, B])
    ohb = sb("ohb", [S, B, E1], BF16)
    cum = sb("cum", [S, 2, B, E1])
    cnt = sb("cnt", [S, B, E1])
    rank = sb("rank4", [S, B, E1])
    more = sb("more", [S, E1, B * S // P])
    tiles, start, end = sb("tiles", [S, E1]), sb("start", [S, E1]), sb("end", [S, E1])
    lt = sb("lt", [S, E1, E1])
    passed = sb("passed", [S, MT, E1])
    texp = sb("texp", [S, MT])
    texp_i = sb("texp_i", [S, MT], I32)
    place, place_i = sb("place", [S, B]), sb("place_i", [S, B], U32)
    xt, xT = sb("xt", [P, 2, D]), sb("xT", [P, 2, DC, P])
    th, u = sb("th", [P, 2, F1]), sb("u", [P, 2, F1])
    uT, ysb = sb("uT4", [P, 2, FC, P]), sb("ysb", [P, 2, D])
    yg = sb("yg", [S, B, D])
    xs = nc.dram_tensor("rows_by_place", [MT * P, D], F32).ap()
    ys = nc.dram_tensor("results_by_place", [MT * P, D], F32).ap()

    pt, pd = psum("pt4", [P, 512]), psum("pd4", [P, 512])
    ph = psum("ph4", [P, 2, 2, 512])
    pz, py = psum("pz4", [P, 512]), psum("py4", [P, 512])

    s_in, u_in = sem("s_in"), sem("u_in")
    made, zeroed = sem("made"), sem("zeroed")
    apart = sem("apart")
    statd, agg = sem("statd"), sem("agg")
    roots = sem("roots")
    lnd, nrm = sem("lnd"), sem("nrm")
    kept, nxd = sem("kept"), sem("nxd")
    tpd, tup, dotd, dup = sem("tpd"), sem("tup"), sem("dotd"), sem("dup")
    v = sem("v")
    routed_pe = sem("routed_pe")
    scattered, stored = sem("scattered"), sem("stored")
    gathered = [sem(f"gathered{g}") for g in range(NG)]
    x_in = [sem("x_in0"), sem("x_in1")]
    y_out = [sem("y_out0"), sem("y_out1")]
    t_pe, t_up, up_a, up_g, thd, gated, z_pe, z_up, y_pe, y_up = (
        sem(n) for n in ("t_pe", "t_up", "up_a", "up_g", "thd", "gated", "z_pe", "z_up", "y_pe", "y_up"))
    added = sem("added")

    block = ctx.enter_context(nc.Block())

    def tiles_loop(eng, body):
        body(0, 0, True, False)
        body(1, 1, False, False)
        with eng.Fori(1, (MT - 1) // 2) as j:
            body(2 * j, 0, False, True)
            body(2 * j + 1, 1, False, True)
        body(MT - 1, 0, False, True)

    @block.sync
    def _(sp):
        sp.dma_start(scale[:], a["scale"].to_broadcast([S, D])).then_inc(s_in.sem, 16)
        sp.dma_start(cT1[:], a["centT"].rearrange("(c p) e -> p c e", p=P)).then_inc(s_in.sem, 16)
        sp.wait_ge(made.sem, 2)
        sp.dma_start(xs.rearrange("(t p) d -> p t d", p=P), zeros[:, :].unsqueeze(1).to_broadcast([P, MT, D])).then_inc(zeroed.sem, 16)
        for e in range(E1):
            sp.dma_start(up[:, e], a["up"][e].rearrange("(c p) n -> p c n", p=P)).then_inc(u_in.sem, 16)
            sp.dma_start(down[:, e], a["down"][e].rearrange("(c p) n -> p c n", p=P)).then_inc(u_in.sem, 16)
        sp.wait_ge(scattered.sem, 16 * B)

        def load(j, par):
            sp.dma_start(xt[:, par, :], xs[bass.ts(j, P), :]).then_inc(x_in[par].sem, 16)

        load(0, 0)
        load(1, 1)

        def body(j, par, first, full):
            if not (isinstance(j, int) and j + 2 >= MT):
                sp.wait_ge(t_pe.sem, j + 1)
                sp.sem_inc(apart.sem, 1)
                load(j + 2, par)
            sp.wait_ge(y_up.sem, j + 1)
            sp.sem_inc(apart.sem, 1)
            sp.dma_start(ys[bass.ts(j, P), :], ysb[:, par, :]).then_inc(y_out[par].sem, 16)

        body(0, 0, True, False)
        body(1, 1, False, False)
        with sp.Fori(1, (MT - 1) // 2 - 1) as j:
            body(2 * j, 0, False, True)
            body(2 * j + 1, 1, False, True)
        body(MT - 3, 0, False, True)
        body(MT - 2, 1, False, True)
        body(MT - 1, 0, False, True)
        for b in range(B):
            sp.wait_ge(added.sem, b + 1)
            sp.dma_start(out[b], x_all[:, b, :]).then_inc(stored.sem, 16)
        sp.wait_ge(stored.sem, 16 * B)

    @block.tensor
    def _(pe):
        pe.wait_ge(v.sem, 1)
        pe.wait_ge(made.sem, 12)
        for c in range(DC):
            m = pe.matmul(pz[:S, 0:E1], onesf[:, :], csq[:, c, :], start=(c == 0), stop=(c == DC - 1))
        m.then_inc(routed_pe.sem, 1)
        with pe.Fori(0, B // 2) as j:
            for par in range(2):
                b = 2 * j + par
                pe.wait_ge(nrm.sem, b + 3)
                pe.wait_ge(tup.sem, b + 2)
                for c in range(DC):
                    m = pe.transpose(pt[:, c * S:(c + 1) * S], xn[:, par, c * P:(c + 1) * P], ident[:S, :S])
                m.then_inc(tpd.sem, 1)
                pe.wait_ge(tup.sem, b + 3)
                pe.wait_ge(dup.sem, b + 2)
                for c in range(DC):
                    m = pe.matmul(pd[:S, 0:E1], xnT[:, par, c, :], cT1[:, c, :], start=(c == 0), stop=(c == DC - 1))
                m.then_inc(dotd.sem, 1)
        pe.wait_ge(v.sem, 8)
        pe.wait_ge(dup.sem, B + 2)
        pe.matmul(pd[:S, 0:BE], before[:, :], ohb[:, :, :].rearrange("s b e -> s (b e)"), start=True, stop=True)
        pe.matmul(pz[:S, 0:BE], onesb[:, :], ohb[:, :, :].rearrange("s b e -> s (b e)"), start=True, stop=True).then_inc(routed_pe.sem, 1)

        def turn(j, par, first):
            pe.wait_ge(x_in[par].sem, 8 * (j - par) + 16)
            if not first:
                pe.wait_ge(t_up.sem, j)
            else:
                pe.wait_ge(dotd.sem, B)
            for c in range(DC):
                m = pe.transpose(pt[:, c * P:(c + 1) * P], xt[:, par, c * P:(c + 1) * P], ident[:, :])
            m.then_inc(t_pe.sem, 1)

        def half(j, par, h, e, sig):
            for c in range(DC):
                m = pe.matmul(ph[:, par, h, :], xT[:, par, c, :], up[:, e, c, h * F1:(h + 1) * F1],
                              start=(c == 0), stop=(c == DC - 1))
            m.then_inc(sig.sem, 1)

        def turn_u(j, par, first):
            pe.wait_ge(gated.sem, j + 1)
            if not first:
                pe.wait_ge(z_up.sem, j)
            for f in range(FC):
                m = pe.transpose(pz[:, f * P:(f + 1) * P], u[:, par, f * P:(f + 1) * P], ident[:, :])
            m.then_inc(z_pe.sem, 1)

        def second(j, par, first, e):
            pe.wait_ge(z_up.sem, j + 1)
            if not first:
                pe.wait_ge(y_up.sem, j)
            for f in range(FC):
                m = pe.matmul(py[:, 0:D], uT[:, par, f, :], down[:, e, f, :], start=(f == 0), stop=(f == FC - 1))
            m.then_inc(y_pe.sem, 1)

        def expert(j):
            return pe.value_load(texp_i[0:1, bass.ds(j, 1)], min_val=0, max_val=E1 - 1)

        pe.wait_ge(v.sem, 23)
        turn(0, 0, True)
        pe.wait_ge(u_in.sem, 16 * 2 * E1)

        def body(j, par, first, full):
            e = expert(j)
            pe.wait_ge(t_up.sem, j + 1)
            if full:
                pe.wait_ge(gated.sem, j - 1)
            half(j, par, 1, e, up_g)
            if not first:
                turn_u(j - 1, 1 - par, isinstance(j, int) and j == 1)
            half(j, par, 0, e, up_a)
            if not (isinstance(j, int) and j == MT - 1):
                turn(j + 1, 1 - par, False)
            if not first:
                second(j - 1, 1 - par, isinstance(j, int) and j == 1, expert(j - 1))

        tiles_loop(pe, body)
        turn_u(MT - 1, 0, False)
        second(MT - 1, 0, False, expert(MT - 1))

    @block.scalar
    def _(act):
        act.sem_inc(tup.sem, 2)
        act.sem_inc(nxd.sem, 2)
        with act.Fori(0, B // 2) as j:
            for par in range(2):
                b = 2 * j + par
                act.wait_ge(nrm.sem, b + 3)
                act.wait_ge(nxd.sem, b + 2)
                act.activation(sq[:], xn[:, par, :], ACT.Square, accum_out=nx[:, bass.ds(b, 1)]).then_inc(nxd.sem, 1)
                act.wait_ge(tpd.sem, b + 1)
                act.wait_ge(dotd.sem, b)
                act.activation(xnT[:, par].rearrange("p c s -> p (c s)"), pt[:, 0:DC * S], ACT.Copy).then_inc(tup.sem, 1)

        def body(j, par, first, full):
            act.wait_ge(up_g.sem, j + 1)
            if full:
                act.wait_ge(gated.sem, j - 1)
            act.activation(th[:, par, :], ph[:, par, 1, :], ACT.Tanh, scale=0.5).then_inc(thd.sem, 1)
            if not first:
                up_z(j - 1, 1 - par)

        def up_z(j, par):
            act.wait_ge(z_pe.sem, j + 1)
            act.activation(uT[:, par].rearrange("p f s -> p (f s)"), pz[:, :], ACT.Copy).then_inc(z_up.sem, 1)

        tiles_loop(act, body)
        up_z(MT - 1, 0)

    @block.vector
    def _(dve):
        dve.wait_ge(s_in.sem, 32)
        dve.tensor_tensor(csq[:], cT1[:], cT1[:], ALU.mult).then_inc(v.sem, 1)
        with dve.Fori(0, B) as b:
            dve.bn_stats(st[:, b, :], x_all[:, b, :]).then_inc(statd.sem, 1)
        dve.wait_ge(statd.sem, B)
        for b in range(B):
            dve.bn_aggr(mv[:, b, :], st[:, b, :]).then_inc(agg.sem, 1)
        dve.sem_inc(lnd.sem, 2)
        dve.sem_inc(nrm.sem, 2)
        dve.sem_inc(dup.sem, 2)
        dve.wait_ge(roots.sem, 6)

        def dot_up(b):
            dve.wait_ge(dotd.sem, b + 1)
            dve.tensor_copy(dots[:, b, :], pd[:S, 0:E1]).then_inc(dup.sem, 1)

        def norm(b, par):
            dve.wait_ge(kept.sem, b + 1)
            dve.tensor_scalar(xl[:, par, :], x_all[:, b, :], mv[:, b, 0:1], rt[:, 1, bass.ds(b, 1)],
                              ALU.subtract, ALU.mult).then_inc(lnd.sem, 1)
            dve.wait_ge(lnd.sem, b + 3)
            dve.wait_ge(tpd.sem, b - 1) if isinstance(b, int) and b > 1 else None
            dve.wait_ge(nxd.sem, b + 1)
            dve.scalar_tensor_tensor(out=xn[:, par, :], in0=xl[:, par, :], scalar=rt[:, 5, bass.ds(b, 1)], in1=scale[:],
                                     op0=ALU.mult, op1=ALU.mult).then_inc(nrm.sem, 1)

        norm(0, 0)
        norm(1, 1)
        with dve.Fori(1, B // 2) as j:
            for par in range(2):
                b = 2 * j + par
                dot_up(b - 2)
                norm(b, par)
        dot_up(B - 2)
        dot_up(B - 1)

        n = [1]

        def chain(ins):
            n[0] += 1
            ins.then_inc(v.sem, 1)
            dve.wait_ge(v.sem, n[0])

        dve.wait_ge(routed_pe.sem, 1)
        chain(dve.tensor_copy(ny[:], pz[:S, 0:E1]))
        dve.wait_ge(nxd.sem, B + 2)
        dve.wait_ge(dup.sem, B + 2)
        chain(dve.tensor_tensor(dist[:], nx[:, :].unsqueeze(2).to_broadcast([S, B, E1]),
                                ny[:, :].unsqueeze(1).to_broadcast([S, B, E1]), ALU.add))
        chain(dve.scalar_tensor_tensor(out=dist[:], in0=dots[:], scalar=2.0, in1=dist[:], op0=ALU.mult, op1=ALU.subtract))
        chain(dve.tensor_reduce(best[:, 0, :], dist[:], AX.X, ALU.max))
        chain(dve.tensor_tensor(cand[:], dist[:], best[:, 0, :].unsqueeze(2).to_broadcast([S, B, E1]), ALU.is_ge))
        chain(dve.tensor_tensor(cand[:], cand[:], rank_e[:, :].unsqueeze(1).to_broadcast([S, B, E1]), ALU.mult))
        dve.tensor_reduce(best[:, 1, :], cand[:], AX.X, ALU.max).then_inc(statd.sem, 1)
        dve.wait_ge(statd.sem, B + 1)
        chain(dve.tensor_tensor(ohb[:], cand[:], best[:, 1, :].unsqueeze(2).to_broadcast([S, B, E1]), ALU.is_equal))
        chain(dve.tensor_copy(oh[:], ohb[:]))
        dve.wait_ge(routed_pe.sem, 2)
        chain(dve.tensor_copy(cnt[:], pz[:S, 0:BE].rearrange("s (b e) -> s b e", b=B)))
        src = cnt
        for k in range(4):
            w, dst = 1 << k, cum[:, k % 2]
            prev = src[:, :, :] if k == 0 else src
            dve.tensor_copy(dst[:, 0:w, :], prev[:, 0:w, :])
            chain(dve.tensor_tensor(dst[:, w:B, :], prev[:, w:B, :], prev[:, 0:B - w, :], ALU.add))
            src = dst
        total = src[:, B - 1, :]
        chain(dve.tensor_tensor(more[:], total.unsqueeze(2).to_broadcast([S, E1, B * S // P]), kk[:], ALU.is_gt))
        chain(dve.tensor_reduce(tiles[:], more[:], AX.X, ALU.add))
        chain(dve.tensor_tensor(lt[:], tiles[:, :].unsqueeze(1).to_broadcast([S, E1, E1]), less[:], ALU.mult))
        chain(dve.tensor_reduce(start[:], lt[:], AX.X, ALU.add))
        chain(dve.tensor_tensor(end[:], start[:], tiles[:], ALU.add))
        chain(dve.tensor_tensor(passed[:], end[:, :].unsqueeze(1).to_broadcast([S, MT, E1]), tj[:], ALU.is_le))
        chain(dve.tensor_reduce(texp[:], passed[:], AX.X, ALU.add))
        chain(dve.tensor_scalar(texp_i[:], texp[:], float(E1 - 1), None, ALU.min))
        dve.tensor_tensor(rank[:], src, cnt[:], ALU.subtract).then_inc(statd.sem, 1)
        dve.wait_ge(statd.sem, B + 2)
        dve.tensor_tensor(rank[:], pd[:S, 0:BE].rearrange("s (b e) -> s b e", b=B), rank[:], ALU.add).then_inc(statd.sem, 1)
        dve.wait_ge(statd.sem, B + 3)
        dve.tensor_scalar(start[:], start[:], float(P), None, ALU.mult).then_inc(statd.sem, 1)
        dve.wait_ge(statd.sem, B + 4)
        dve.tensor_tensor(rank[:], rank[:], start[:, :].unsqueeze(1).to_broadcast([S, B, E1]), ALU.add).then_inc(statd.sem, 1)
        dve.wait_ge(statd.sem, B + 5)
        dve.tensor_tensor(rank[:], rank[:], oh[:], ALU.mult).then_inc(statd.sem, 1)
        dve.wait_ge(statd.sem, B + 6)
        dve.tensor_reduce(place[:], rank[:], AX.X, ALU.add).then_inc(statd.sem, 1)
        dve.wait_ge(statd.sem, B + 7)
        chain(dve.tensor_copy(place_i[:], place[:]))

        def turned(j, par, first):
            dve.wait_ge(t_pe.sem, j + 1)
            if not first:
                dve.wait_ge(up_a.sem, j - 1)
            dve.tensor_copy(xT[:, par].rearrange("p c s -> p (c s)"), pt[:, 0:DC * P]).then_inc(t_up.sem, 1)

        def results(j, par, early):
            dve.wait_ge(y_pe.sem, j + 1)
            if not early:
                dve.wait_ge(y_out[par].sem, 8 * (j - par))
            dve.tensor_copy(ysb[:, par, :], py[:, 0:D]).then_inc(y_up.sem, 1)

        def body(j, par, first, full):
            dve.wait_ge(thd.sem, j + 1)
            if full:
                dve.wait_ge(z_pe.sem, j - 1)
            dve.scalar_tensor_tensor(out=u[:, par, :], in0=th[:, par, :], scalar=1.0, in1=ph[:, par, 1, :],
                                     op0=ALU.add, op1=ALU.mult).then_inc(lnd.sem, 1)
            dve.wait_ge(lnd.sem, j + B + 3)
            dve.wait_ge(up_a.sem, j + 1)
            dve.scalar_tensor_tensor(out=u[:, par, :], in0=u[:, par, :], scalar=0.5, in1=ph[:, par, 0, :],
                                     op0=ALU.mult, op1=ALU.mult).then_inc(gated.sem, 1)
            if not (isinstance(j, int) and j == MT - 1):
                turned(j + 1, 1 - par, isinstance(j, int) and j == 0)
            if not first:
                results(j - 1, 1 - par, isinstance(j, int) and j <= 2)

        turned(0, 0, True)
        tiles_loop(dve, body)
        results(MT - 1, 0, False)
        for b in range(B):
            if b % GB == 0:
                dve.wait_ge(gathered[b // GB].sem, 16 * GB)
            dve.tensor_tensor(x_all[:, b, :], x_all[:, b, :], yg[:, b, :], ALU.add).then_inc(added.sem, 1)

    @block.gpsimd
    def _(pool):
        pool.memset(mhalf[:], -0.5).then_inc(made.sem, 1)
        pool.memset(zeros[:], 0.0).then_inc(made.sem, 1)
        pool.memset(onesf[:], 1.0).then_inc(made.sem, 1)
        pool.memset(onesb[:], 1.0).then_inc(made.sem, 1)
        pool.memset(before[:], 1.0).then_inc(made.sem, 1)
        pool.memset(less[:], 1.0).then_inc(made.sem, 1)
        pool.wait_ge(made.sem, 6)
        pool.affine_select(out=before[:], in_=before[:], compare_op=ALU.is_gt, fill=0.0, base=0,
                           pattern=[[1, S]], channel_multiplier=-1).then_inc(made.sem, 1)
        pool.affine_select(out=less[:], in_=less[:], compare_op=ALU.is_gt, fill=0.0, base=0,
                           pattern=[[1, E1], [-1, E1]], channel_multiplier=0).then_inc(made.sem, 1)
        pool.iota(rank_e[:], [[-1, E1]], base=E1, channel_multiplier=0, allow_small_or_imprecise_dtypes=True).then_inc(made.sem, 1)
        pool.iota(kk[:], [[0, E1], [P, B * S // P]], base=0, channel_multiplier=0, allow_small_or_imprecise_dtypes=True).then_inc(made.sem, 1)
        pool.iota(tj[:], [[1, MT], [0, E1]], base=0, channel_multiplier=0, allow_small_or_imprecise_dtypes=True).then_inc(made.sem, 1)
        pool.engine_nop().then_inc(made.sem, 1)
        pool.wait_ge(agg.sem, B)
        half = mhalf[:S, 0:1].to_broadcast([S, B])
        pool.tensor_scalar(rt[:, 0, :], mv[:, :, 1], LN_EPS, None, ALU.add).then_inc(roots.sem, 1)
        pool.wait_ge(roots.sem, 1)
        pool.tensor_tensor(rt[:, 1, :], rt[:, 0, :], half, ALU.pow).then_inc(roots.sem, 1)
        pool.wait_ge(roots.sem, 2)
        pool.tensor_tensor(rt[:, 2, :], mv[:, :, 1], rt[:, 1, :], ALU.mult).then_inc(roots.sem, 1)
        pool.wait_ge(roots.sem, 3)
        pool.tensor_tensor(rt[:, 3, :], rt[:, 2, :], rt[:, 1, :], ALU.mult).then_inc(roots.sem, 1)
        pool.wait_ge(roots.sem, 4)
        pool.tensor_scalar(rt[:, 4, :], rt[:, 3, :], RMS_EPS, None, ALU.add).then_inc(roots.sem, 1)
        pool.wait_ge(roots.sem, 5)
        pool.tensor_tensor(rt[:, 5, :], rt[:, 4, :], half, ALU.pow).then_inc(roots.sem, 1)
        pool.sem_inc(kept.sem, 2)
        with pool.Fori(0, B // 2) as j:
            for par in range(2):
                b = 2 * j + par
                pool.wait_ge(nrm.sem, b + 3)
                pool.sem_inc(apart.sem, 1)
                pool.tensor_tensor(x_all[:, b, :], x_all[:, b, :], xl[:, par, :], ALU.add)
                pool.tensor_copy(xn_all[:, b, :], xn[:, par, :]).then_inc(kept.sem, 1)
        pool.wait_ge(zeroed.sem, 16)
        pool.wait_ge(v.sem, 23)
        pool.wait_ge(kept.sem, B + 2)
        for b in range(B):
            pool.indirect_dma_start(out=xs, out_offset=bass.IndirectOffsetOnAxis(ap=place_i[:, b:b + 1], axis=0),
                                    in_=xn_all[:, b, :], in_offset=None).then_inc(scattered.sem, 16)
        pool.wait_ge(y_out[0].sem, 16 * ((MT + 1) // 2))
        pool.wait_ge(y_out[1].sem, 16 * (MT // 2))
        for b in range(B):
            pool.indirect_dma_start(out=yg[:, b, :], out_offset=None, in_=ys,
                                    in_offset=bass.IndirectOffsetOnAxis(ap=place_i[:, b:b + 1], axis=0)).then_inc(gathered[b // GB].sem, 16)


def program(nc, a, out):
    with ExitStack() as ctx:
        def sb(c, name, shape, dt=F32):
            return c.enter_context(nc.sbuf_tensor(name, shape, dt))

        t = {"x_all": sb(ctx, "x_all", [S, B, D]), "ident": sb(ctx, "ident", [P, P])}
        with ExitStack() as dense:
            t.update({"xnT_all": sb(dense, "xnT_all", [P, DC, B * S]), "gates": sb(dense, "gates", [S, B, E0]),
                      "w1": sb(dense, "w1", [P, DC, E0 * F0]), "b1": sb(dense, "b1", [P, E0]), "w2": sb(dense, "w2", [P, E0, D])})
            for phase in (phase_1, phase_2):
                with ExitStack() as own:
                    phase(nc, own, a, t)
                nc.all_engine_barrier()
        with ExitStack() as own:
            phase_3(nc, own, a, t)
        nc.all_engine_barrier()
        with ExitStack() as own:
            phase_4(nc, own, a, t, out)


def lay_out(**x):
    import numpy as np
    x = {k: np.asarray(v) for k, v in x.items()}
    c = np.ascontiguousarray

    def heads(w):
        return c(w.transpose(1, 0, 2).reshape(D, H * DK))

    def padded(w):
        w = w.reshape(H, DK, -1)
        return c(np.concatenate([w, np.zeros((H, HP - DK, w.shape[2]), w.dtype)], 1).reshape(H * HP, -1))

    def columns(v):
        return c(v.reshape(-1, P).T)

    return {
        "x": c(x["x"]),
        "ctx": c(x["ctx_1024"]),
        "ctxT": c(x["ctx_1024"].transpose(0, 2, 1)),
        "mask": c(x["mask_BxSxS2_bk1"]),
        "wq": heads(x["L0_xattn_Wq"]), "wk": heads(x["L0_xattn_Wk"]), "wv": heads(x["L0_xattn_Wv"]),
        "bq": columns(x["L0_xattn_bq"].reshape(-1)), "bk": columns(x["L0_xattn_bk"].reshape(-1)),
        "bv": columns(padded(x["L0_xattn_bv"].reshape(-1, 1)).reshape(-1)),
        "wo": padded(x["L0_xattn_Wo"]), "bo": c(x["L0_xattn_bo"]),
        "w1": c(x["L0_ffn_w1"].transpose(1, 0, 2).reshape(D, E0 * F0)), "b1": c(x["L0_ffn_b1"].T),
        "w2": c(x["L0_ffn_w2"]), "b2": c(x["L0_ffn_b2"]), "cent": c(x["L0_ffn_centroids"]),
        "w_routeT": c(x["L0_ffn_w_route"].T),
        "xwq": c(x["L1_xattn_Wq"]), "xwk": c(x["L1_xattn_Wk"]), "xwv": c(x["L1_xattn_Wv"]),
        "wihT": c(x["L1_xattn_gru_wih"].T), "whhT": c(x["L1_xattn_gru_whh"].T),
        "bih": columns(x["L1_xattn_gru_bih"]), "bhh": columns(x["L1_xattn_gru_bhh"]),
        "slot_w": columns(x["L1_xattn_slot_norm_w"]), "in_w": columns(x["L1_xattn_input_norm_w"]), "in_w_row": c(x["L1_xattn_input_norm_w"].reshape(1, D)),
        "scale": c(x["L1_ffn_scale"].reshape(1, D)), "centT": c(x["L1_ffn_centroids"].T), "cent1": c(x["L1_ffn_centroids"]),
        "up": c(x["L1_ffn_up_w"]), "down": c(x["L1_ffn_down_w"]),
    }


def kernel(**inputs):
    import numpy as np
    import concourse.bacc as bacc
    from concourse import mybir as _mybir
    from concourse.bass_utils import run_bass_kernel_spmd

    nc = bacc.Bacc("TRN2", target_bir_lowering=False, num_devices=1)
    arrays, aps = {}, {}
    for name, array in lay_out(**inputs).items():
        arrays[f"in_{name}_dram"] = array
        aps[name] = nc.dram_tensor(f"in_{name}_dram", array.shape, _mybir.dt.from_np(array.dtype), kind="ExternalInput").ap()
    out = nc.dram_tensor("out_0_dram", (B, S, D), _mybir.dt.from_np(np.dtype("float32")), kind="ExternalOutput").ap()
    program(nc, aps, out)
    result = run_bass_kernel_spmd(nc, [arrays], core_ids=[0])
    return result.results[0]["out_0_dram"]
```

```python
from contextlib import ExitStack

import concourse.bass as bass
from concourse import mybir

F32 = mybir.dt.float32
F32R = mybir.dt.float32r
BF16 = mybir.dt.bfloat16
U8 = mybir.dt.uint8
U32 = mybir.dt.uint32
I32 = mybir.dt.int32
ALU = mybir.AluOpType
ACT = mybir.ActivationFunctionType
AX = mybir.AxisListType

B, S, D, KEYS = 16, 112, 256, 375
P = 128
DC = D // P
H, DK = 16, 16
HC = P // DK
KT = 3
KP = KEYS // KT
HP = 32
HG = H // 4
E0, F0 = 8, 128
E1, F1 = 8, 512
GB = 4
NG = B // GB
GN = GB * S
LN_EPS, RMS_EPS, SLOT_EPS = 1e-5, 1e-6, 1e-6
NORM_EPS = 1e-12
ROUNDS = 3
MASKED = -1e-6
MT = (B * S) // P + E1 - 1


class Sig:

    def __init__(self, sem, per=1):
        self.sem, self.per = sem, per

    def __call__(self, i, k):
        return self.sem, i * self.per + k


def norm_roots(pool, sig, wait, apart, mv, half, tmp, mean, roots, at):
    var = mv[:, :, 1]
    pool.sem_inc(apart.sem, 1)
    pool.tensor_scalar(tmp[:, 0, :], var, LN_EPS, None, ALU.add).then_inc(sig.sem, 1)
    pool.wait_ge(*wait(1))
    pool.sem_inc(apart.sem, 1)
    pool.tensor_tensor(roots[:, 0, at], tmp[:, 0, :], half, ALU.pow).then_inc(sig.sem, 1)
    pool.wait_ge(*wait(2))
    pool.sem_inc(apart.sem, 1)
    pool.tensor_tensor(tmp[:, 1, :], var, roots[:, 0, at], ALU.mult).then_inc(sig.sem, 1)
    pool.wait_ge(*wait(3))
    pool.sem_inc(apart.sem, 1)
    pool.tensor_tensor(tmp[:, 2, :], tmp[:, 1, :], roots[:, 0, at], ALU.mult).then_inc(sig.sem, 1)
    pool.wait_ge(*wait(4))
    pool.sem_inc(apart.sem, 1)
    pool.tensor_scalar(tmp[:, 3, :], tmp[:, 2, :], RMS_EPS, None, ALU.add).then_inc(sig.sem, 1)
    pool.wait_ge(*wait(5))
    pool.sem_inc(apart.sem, 1)
    pool.tensor_tensor(roots[:, 1, at], tmp[:, 3, :], half, ALU.pow).then_inc(sig.sem, 1)
    pool.sem_inc(apart.sem, 1)
    pool.tensor_copy(mean[:, at], mv[:, :, 0]).then_inc(sig.sem, 1)


def phase_1(nc, ctx, a, t):
    def sb(name, shape, dt=F32):
        return ctx.enter_context(nc.sbuf_tensor(name, shape, dt))

    def psum(name, shape):
        return ctx.enter_context(nc.psum_tensor(name, shape, F32))

    def sem(name, per=1):
        return Sig(ctx.enter_context(nc.semaphore(name)), per)

    x_all, ident, xnT_all, gates_all = t["x_all"], t["ident"], t["xnT_all"], t["gates"]
    R = 4
    LT, LA = 2, 3

    wq = sb("wq", [P, DC, D])
    wk = sb("wk", [P, DC, D])
    wv = sb("wv", [P, DC, D])
    wo = sb("wo", [P, HG, D])
    bq = sb("bq", [P, DC])
    bk = sb("bk", [P, DC])
    bv = sb("bv", [P, HG])
    bo = sb("bo", [1, D])
    bvb = sb("bvb", [P, HG, P])
    bvo = sb("bvo", [P, D])
    b2 = sb("b2", [E0, D])
    cent = sb("cent", [E0, D])
    csq = sb("csq", [E0, D])
    cn = sb("cn", [E0, 3])
    cr = sb("cr", [P, DC, 2 * E0])
    hmask = sb("hmask", [P, HC])
    ones = sb("ones", [P, P])
    mhalf = sb("mhalf", [P, 1])
    ctxT = [sb(f"ctxT{i}", [P, DC, KEYS]) for i in range(2)]
    mask8 = [sb(f"mask8_{i}", [S, KEYS], U8) for i in range(2)]
    maskf = [sb(f"maskf{i}", [S, KEYS]) for i in range(2)]
    kT = [sb(f"kT{i}", [P, DC, KEYS]) for i in range(2)]
    v = [sb(f"v{i}", [KP, KT, H, HP]) for i in range(2)]
    qm = [sb(f"qm{i}", [P, H, S]) for i in range(2)]
    nmax = [sb(f"nmax{i}", [S, H]) for i in range(2)]
    esum = [sb(f"esum{i}", [S, H]) for i in range(2)]
    st, mv, rstd = sb("st", [S, 6]), sb("mv", [S, 2]), sb("rstd", [S, 2])
    xn, xnT, qT = sb("xn", [S, D]), sb("xnT", [P, DC, S]), sb("qT", [P, DC, S])
    rec, recx = sb("rec", [S, H]), sb("recx", [S, H, HP])
    oT, oTn = sb("oT", [P, HG, S]), sb("oTn", [P, HG, S])
    st2, mv2, rs2 = sb("st2", [S, 6]), sb("mv2", [S, 2]), sb("rs2", [S, 6])
    xn2, xnT2 = sb("xn2", [S, D]), sb("xnT2", [P, DC, S])
    lg, lgt, top, keep = sb("lg", [S, 2 * E0]), sb("lgt", [S, E0]), sb("top", [S, 8]), sb("keep", [S, E0])
    ntop, eg, ek = sb("ntop", [S, 1]), sb("eg", [S, E0]), sb("ek", [S, E0])
    gs, gr, gate, gT = sb("gs", [S, 1]), sb("gr", [S, 1]), sb("gate", [S, E0]), sb("gT", [E0, S])
    sm = sb("sm", [S, R, KEYS])
    ex = sb("ex", [S, R, KEYS])
    eT = sb("eT", [KP, R, KT, S])

    ps = psum("ps", [P, 2, 512])
    pt = psum("pt", [P, 2, 512])
    po = psum("po", [P, 2, 512])
    pf = psum("pf", [P, 2, 512])

    NW = 11
    NF, NT = 6, 6
    w_in, x_in, w2_in = sem("w_in"), sem("x_in"), sem("w2_in")
    apart = sem("apart")
    made = sem("made")
    su_d, su_p, su_pe = sem("su_d"), sem("su_p"), sem("su_pe")
    loaded = [sem("loaded0", 32), sem("loaded1", 32)]
    conv = sem("conv")
    scored = sem("scored", H)
    masked = sem("masked", H)
    maxed = sem("maxed", H)
    exped = sem("exped", H)
    turned = sem("turned", H)
    eT_up = sem("eT_up", H)
    times_v = sem("times_v", H)
    f_pe, f_ev = sem("f_pe", NF), sem("f_ev", NF)
    t_pe, t_ev = sem("t_pe", NT), sem("t_ev", NT)
    f_d, f_p = sem("f_d", 3), sem("f_p", 3)
    qm_up = sem("qm_up", DC)
    t_d, t_p = sem("t_d", 13), sem("t_p", 8)
    recd = sem("recd", 1)
    t_a = sem("t_a", 1)
    oT_up = sem("oT_up", 1)

    PF = [("f", 0, 2), ("t", 0, 3), ("f", 1, 4), ("t", 1, 5), ("f", 2, 6), ("f", 3, 7), ("t", 2, 8),
          ("f", 4, 9), ("t", 3, 10), ("f", 5, 12), ("t", 4, 13), ("t", 5, 15)]
    BANK = {(k, n): i % 2 for i, (k, n, _) in enumerate(PF)}

    def last_use(k, n, b, prev, nxt):
        i = [u[:2] for u in PF].index((k, n))
        here = [u for j, u in enumerate(PF[:i]) if j % 2 == i % 2 and (nxt if u[0] == "f" else prev)]
        if here:
            kk, m, _ = here[-1]
            return f_ev(b + 1, m + 1) if kk == "f" else t_ev(b - 1, m + 1)
        static = isinstance(b, int)
        before = [u for j, u in enumerate(PF) if j % 2 == i % 2 and (u[0] == "f" or not (static and b <= 1))]
        kk, m, _ = before[-1]
        return f_ev(b, m + 1) if kk == "f" else t_ev(b - 2, m + 1)

    def fbank(k, n):
        return pf[:, BANK[(k, n)], :]

    def bodies(eng, body):
        body(0, 0, False, True)
        body(1, 1, True, True)
        with eng.Fori(1, B // 2 - 1) as j:
            body(2 * j, 0, True, True)
            body(2 * j + 1, 1, True, True)
        body(B - 2, 0, True, True)
        body(B - 1, 1, True, False)

    block = ctx.enter_context(nc.Block())

    @block.sync
    def _(sp):
        def load(b, par):
            sp.dma_start(ctxT[par][:], a["ctxT"][b].rearrange("(c p) m -> p c m", p=P)).then_inc(loaded[par].sem, 16)
            sp.dma_start(mask8[par][:], a["mask"][b]).then_inc(loaded[par].sem, 16)

        sp.dma_start(x_all[:], a["x"].rearrange("b s d -> s b d")).then_inc(x_in.sem, 16)
        load(0, 0)
        for dst, src in ((wq[:], a["wq"].rearrange("(c p) n -> p c n", p=P)),
                         (wk[:], a["wk"].rearrange("(c p) n -> p c n", p=P)),
                         (wv[:], a["wv"].rearrange("(c p) n -> p c n", p=P)),
                         (bq[:], a["bq"]),
                         (bk[:], a["bk"]),
                         (cent[:], a["cent"]),
                         (cr[:, :, E0:2 * E0], a["w_routeT"].rearrange("(c p) e -> p c e", p=P)),
                         (wo[:], a["wo"].rearrange("(c p) n -> p c n", p=P)),
                         (bv[:], a["bv"]),
                         (bo[:], a["bo"].rearrange("(o n) -> o n", o=1)),
                         (b2[:], a["b2"])):
            sp.dma_start(dst, src).then_inc(w_in.sem, 16)
        load(1, 1)
        sp.dma_start(t["w1"], a["w1"].rearrange("(c p) n -> p c n", p=P)).then_inc(w2_in.sem, 16)
        sp.dma_start(t["w2"], a["w2"].rearrange("e p n -> p e n")).then_inc(w2_in.sem, 16)
        sp.dma_start(t["b1"][:], a["b1"]).then_inc(w2_in.sem, 16)

        slot_weight_loads(sp, a, t)
        for i in range(GB):
            context_loads(sp, a, i, t["cx0"], t["cT0"], i, t["c_in0"])

        with sp.Fori(0, B // 2 - 1) as j:
            for par in range(2):
                sp.wait_ge(*f_pe(2 * j + par, NF))
                sp.sem_inc(apart.sem, 1)
                sp.wait_ge(*conv(2 * j + par, 1))
                sp.sem_inc(apart.sem, 1)
                load(2 * j + par + 2, par)
        sp.wait_ge(w2_in.sem, 48)

    @block.tensor
    def _(pe):
        def front(b, n, par):
            out = fbank("f", n)
            if n == 0:
                pe.wait_ge(*f_d(b, 3))
                for c in range(DC):
                    m = pe.transpose(out[:, c * S:(c + 1) * S], xn[:, c * P:(c + 1) * P], ident[:S, :S])
            elif n == 1:
                pe.wait_ge(*f_ev(b, 1))
                for o in range(DC):
                    for c in range(DC):
                        m = pe.matmul(out[:, o * S:(o + 1) * S], wq[:, c, o * P:(o + 1) * P], xnT[:, c, :],
                                      start=(c == 0), stop=(c == DC - 1))
            elif n in (2, 3):
                o = n - 2
                if n == 2:
                    pe.wait_ge(loaded[par].sem, 16 * (b - par) + 32)
                for c in range(DC):
                    m = pe.matmul(out[:, 0:KEYS], wk[:, c, o * P:(o + 1) * P], ctxT[par][:, c, :],
                                  start=(c == 0), stop=(c == DC - 1))
            else:
                for kt in ((0, 1) if n == 4 else (2,)):
                    for c in range(DC):
                        m = pe.matmul(out[:KP, kt % 2 * D:(kt % 2 + 1) * D], ctxT[par][:, c, kt * KP:(kt + 1) * KP],
                                      wv[:, c, :], start=(c == 0), stop=(c == DC - 1))
            m.then_inc(f_pe.sem, 1)

        def tail(b, n):
            out = fbank("t", n)
            if n == 0:
                pe.wait_ge(*t_d(b, 1))
                for g in range(HG):
                    m = pe.transpose(out[:, g * S:(g + 1) * S],
                                     recx[:, 4 * g:4 * g + 4, :].rearrange("s h p -> s (h p)"), ident[:S, :S])
            elif n == 1:
                pe.wait_ge(*t_ev(b, 1))
                for g in range(HG):
                    m = pe.matmul(out[:S, 0:D], oTn[:, g, :], wo[:, g, :], start=(g == 0), stop=(g == HG - 1))
            elif n == 2:
                pe.wait_ge(*t_d(b, 4))
                for c in range(DC):
                    m = pe.transpose(out[:, c * S:(c + 1) * S], xn2[:, c * P:(c + 1) * P], ident[:S, :S])
            elif n == 3:
                pe.wait_ge(*t_ev(b, 3))
                for c in range(DC):
                    m = pe.matmul(out[:S, 0:2 * E0], xnT2[:, c, :], cr[:, c, :], start=(c == 0), stop=(c == DC - 1))
            elif n == 4:
                pe.wait_ge(*t_d(b, 13))
                m = pe.transpose(out[:E0, 0:S], gate[:, :], ident[:S, :S])
            else:
                pe.wait_ge(*t_ev(b, 5))
                m = pe.matmul(out[:S, 0:D], gT[:, :], b2[:, :], start=True, stop=True)
            m.then_inc(t_pe.sem, 1)

        def score(b, s, par, ring_full):
            if ring_full:
                pe.wait_ge(*masked(b, s - 1))
            pe.matmul(ps[:S, s % 2, 0:KEYS], qm[par][:, s, :], kT[par][:, s // HC, :],
                      start=True, stop=True).then_inc(scored.sem, 1)

        def turn(b, s, ring_full):
            pe.wait_ge(*exped(b, s + 1))
            if ring_full:
                pe.wait_ge(*eT_up(b, s - 1))
            for kt in range(KT):
                m = pe.transpose(pt[:KP, s % 2, kt * S:(kt + 1) * S], ex[:, s % R, kt * KP:(kt + 1) * KP], ident[:S, :S])
            m.then_inc(turned.sem, 1)

        def attend(b, s, par, wait_out):
            hh = s % H
            g, j = hh // 4, hh % 4
            pe.wait_ge(*eT_up(b, s + 1))
            if wait_out:
                pe.wait_ge(*oT_up(b - 2, 1))
            for kt in range(KT):
                m = pe.matmul(po[j * HP:(j + 1) * HP, par, g * S:(g + 1) * S], v[par][:, kt, hh, :],
                              eT[:, s % R, kt, :], start=(kt == 0), stop=(kt == KT - 1))
            m.then_inc(times_v.sem, 1)

        def body(b, par, prev, nxt):
            pe.wait_ge(*qm_up(b, DC))
            pe.wait_ge(*f_ev(b, NF))
            for s in range(H):
                score(b, s, par, prev or s >= 2)
                if prev or s >= LT:
                    turn(b, s - LT, prev or s >= LT + 2)
                if prev or s >= LA:
                    mine = s >= LA
                    attend(b, s - LA, par if mine else 1 - par, s == LA and not (isinstance(b, int) and b < 2))
                for k, n, at in PF:
                    if at == s and (nxt if k == "f" else prev):
                        pe.wait_ge(*last_use(k, n, b, prev, nxt))
                        if k == "f":
                            front(b + 1, n, 1 - par)
                        else:
                            tail(b - 1, n)

        pe.wait_ge(made.sem, 6)
        pe.wait_ge(w_in.sem, 16 * NW)
        pe.wait_ge(su_d.sem, 2)
        for g in range(HG):
            pe.matmul(pf[:, 0, 0:D], bvb[:, g, :], wo[:, g, :], start=(g == 0), stop=False)
        pe.matmul(pf[:, 0, 0:D], ones[0:1, :], bo[:, :], start=False, stop=True)
        pe.wait_ge(su_d.sem, 3)
        for c in range(DC):
            m = pe.transpose(pf[:, 1, c * E0:(c + 1) * E0], csq[:, c * P:(c + 1) * P], ident[:E0, :E0])
        m.then_inc(su_pe.sem, 1)
        pe.wait_ge(su_d.sem, 5)
        pe.wait_ge(made.sem, 8)
        for n in range(NF):
            if n == 3:
                pe.wait_ge(*f_ev(0, 2))
            elif n == 2:
                pass
            elif n == 4:
                pe.wait_ge(*f_ev(0, 3))
            elif n == 5:
                pe.wait_ge(*f_ev(0, 4))
            if n:
                pe.wait_ge(*f_ev(0, n))
            front(0, n, 0)
        bodies(pe, body)
        last = B - 1
        for s in range(H - LT, H):
            turn(last, s, True)
            attend(last, s - LA + LT, 1, False)
        for s in range(H - LA + LT, H):
            attend(last, s, 1, False)
        for n in range(NT):
            pe.wait_ge(*(t_ev(last, n) if n else t_ev(last - 1, NT)))
            tail(last, n)

    @block.scalar
    def _(act):
        def exp(b, s, par, ring_full):
            act.wait_ge(*maxed(b, s + 1))
            if ring_full:
                act.wait_ge(*turned(b, s - R + 1))
            act.activation(ex[:, s % R, :], sm[:, s % R, :], ACT.Exp, bias=nmax[par][:, s % H:s % H + 1],
                           accum_out=esum[par][:, s % H:s % H + 1]).then_inc(exped.sem, 1)

        def up(b, s, ring_full):
            act.wait_ge(*turned(b, s + 1))
            if ring_full:
                act.wait_ge(*times_v(b, s - R + 1))
            act.activation(eT[:, s % R, :, :].rearrange("p t s -> p (t s)"), pt[:KP, s % 2, 0:KT * S],
                           ACT.Copy).then_inc(eT_up.sem, 1)

        def o_up(b, par, first):
            act.wait_ge(*times_v(b, H))
            if not first:
                act.wait_ge(*t_ev(b - 1, 1))
            act.activation(oT[:, :, :].rearrange("p g s -> p (g s)"), po[:, par, 0:HG * S], ACT.Copy).then_inc(oT_up.sem, 1)

        def gate_exp(b):
            act.wait_ge(*t_d(b, 9))
            act.activation(eg[:], lgt[:], ACT.Exp, bias=ntop[:]).then_inc(t_a.sem, 1)

        def body(b, par, prev, nxt):
            for s in range(H):
                if prev or s >= 1:
                    exp(b, s - 1, par if s >= 1 else 1 - par, prev or s >= R + 1)
                if prev or s >= LT:
                    up(b, s - LT, prev or s >= R + LT)
                if prev and s == LA:
                    o_up(b - 1, 1 - par, isinstance(b, int) and b == 1)
                if prev and s == 11:
                    gate_exp(b - 1)

        bodies(act, body)
        last = B - 1
        exp(last, H - 1, 1, True)
        for s in range(H - LT, H):
            up(last, s, True)
        o_up(last, 1, False)
        gate_exp(last)

    @block.vector
    def _(dve):
        def mask_max(b, s, par, ring_full):
            if s == 0:
                dve.wait_ge(*conv(b, 1))
            dve.wait_ge(*scored(b, s + 1))
            if ring_full:
                dve.wait_ge(*exped(b, s - R + 1))
            dve.scalar_tensor_tensor(out=sm[:, s % R, :], in0=ps[:S, s % 2, 0:KEYS], scalar=-MASKED,
                                     in1=maskf[par][:], op0=ALU.add, op1=ALU.mult).then_inc(masked.sem, 1)
            dve.wait_ge(*masked(b, s + 1))
            dve.tensor_reduce(nmax[par][:, s:s + 1], sm[:, s % R, :], AX.X, ALU.max, negate=True).then_inc(maxed.sem, 1)

        def stats(b):
            dve.sem_inc(apart.sem, 1)
            dve.bn_stats(st[:], x_all[:, b, :]).then_inc(f_d.sem, 1)
            dve.wait_ge(*f_d(b, 1))
            dve.sem_inc(apart.sem, 1)
            dve.bn_aggr(mv[:], st[:]).then_inc(f_d.sem, 1)

        def normalise(b, first):
            dve.wait_ge(*f_p(b, 2))
            if not first:
                dve.wait_ge(*f_pe(b - 1, 1))
            dve.tensor_scalar(xn[:], x_all[:, b, :], mv[:, 0:1], rstd[:, 1:2], ALU.subtract, ALU.mult).then_inc(f_d.sem, 1)

        def front(b, n, par, first):
            src = fbank("f", n)
            dve.wait_ge(*f_pe(b, n + 1))
            if n == 0:
                m = dve.tensor_copy(xnT[:, :, :].rearrange("p c s -> p (c s)"), src[:, 0:DC * S])
            elif n == 1:
                if not first:
                    dve.wait_ge(*qm_up(b - 1, DC))
                for c in range(DC):
                    m = dve.tensor_scalar(qT[:, c, :], src[:, c * S:(c + 1) * S], bq[:, c:c + 1], DK ** -0.5,
                                          ALU.add, ALU.mult)
            elif n in (2, 3):
                m = dve.tensor_scalar(kT[par][:, n - 2, :], src[:, 0:KEYS], bk[:, n - 2:n - 1], None, ALU.add)
            elif n == 4:
                m = dve.tensor_copy(v[par][:, 0:2, :, 0:DK], src[:KP, 0:2 * D].rearrange("p (t h d) -> p t h d", t=2, h=H))
            else:
                m = dve.tensor_copy(v[par][:, 2, :, 0:DK], src[:KP, 0:D].rearrange("p (h d) -> p h d", h=H))
            m.then_inc(f_ev.sem, 1)

        def recip(b, par, first):
            dve.wait_ge(*exped(b, H))
            dve.reciprocal(rec[:], esum[par][:]).then_inc(recd.sem, 1)
            dve.wait_ge(*recd(b, 1))
            if not first:
                dve.wait_ge(*t_pe(b - 1, 1))
            dve.tensor_copy(recx[:], rec[:, :].unsqueeze(2).to_broadcast([S, H, HP])).then_inc(t_d.sem, 1)

        def tail(b, n, first):
            src = fbank("t", n)
            dve.wait_ge(*t_pe(b, n + 1))
            if n == 0:
                dve.wait_ge(*oT_up(b, 1))
                if not first:
                    dve.wait_ge(*t_pe(b - 1, 2))
                dve.tensor_tensor(oTn[:, :, :].rearrange("p g s -> p (g s)"), src[:, 0:HG * S],
                                  oT[:, :, :].rearrange("p g s -> p (g s)"), ALU.mult).then_inc(t_ev.sem, 1)
            elif n == 1:
                dve.wait_ge(*f_p(b, 3))
                dve.tensor_tensor(x_all[:, b, :], src[:S, 0:D], x_all[:, b, :], ALU.add).then_inc(t_ev.sem, 1)
                dve.wait_ge(*t_ev(b, 2))
                dve.sem_inc(apart.sem, 1)
                dve.bn_stats(st2[:], x_all[:, b, :]).then_inc(t_d.sem, 1)
                dve.wait_ge(*t_d(b, 2))
                if not first:
                    dve.wait_ge(*t_p(b - 1, 6))
                dve.sem_inc(apart.sem, 1)
                dve.bn_aggr(mv2[:], st2[:]).then_inc(t_d.sem, 1)
            elif n == 2:
                if not first:
                    dve.wait_ge(*t_p(b - 1, 7))
                dve.tensor_copy(xnT2[:, :, :].rearrange("p c s -> p (c s)"), src[:, 0:DC * S]).then_inc(t_ev.sem, 1)
            elif n == 3:
                dve.tensor_copy(lg[:], src[:S, 0:2 * E0]).then_inc(t_ev.sem, 1)
                dve.wait_ge(*t_ev(b, 4))
                dve.wait_ge(*t_p(b, 6))
                dve.scalar_tensor_tensor(out=lgt[:], in0=lg[:, 0:E0], scalar=rs2[:, 5:6], in1=lg[:, E0:2 * E0],
                                         op0=ALU.mult, op1=ALU.add).then_inc(t_d.sem, 1)
                dve.wait_ge(*t_d(b, 5))
                dve.sem_inc(apart.sem, 1)
                dve.max(top[:], lgt[:]).then_inc(t_d.sem, 1)
                dve.wait_ge(*t_d(b, 6))
                dve.tensor_scalar(keep[:], lgt[:], top[:, 1:2], None, ALU.is_ge).then_inc(t_d.sem, 1)
                dve.tensor_scalar(ntop[:], top[:, 0:1], -1.0, None, ALU.mult).then_inc(t_d.sem, 1)
                dve.engine_nop().then_inc(t_d.sem, 1)
            elif n == 4:
                dve.tensor_copy(gT[:], src[:E0, 0:S]).then_inc(t_ev.sem, 1)
            else:
                dve.tensor_tensor(x_all[:, b, :], src[:S, 0:D], x_all[:, b, :], ALU.add).then_inc(t_ev.sem, 1)

        def normalise2(b):
            dve.wait_ge(*t_p(b, 2))
            dve.tensor_scalar(xn2[:], x_all[:, b, :], mv2[:, 0:1], rs2[:, 1:2], ALU.subtract, ALU.mult).then_inc(t_d.sem, 1)

        def gates(b, first):
            dve.wait_ge(*t_a(b, 1))
            dve.wait_ge(*t_d(b, 9))
            dve.tensor_tensor(ek[:], eg[:], keep[:], ALU.mult).then_inc(t_d.sem, 1)
            dve.wait_ge(*t_d(b, 10))
            dve.tensor_reduce(gs[:], ek[:], AX.X, ALU.add).then_inc(t_d.sem, 1)
            dve.wait_ge(*t_d(b, 11))
            dve.reciprocal(gr[:], gs[:]).then_inc(t_d.sem, 1)
            dve.wait_ge(*t_d(b, 12))
            if not first:
                dve.wait_ge(*t_p(b - 1, 8))
            dve.tensor_scalar(gate[:], ek[:], gr[:], None, ALU.mult).then_inc(t_d.sem, 1)

        def body(b, par, prev, nxt):
            first_t = isinstance(b, int) and b == 1
            for s in range(H):
                mask_max(b, s, par, prev or s >= R)
                if s == H - 1 and not (isinstance(b, int) and b >= B - 2):
                    stats(b + 2)
                if nxt and s == 1:
                    normalise(b + 1, False)
                if prev and s == 1:
                    recip(b - 1, 1 - par, first_t)
                for k, n, at in PF:
                    if at != s - 1 or not (nxt if k == "f" else prev):
                        continue
                    if k == "f":
                        front(b + 1, n, 1 - par, False)
                    else:
                        tail(b - 1, n, first_t)
                if prev and s == 7:
                    normalise2(b - 1)
                if prev and s == 12:
                    gates(b - 1, first_t)
            if prev:
                tail(b - 1, 5, first_t)

        dve.wait_ge(w_in.sem, 16 * NW)
        dve.tensor_copy(bvb[:], bv[:, :].unsqueeze(2).to_broadcast([P, HG, P])).then_inc(su_d.sem, 1)
        dve.tensor_tensor_reduce(csq[:], cent[:], cent[:], 1.0, 0.0, ALU.mult, ALU.add, cn[:, 0:1]).then_inc(su_d.sem, 1)
        dve.wait_ge(su_p.sem, 2)
        dve.tensor_scalar(csq[:], cent[:], cn[:, 2:3], None, ALU.mult).then_inc(su_d.sem, 1)
        dve.wait_ge(su_pe.sem, 1)
        dve.tensor_copy(bvo[:], pf[:, 0, 0:D]).then_inc(su_d.sem, 1)
        dve.tensor_copy(cr[:, :, 0:E0], pf[:, 1, 0:DC * E0].rearrange("p (c e) -> p c e", c=DC)).then_inc(su_d.sem, 1)
        dve.wait_ge(x_in.sem, 16)
        stats(0)
        normalise(0, True)
        stats(1)
        dve.wait_ge(made.sem, 8)
        for n in range(NF):
            front(0, n, 0, True)
        bodies(dve, body)
        last = B - 1
        recip(last, 1, False)
        for n in range(NT):
            tail(last, n, False)
            if n == 1:
                normalise2(last)
            if n == 3:
                gates(last, False)

    @block.gpsimd
    def _(pool):
        def root(b, sig, k, var, tmp, out):
            pool.sem_inc(apart.sem, 1)
            pool.tensor_scalar(tmp, var, LN_EPS, None, ALU.add).then_inc(sig.sem, 1)
            pool.wait_ge(*sig(b, k))
            pool.tensor_tensor(out, tmp, mhalf[:S, :], ALU.pow).then_inc(sig.sem, 1)

        def front(b, par, early):
            pool.wait_ge(*f_d(b, 2))
            root(b, f_p, 1, mv[:, 1:2], rstd[:, 0:1], rstd[:, 1:2])
            pool.wait_ge(loaded[par].sem, 16 * (b - par) + 32)
            if not early:
                pool.wait_ge(*masked(b - 2, H))
            pool.sem_inc(apart.sem, 1)
            pool.tensor_copy(maskf[par][:], mask8[par][:]).then_inc(conv.sem, 1)
            pool.wait_ge(*f_d(b, 3))
            pool.tensor_tensor(x_all[:, b, :], x_all[:, b, :], bvo[:S, :], ALU.add).then_inc(f_p.sem, 1)

        def mask_q(b, par, early):
            pool.wait_ge(*f_ev(b, 2))
            if not early:
                pool.wait_ge(*scored(b - 2, H))
            for c in range(DC):
                pool.tensor_tensor(qm[par][:, c * HC:(c + 1) * HC, :],
                                   qT[:, c, :].unsqueeze(1).to_broadcast([P, HC, S]),
                                   hmask[:, :].unsqueeze(2).to_broadcast([P, HC, S]), ALU.mult).then_inc(qm_up.sem, 1)

        def tail_2(b):
            pool.wait_ge(*t_d(b, 3))
            root(b, t_p, 1, mv2[:, 1:2], rs2[:, 0:1], rs2[:, 1:2])
            pool.wait_ge(*t_p(b, 2))
            pool.tensor_tensor(rs2[:, 2:3], mv2[:, 1:2], rs2[:, 1:2], ALU.mult).then_inc(t_p.sem, 1)
            pool.wait_ge(*t_p(b, 3))
            pool.tensor_tensor(rs2[:, 3:4], rs2[:, 2:3], rs2[:, 1:2], ALU.mult).then_inc(t_p.sem, 1)
            pool.wait_ge(*t_p(b, 4))
            pool.sem_inc(apart.sem, 1)
            pool.tensor_scalar(rs2[:, 4:5], rs2[:, 3:4], float(D), NORM_EPS ** 2, ALU.mult, ALU.max).then_inc(t_p.sem, 1)
            pool.wait_ge(*t_p(b, 5))
            pool.tensor_tensor(rs2[:, 5:6], rs2[:, 4:5], mhalf[:S, :], ALU.pow).then_inc(t_p.sem, 1)

        def tail_3(b):
            pool.wait_ge(*t_ev(b, 3))
            pool.sem_inc(apart.sem, 1)
            pool.tensor_copy(xnT_all[:, :, bass.ts(b, S)], xnT2[:]).then_inc(t_p.sem, 1)
            pool.wait_ge(*t_d(b, 13))
            pool.sem_inc(apart.sem, 1)
            pool.tensor_copy(gates_all[:, b, :], gate[:]).then_inc(t_p.sem, 1)

        def body(b, par, prev, nxt):
            static = isinstance(b, int)
            if nxt:
                front(b + 1, 1 - par, static and b == 0)
            if nxt:
                mask_q(b + 1, 1 - par, static and b == 0)
            if prev:
                tail_2(b - 1)
                tail_3(b - 1)

        pool.memset(ident[:], 0.0).then_inc(made.sem, 1)
        pool.memset(hmask[:], 1.0).then_inc(made.sem, 1)
        pool.memset(ones[:], 1.0).then_inc(made.sem, 1)
        pool.memset(mhalf[:], -0.5).then_inc(made.sem, 1)
        pool.wait_ge(made.sem, 4)
        pool.affine_select(out=ident[:], in_=ident[:], compare_op=ALU.not_equal, fill=1.0, base=0,
                           pattern=[[-1, P]], channel_multiplier=1).then_inc(made.sem, 1)
        pool.affine_select(out=hmask[:], in_=hmask[:], compare_op=ALU.is_ge, fill=0.0, base=0,
                           pattern=[[-DK, HC]], channel_multiplier=1).then_inc(made.sem, 1)
        pool.wait_ge(made.sem, 6)
        pool.affine_select(out=hmask[:], in_=hmask[:], compare_op=ALU.is_ge, fill=0.0, base=DK - 1,
                           pattern=[[DK, HC]], channel_multiplier=-1).then_inc(made.sem, 1)
        for par in range(2):
            m = pool.memset(v[par][:], 0.0)
        m.then_inc(made.sem, 1)
        pool.wait_ge(su_d.sem, 2)
        pool.sem_inc(apart.sem, 1)
        pool.tensor_scalar(cn[:, 1:2], cn[:, 0:1], NORM_EPS ** 2, None, ALU.max).then_inc(su_p.sem, 1)
        pool.wait_ge(su_p.sem, 1)
        pool.tensor_tensor(cn[:, 2:3], cn[:, 1:2], mhalf[:E0, :], ALU.pow).then_inc(su_p.sem, 1)
        pool.wait_ge(su_d.sem, 4)
        pool.wait_ge(made.sem, 8)
        front(0, 0, True)
        mask_q(0, 0, True)
        bodies(pool, body)
        last = B - 1
        tail_2(last)
        tail_3(last)



def phase_2(nc, ctx, a, t):
    def sb(name, shape, dt=F32):
        return ctx.enter_context(nc.sbuf_tensor(name, shape, dt))

    def sem(name, per=1):
        return Sig(ctx.enter_context(nc.semaphore(name)), per)

    x_all, xnT_all, gates_all, w1, b1, w2 = (t[k] for k in ("x_all", "xnT_all", "gates", "w1", "b1", "w2"))
    hid = sb("hid", [P, 2, GN])
    ph = ctx.enter_context(nc.psum_tensor("ph", [P, 2, 512], F32))
    py = ctx.enter_context(nc.psum_tensor("py", [P, 2, GB, D], F32))
    hidden = sem("hidden", E0)
    gelud = sem("gelud", E0)
    expert = sem("expert", E0)
    added = sem("added", E0 * GB)
    st, mv, mhalf = sb("p2_st", [S, GB, 6]), sb("p2_mv", [S, GB, 2]), sb("mhalf2", [S, 1])
    tmp = sb("tmp2", [S, 4, GB])
    stat = sem("stat", 2 * GB)
    root = sem("root", 7)
    apart, halved = sem("apart2"), sem("halved")
    wq, wk, wv, wih, whh, bih, bhh, slot_w, in_w, in_row = (t[k] for k in SLOT_WEIGHTS)
    wqk, wg, wh = t["wqk"], t["wg"], t["wh"]
    fact = sb("fact", [P, DC, D])
    pw = ctx.enter_context(nc.psum_tensor("pw", [P, DC * D], F32))
    rows = sb("rows", [KP, 2, KT, D])
    sqr = sb("sqr", [KP, D])
    rsq, rms = sb("rsq", [KP, GB * KT]), sb("rms", [KP, GB * KT])
    half_k = sb("half_k", [KP, 1])
    folded = sem("folded")
    su = sem("su2")
    rows_in = [sem("rows_in0"), sem("rows_in1")]
    squared = sem("squared", GB * KT)
    rooted = sem("rooted", 3)
    block = ctx.enter_context(nc.Block())

    def groups(eng, body):
        body(0, True)
        with eng.Fori(1, NG) as g:
            body(g, False)

    @block.sync
    def _(sp):
        def load(b, par):
            sp.dma_start(rows[:, par], a["ctx"][b].rearrange("(t p) d -> p t d", p=KP)).then_inc(rows_in[par].sem, 16)

        load(0, 0)
        load(1, 1)
        with sp.Fori(1, B // 2) as j:
            for par in range(2):
                sp.wait_ge(squared.sem, (2 * j + par - 1) * KT)
                sp.sem_inc(apart.sem, 1)
                load(2 * j + par, par)

    @block.tensor
    def _(pe):
        def second(g, e, first):
            pe.wait_ge(*gelud(g, e + 1))
            if first and e < 2:
                pe.wait_ge(su.sem, 2 * e + 2)
            if not first:
                pe.wait_ge(*added(g, (e - 1) * GB))
            for i in range(GB):
                m = pe.matmul(py[:S, e % 2, i, :], hid[:, e % 2, i * S:(i + 1) * S], w2[:, e % E0, :],
                              start=True, stop=True)
            m.then_inc(expert.sem, 1)

        def body(g, first):
            for e in range(E0):
                if not (first and e < 2):
                    pe.wait_ge(*gelud(g, e - 1))
                for c in range(DC):
                    m = pe.matmul(ph[:, e % 2, 0:GN], w1[:, c, e * F0:(e + 1) * F0], xnT_all[:, c, bass.ts(g, GN)],
                                  start=(c == 0), stop=(c == DC - 1))
                m.then_inc(hidden.sem, 1)
                if not (first and e < 1):
                    second(g, e - 1, first and e < 3)
        pe.wait_ge(t["slot_w_in"].sem, 160)
        for c in range(DC):
            for lo in (0, 512):
                for o in range(DC):
                    m = pe.matmul(py[:, c].rearrange("p i d -> p (i d)")[:, lo:min(lo + 512, 3 * D)], wv[:, o, c * P:(c + 1) * P],
                                  wih[:, o, lo:min(lo + 512, 3 * D)], start=(o == 0), stop=(o == DC - 1))
            m.then_inc(folded.sem, 1)
        for c in range(DC):
            for o in range(DC):
                m = pe.matmul(pw[:, c * D:(c + 1) * D], wq[:, o, c * P:(c + 1) * P], wk[:, o, :], start=(o == 0), stop=(o == DC - 1))
        m.then_inc(folded.sem, 1)
        groups(pe, body)
        second(NG - 1, E0 - 1, False)

    @block.scalar
    def _(act):
        def body(g, first):
            for e in range(E0):
                act.wait_ge(*hidden(g, e + 1))
                if not (first and e < 2):
                    act.wait_ge(*expert(g, e - 1))
                act.activation(hid[:, e % 2, :], ph[:, e % 2, 0:GN], ACT.Gelu, bias=b1[:, e:e + 1]).then_inc(gelud.sem, 1)
                for j in (2 * e, 2 * e + 1):
                    if j < GB * KT:
                        square(g, j, first)

        def square(g, j, first):
            i, kt = j // KT, j % KT
            if kt == 0:
                act.wait_ge(rows_in[i % 2].sem, 16 * (2 * g + i // 2 + 1))
            if j == 0 and not first:
                act.wait_ge(*rooted(g - 1, 1))
            if not (first and j == 0):
                act.wait_ge(*squared(g, j))
            act.activation(sqr[:], rows[:, i % 2, kt, :], ACT.Square, accum_out=rsq[:, j:j + 1]).then_inc(squared.sem, 1)

        groups(act, body)

    @block.vector
    def _(dve):
        def body(g, first):
            for e in range(E0):
                dve.wait_ge(*expert(g, e + 1))
                for i in range(GB):
                    if e:
                        dve.wait_ge(*added(g, (e - 1) * GB + i + 1))
                    x = x_all[:, g * GB + i, :]
                    dve.scalar_tensor_tensor(out=x, in0=py[:S, e % 2, i, :], scalar=gates_all[:, g * GB + i, e:e + 1],
                                             in1=x, op0=ALU.mult, op1=ALU.add).then_inc(added.sem, 1)
            for i in range(GB):
                dve.wait_ge(*added(g, (E0 - 1) * GB + i + 1))
                dve.sem_inc(apart.sem, 1)
                dve.bn_stats(st[:, i, :], x_all[:, g * GB + i, :]).then_inc(stat.sem, 1)
            if not first:
                dve.wait_ge(*root(g - 1, 7))
            for i in range(GB):
                dve.wait_ge(*stat(g, i + 1))
                dve.sem_inc(apart.sem, 1)
                dve.bn_aggr(mv[:, i, :], st[:, i, :]).then_inc(stat.sem, 1)
        hi, lo = wg
        for c in range(DC):
            full = py[:, c].rearrange("p i d -> p (i d)")
            dve.wait_ge(folded.sem, c + 1)
            for at in (slice(0, 512), slice(512, 3 * D)):
                m = dve.tensor_scalar(hi[:, c, at], full[:, at], in_w[:, c:c + 1], None, ALU.mult)
            m.then_inc(su.sem, 1)
            dve.wait_ge(su.sem, 2 * c + 1)
            for at in (slice(0, 512), slice(512, 3 * D)):
                m = dve.scalar_tensor_tensor(out=lo[:, c, at], in0=full[:, at], scalar=in_w[:, c:c + 1],
                                             in1=hi[:, c, at].bitcast(F32), op0=ALU.mult, op1=ALU.subtract)
            m.then_inc(su.sem, 1)
        for c in range(DC):
            m = dve.tensor_scalar(fact[:, c, :], in_row[:], slot_w[:, c:c + 1], D ** -0.5, ALU.mult, ALU.mult)
        m.then_inc(su.sem, 1)
        dve.tensor_copy(wh[0][:], whh[:])
        dve.tensor_tensor(t["brz"][:], bih[:, 0:4], bhh[:, 0:4], ALU.add).then_inc(su.sem, 1)
        dve.wait_ge(su.sem, 6)
        dve.tensor_scalar(t["brz"][:], t["brz"][:], 0.5, None, ALU.mult)
        dve.wait_ge(folded.sem, 3)
        dve.tensor_tensor(wqk[:, :, :].rearrange("p c d -> p (c d)"), pw[:, :], fact[:, :, :].rearrange("p c d -> p (c d)"), ALU.mult)
        dve.tensor_tensor(wh[1][:], whh[:], wh[0][:].bitcast(F32), ALU.subtract)
        groups(dve, body)

    @block.gpsimd
    def _(pool):
        def body(g, first):
            at = bass.ds(g * GB * KT, GB * KT)
            pool.wait_ge(*squared(g, GB * KT))
            pool.sem_inc(apart.sem, 1)
            pool.tensor_scalar(rms[:], rsq[:], 1.0 / D, RMS_EPS, ALU.mult, ALU.add).then_inc(rooted.sem, 1)
            pool.wait_ge(*rooted(g, 1))
            pool.sem_inc(apart.sem, 1)
            pool.tensor_tensor(t["row_root"][:, at], rms[:], half_k[:, 0:1].to_broadcast([KP, GB * KT]), ALU.pow).then_inc(rooted.sem, 1)
            pool.wait_ge(*rooted(g, 2))
            pool.sem_inc(apart.sem, 1)
            pool.tensor_tensor(t["row_rms"][:, at], rms[:], t["row_root"][:, at], ALU.mult).then_inc(rooted.sem, 1)
            pool.wait_ge(*stat(g, 2 * GB))
            norm_roots(pool, root, lambda k: root(g, k), apart, mv, mhalf[:, 0:1].to_broadcast([S, GB]), tmp,
                       t["mean"], t["roots"], bass.ds(g * GB, GB))

        pool.memset(half_k[:], -0.5)
        pool.memset(mhalf[:], -0.5).then_inc(halved.sem, 1)
        pool.wait_ge(halved.sem, 1)
        groups(pool, body)



SLOT_WEIGHTS = {"xwq": [P, DC, D], "xwk": [P, DC, D], "xwv": [P, DC, D], "wihT": [P, DC, 3 * D], "whhT": [P, DC, 3 * D],
                "bih": [P, 6], "bhh": [P, 6], "slot_w": [P, DC], "in_w": [P, DC], "in_w_row": [P, D]}


def slot_weight_loads(sp, a, t):
    for name, shape in SLOT_WEIGHTS.items():
        src = a[name]
        if name == "in_w_row":
            src = src.to_broadcast(shape)
        elif len(shape) == 3:
            src = src.rearrange("(c p) n -> p c n", p=P)
        sp.dma_start(t[name][:], src).then_inc(t["slot_w_in"].sem, 16)


def context_loads(sp, a, b, cx, cT, i, c_in):
    for kt in range(KT):
        sp.dma_start(cx[:, i, kt, 0:D], a["ctx"][b, kt * KP:(kt + 1) * KP, :]).then_inc(c_in.sem, 16)
    sp.dma_start(cT[:, i], a["ctxT"][b].rearrange("(c p) m -> p c m", p=P)).then_inc(c_in.sem, 16)


def phase_3(nc, ctx, a, t):
    def sb(name, shape, dt=F32):
        return ctx.enter_context(nc.sbuf_tensor(name, shape, dt))

    def psum(name, shape):
        return ctx.enter_context(nc.psum_tensor(name, shape, F32))

    sigs = {}

    def sem(name, per, owner):
        s = Sig(ctx.enter_context(nc.semaphore("r_" + name)), per)
        sigs.setdefault(owner, []).append(s)
        return s

    def at(s, K, k):
        return s.sem, (K + 1) * s.per + k

    def prime(eng, owner):
        for s in sigs[owner]:
            eng.sem_inc(s.sem, s.per)

    x_all, ident = t["x_all"], t["ident"]
    UNITS = 2 * ROUNDS
    G3 = 3 * D

    wq, wk, wv, wih, whh, bih, bhh, slot_w, in_w, in_row = (t[k] for k in SLOT_WEIGHTS)
    wqk, brz, wg, wh, row_root, row_rms = (t[k] for k in ("wqk", "brz", "wg", "wh", "row_root", "row_rms"))
    ones = sb("ones3", [P, 1])
    mhalf = sb("mhalf3", [P, 1])
    cx = [t["cx0"], sb("cx1", [KP, GB, KT, D + 1])]
    cT = [t["cT0"], sb("cT1", [P, GB, DC, KEYS])]
    hT = [sb(f"hT{g}", [P, DC, GN]) for g in range(2)]
    hs = [[sb(f"h_{part}{g}", [P, DC, GN], F32R) for part in ("hi", "lo")] for g in range(2)]
    us = [[sb(f"u_{part}{g}", [P, DC, GN], F32R) for part in ("hi", "lo")] for g in range(2)]
    kr = [sb(f"kr{g}", [KP, GB * KT]) for g in range(2)]
    mean, roots = t["mean"], t["roots"]
    sl = sb("sl", [S, 2, D])
    st, mv, tmp = sb("st3", [S, GB, 6]), sb("mv3", [S, GB, 2]), sb("tmp3", [S, 4, GB])
    zeros = sb("zeros", [P, D])
    hsq = sb("hsq", [P, DC, GN])
    ms, rinv = sb("ms", [S, GB]), sb("rinv", [S, GB])
    qs, qT = sb("qs", [S, 2, D]), sb("qT3", [P, 2, DC, S])
    nm, nb = sb("nm3", [KP, GB, KT]), sb("nb3", [KP, GB, KT])
    e = sb("e3", [KP, GB, KT, S])
    es, er = sb("es3", [KP, GB, KT]), sb("er3", [KP, GB, KT])
    uk, un = sb("uk", [S, 2, 2]), sb("un", [S, 2, D])
    tr, tz = sb("tr", [P, DC, GN]), sb("tz", [P, DC, GN])
    hh, nn = whh[:, :, 0:GN], wih[:, :, 0:GN]
    df = tr

    pa, pg, pc, pu = (psum(n, [P, 2, 512]) for n in ("pa", "pg", "pc", "pu"))

    made = Sig(ctx.enter_context(nc.semaphore("x_made")))
    blank = Sig(ctx.enter_context(nc.semaphore("x_blank")))
    apart = Sig(ctx.enter_context(nc.semaphore("x_apart")))
    c_in = [t["c_in0"], sem("c_in1", 16 * (KT + 1) * GB, "sp")]
    sigs["sp"].append(c_in[0])
    U4 = UNITS * GB
    pe_i = sem("pe_i", 2 * GB, "pe")
    pe_ss = sem("pe_ss", UNITS - 2, "pe")
    pe_q = sem("pe_q", U4, "pe")
    pe_t = sem("pe_t", U4, "pe")
    pe_s = sem("pe_s", U4, "pe")
    pe_u = sem("pe_u", U4, "pe")
    pe_x = sem("pe_x", U4, "pe")
    pe_g = sem("pe_g", UNITS * 8, "pe")
    pe_f = sem("pe_f", 2 * GB, "pe")
    a_i = sem("a_i", 2 * GB, "act")
    a_q = sem("a_q", U4, "act")
    a_e = sem("a_e", U4, "act")
    a_g = sem("a_g", UNITS * 6, "act")
    a_h = sem("a_h", (UNITS - 2) * 2, "act")
    a_hi = sem("a_hi", UNITS * DC, "act")
    d_n = sem("d_n", 2 * GB, "dve")
    d_ss = sem("d_ss", UNITS - 2, "dve")
    d_t = sem("d_t3", U4, "dve")
    d_m = sem("d_m3", 2 * U4, "dve")
    d_e = sem("d_e", 3 * U4, "dve")
    d_u = sem("d_u", 3 * U4, "dve")
    d_xh, d_x = sem("d_xh", U4, "dve"), sem("d_x", U4, "dve")
    d_g = sem("d_g", UNITS * 8, "dve")
    d_h = sem("d_h", UNITS * 2, "dve")
    d_f = sem("d_f3", 2 * GB, "dve")
    d_l = sem("d_l", 2 * (2 * GB), "dve")
    p_l = sem("p_l", 2 * 7, "pool")
    p_lo = sem("p_lo", UNITS * DC, "pool")
    p_k = sem("p_k", 2, "pool")
    p_r = sem("p_r", UNITS - 2, "pool")
    p_d = sem("p_d", UNITS * 2, "pool")

    ATT = [("SS", 0), ("q", 0), ("q", 1), "g", ("T", 0), ("T", 1), ("R", 0), ("q", 2), ("q", 3), "g", ("T", 2), ("S", 0),
           ("R", 1), ("T", 3), ("S", 1), "g", ("S", 2), ("N", 0), "g", ("S", 3), ("N", 1), ("U", 0), "g", ("N", 2), ("U", 1),
           ("X", 0), "g", ("N", 3), ("U", 2), ("X", 1), ("H", 0), ("U", 3), ("X", 2), ("H", 1), ("h", 0), ("X", 3), ("h", 1)]
    LAST = ["g", ("R", 0), "g", ("R", 1), "g", "g", "g", "g", ("H", 0), ("H", 1)]
    STEP = [("hn", 0), ("hn", 1), ("r", 0), ("r", 1), ("xn", 0), ("z", 0), ("xn", 1), ("z", 1)]
    AT_A = {("r", 0): 1, ("r", 1): 2, ("xn", 0): 3, ("z", 0): 4, ("xn", 1): 5, ("z", 1): 6}

    ONCE = {("S", 1): [("slots", 1, 1)]}

    def schedule():
        out = [("rms", 0, 0), ("slots", 0, 0), ("rms", 1, 1)]
        for n in range(UNITS + 1):
            gru = list(range(2, len(STEP)))
            for s in (ATT if n < UNITS else LAST):
                if s == "g":
                    if n:
                        out.append(("g", gru.pop(0), n - 1))
                elif s[0] in ("H", "R"):
                    if n:
                        out.append((*s, n - 1))
                elif s[0] == "SS":
                    if n >= 2:
                        out.append((*s, n))
                elif s[0] == "h":
                    out.append(("g", s[1], n))
                else:
                    out.append((*s, n))
                if n == 0:
                    out += ONCE.get(s, [])
            if n >= UNITS - 1:
                out.append(("fin", (n - 1) % 2, n - 1))
        return out
    SCHEDULE = schedule()

    def iterations(eng, owner, do):
        prime(eng, owner)
        with eng.Fori(0, NG // 2) as K:
            for what, i, n in SCHEDULE:
                do(what, i, n, K)

    block = ctx.enter_context(nc.Block())

    @block.sync
    def _(sp):
        prime(sp, "sp")

        def load(K, g):
            for i in range(GB):
                context_loads(sp, a, (2 * K + g) * GB + i, cx[g], cT[g], i, c_in[g])

        load(0, 1)
        for e in range(E1):
            sp.dma_start(t["down"][:, e], a["down"][e].rearrange("(c p) n -> p c n", p=P)).then_inc(t["down_in"].sem, 16)
        sp.wait_ge(blank.sem, 1)
        sp.dma_start(t["rows_by_place"].rearrange("(t p) d -> p t d", p=P),
                     zeros[:, :].unsqueeze(1).to_broadcast([P, MT, D])).then_inc(t["zeroed"].sem, 16)
        with sp.Fori(1, NG // 2) as K:
            for g in range(2):
                sp.wait_ge(*at(pe_u, K, -(1 - g) * GB))
                sp.sem_inc(apart.sem, 1)
                load(K, g)

    @block.tensor
    def _(pe):
        def do(what, i, n, K):
            g, r = n % 2, n // 2
            k = n * GB + i + 1
            if what == "slots":
                for j in range(GB):
                    b = g * GB + j
                    pe.wait_ge(*at(d_n, K, b + 1))
                    if b >= 2:
                        pe.wait_ge(*at(a_i, K, b - 1))
                    else:
                        pe.wait_ge(*at(d_f, K, 0))
                    for c in range(DC):
                        m = pe.transpose(pu[:, b % 2, c * S:(c + 1) * S], sl[:, b % 2, c * P:(c + 1) * P], ident[:S, :S])
                    m.then_inc(pe_i.sem, 1)
            elif what == "SS":
                pe.wait_ge(*at(a_h, K, 2 * n - 2))
                pe.wait_ge(*at(d_t, K, n * GB))
                for j in range(GB):
                    for c in range(DC):
                        m = pe.matmul(pa[:S, 0, j:j + 1], hsq[:, c, j * S:(j + 1) * S], ones[:, 0:1],
                                      start=(c == 0), stop=(c == DC - 1))
                m.then_inc(pe_ss.sem, 1)
            elif what == "q":
                if i == 0:
                    if r:
                        pe.wait_ge(*at(d_ss, K, n - 1))
                    pe.wait_ge(*at(d_t, K, n * GB - 1))
                    if r == 0:
                        pe.wait_ge(*at(a_i, K, (g + 1) * GB))
                    else:
                        pe.wait_ge(*at(d_h, K, 2 * (n - 1)))
                elif i == 1:
                    pe.wait_ge(*at(d_t, K, n * GB))
                else:
                    pe.wait_ge(*at(d_t, K, k - 2))
                for c in range(DC):
                    m = pe.matmul(pa[:S, i % 2, 0:D], hT[g][:, c, i * S:(i + 1) * S], wqk[:, c, :],
                                  start=(c == 0), stop=(c == DC - 1))
                m.then_inc(pe_q.sem, 1)
            elif what == "T":
                pe.wait_ge(*at(a_q, K, k))
                for c in range(DC):
                    m = pe.transpose(pa[:, i % 2, D + c * S:D + (c + 1) * S], qs[:, i % 2, c * P:(c + 1) * P], ident[:S, :S])
                m.then_inc(pe_t.sem, 1)
            elif what == "S":
                if i == 0 and r == 0:
                    pe.wait_ge(*at(c_in[g], K, c_in[g].per))
                pe.wait_ge(*at(d_t, K, k))
                pe.wait_ge(*at(a_e, K, k - 2))
                for kt in range(KT):
                    for c in range(DC):
                        m = pe.matmul(pc[:KP, i % 2, kt * S:(kt + 1) * S], cT[g][:, i, c, kt * KP:(kt + 1) * KP],
                                      qT[:, i % 2, c, :], start=(c == 0), stop=(c == DC - 1))
                m.then_inc(pe_s.sem, 1)
            elif what == "U":
                pe.wait_ge(*at(d_e, K, 3 * k))
                if i == 0 and r == 0:
                    pe.wait_ge(*at(p_k, K, g + 1))
                if n == 0 and i == 0:
                    pe.wait_ge(*at(a_i, K, 2 * GB))
                pe.wait_ge(*at(d_x, K, k - 2))
                for kt in range(KT):
                    m = pe.matmul(pu[:S, i % 2, 0:D + 1], e[:, i, kt, :], cx[g][:, i, kt, :],
                                  start=(kt == 0), stop=(kt == KT - 1))
                m.then_inc(pe_u.sem, 1)
            elif what == "X":
                pe.wait_ge(*at(d_u, K, 3 * k))
                for c in range(DC):
                    m = pe.transpose(pu[:, i % 2, c * S:(c + 1) * S],
                                     un[:, i % 2, c * P:(c + 1) * P], ident[:S, :S])
                m.then_inc(pe_x.sem, 1)
            elif what == "g":
                kind, c = STEP[i]
                out = pg[:, i % 2, 0:GN]
                if i == 0:
                    pe.wait_ge(*at(d_g, K, 8 * n - 2))
                elif i == 1:
                    pe.wait_ge(*at(a_g, K, 6 * n))
                elif i == 2:
                    pe.wait_ge(*at(d_g, K, 8 * n + 1))
                    pe.wait_ge(*at(d_x, K, (n + 1) * GB))
                elif i == 3:
                    pe.wait_ge(*at(d_g, K, 8 * n + 2))
                elif i == 4:
                    pe.wait_ge(*at(a_g, K, 6 * n + 1))
                elif i == 5:
                    pe.wait_ge(*at(a_g, K, 6 * n + 2))
                elif i == 6:
                    pe.wait_ge(*at(d_g, K, 8 * n + 5))
                else:
                    pe.wait_ge(*at(a_g, K, 6 * n + 4))
                col = {"r": 0, "z": D, "hn": 2 * D, "xn": 2 * D}[kind] + c * P
                if i == 0:
                    pe.wait_ge(*at(p_lo, K, DC * (n + 1)))
                sums = ([(wg, us[g])] if kind != "hn" else []) + ([(wh, hs[g])] if kind != "xn" else [])
                terms = [(w[x], s[y], q) for w, s in sums for q in range(DC) for x, y in ((0, 0), (0, 1), (1, 0))]
                for j, (w, s, q) in enumerate(terms):
                    m = pe.matmul(out, w[:, q, col:col + P], s[:, q, :], start=(j == 0), stop=(j == len(terms) - 1))
                m.then_inc(pe_g.sem, 1)
            elif what == "fin":
                for j in range(GB):
                    b = g * GB + j
                    pe.wait_ge(*at(d_h, K, 2 * (n + 1)))
                    if b < 2:
                        pe.wait_ge(*at(a_e, K, U4))
                    else:
                        pe.wait_ge(*at(d_f, K, b - 1))
                    if g == 0 and j < 2:
                        pe.wait_ge(*at(d_u, K, 3 * U4))
                        pe.wait_ge(*at(d_x, K, U4))
                    for c in range(DC):
                        m = pe.transpose(pu[:S, b % 2, c * P:(c + 1) * P], hT[g][:, c, j * S:(j + 1) * S], ident[:, :])
                    m.then_inc(pe_f.sem, 1)

        pe.wait_ge(made.sem, 1)
        iterations(pe, "pe", do)

    @block.scalar
    def _(act):
        def do(what, i, n, K):
            g, r = n % 2, n // 2
            k = n * GB + i + 1
            if what == "slots":
                for j in range(GB):
                    act.wait_ge(*at(pe_i, K, g * GB + j + 1))
                    act.wait_ge(*at(pe_f, K, 0))
                    act.activation(hT[g][:, :, j * S:(j + 1) * S],
                                   pu[:, j % 2, 0:DC * S].rearrange("p (c s) -> p c s", c=DC), ACT.Copy).then_inc(a_i.sem, 1)
                act.wait_ge(*at(a_i, K, (g + 1) * GB))
                for c in range(DC):
                    high(g, c, K)
            elif what == "q":
                act.wait_ge(*at(pe_q, K, k))
                if r:
                    act.wait_ge(*at(p_r, K, n - 1))
                    scale = rinv[:, i:i + 1]
                else:
                    scale = roots[:, 1, bass.ds((2 * K + g) * GB + i, 1)]
                act.wait_ge(*at(pe_t, K, k - 2))
                act.activation(qs[:, i % 2, :], pa[:S, i % 2, 0:D], ACT.Copy, scale=scale).then_inc(a_q.sem, 1)
            elif what == "S":
                act.wait_ge(*at(d_m, K, 2 * k))
                act.wait_ge(*at(pe_u, K, k - GB))
                for kt in range(KT):
                    m = act.activation(e[:, i, kt, :], pc[:KP, i % 2, kt * S:(kt + 1) * S], ACT.Exp,
                                       scale=kr[g][:, i * KT + kt:i * KT + kt + 1], bias=nb[:, i, kt:kt + 1],
                                       accum_out=es[:, i, kt:kt + 1])
                m.then_inc(a_e.sem, 1)
            elif what == "g" and STEP[i] in AT_A:
                kind, c = STEP[i]
                ps = pg[:, i % 2, 0:GN]
                if kind == "xn":
                    act.wait_ge(*at(d_g, K, 8 * n + 5 + c))
                    act.wait_ge(*at(d_h, K, 2 * n))
                    act.activation(nn[:, c, :], hh[:, c, :], ACT.Tanh, bias=bih[:, 4 + c:5 + c]).then_inc(a_g.sem, 1)
                else:
                    act.wait_ge(*at(pe_g, K, 8 * n + i + 1))
                    dst, col = (tr, c) if kind == "r" else (tz, 2 + c)
                    act.wait_ge(*at(d_h, K, 2 * n))
                    act.activation(dst[:, c, :], ps, ACT.Tanh, scale=0.5, bias=brz[:, col:col + 1]).then_inc(a_g.sem, 1)
            elif what == "H" and n + 2 < UNITS:
                act.wait_ge(*at(d_h, K, 2 * n + i + 1))
                square(n + 2, i, K)
                high(n + 2, i, K)

        def high(n, c, K):
            act.wait_ge(*at(pe_g, K, 8 * (n - 1)))
            act.activation(hs[n % 2][0][:, c, :], hT[n % 2][:, c, :], ACT.Copy).then_inc(a_hi.sem, 1)

        def square(n, c, K):
            act.wait_ge(*at(pe_ss, K, n - 2))
            act.activation(hsq[:, c, :], hT[n % 2][:, c, :], ACT.Square).then_inc(a_h.sem, 1)

        iterations(act, "act", do)

    @block.vector
    def _(dve):
        def do(what, i, n, K):
            g, r = n % 2, n // 2
            k = n * GB + i + 1
            if what == "slots":
                for j in range(GB):
                    b, xb = g * GB + j, (2 * K + g) * GB + j
                    dve.wait_ge(*at(pe_i, K, b - 1))
                    dve.tensor_scalar(sl[:, b % 2, :], x_all[:, xb, :], mean[:, bass.ds(xb, 1)], roots[:, 0, bass.ds(xb, 1)],
                                      ALU.subtract, ALU.mult).then_inc(d_n.sem, 1)
            elif what == "SS":
                dve.wait_ge(*at(pe_ss, K, n - 1))
                dve.wait_ge(*at(p_r, K, n - 2))
                dve.tensor_scalar(ms[:], pa[:S, 0, 0:GB], 1.0 / D, RMS_EPS, ALU.mult, ALU.add).then_inc(d_ss.sem, 1)
            elif what == "T":
                dve.wait_ge(*at(pe_t, K, k))
                dve.wait_ge(*at(pe_s, K, k - 2))
                dve.tensor_copy(qT[:, i % 2].rearrange("p c s -> p (c s)"), pa[:, i % 2, D:D + DC * S]).then_inc(d_t.sem, 1)
            elif what == "S":
                dve.wait_ge(*at(pe_s, K, k))
                if i == 0 and r == 0:
                    dve.wait_ge(*at(p_k, K, g + 1))
                dve.wait_ge(*at(a_e, K, k - GB))
                dve.tensor_reduce(nm[:, i, :], pc[:KP, i % 2, 0:KT * S].rearrange("p (t s) -> p t s", t=KT),
                                  AX.X, ALU.max, negate=True).then_inc(d_m.sem, 1)
                dve.wait_ge(*at(d_m, K, 2 * k - 1))
                dve.tensor_tensor(nb[:, i, :], nm[:, i, :], kr[g][:, i * KT:(i + 1) * KT], ALU.mult).then_inc(d_m.sem, 1)
            elif what == "N":
                dve.wait_ge(*at(a_e, K, k))
                dve.reciprocal(er[:, i, :], es[:, i, :]).then_inc(d_e.sem, 1)
                dve.wait_ge(*at(d_e, K, 3 * k - 2))
                dve.tensor_tensor(er[:, i, :], er[:, i, :], kr[g][:, i * KT:(i + 1) * KT], ALU.mult).then_inc(d_e.sem, 1)
                dve.wait_ge(*at(d_e, K, 3 * k - 1))
                dve.tensor_tensor(e[:, i], e[:, i], er[:, i, :].unsqueeze(2).to_broadcast([KP, KT, S]),
                                  ALU.mult).then_inc(d_e.sem, 1)
            elif what == "U":
                dve.wait_ge(*at(pe_u, K, k))
                dve.tensor_scalar(uk[:, i % 2, 0:1], pu[:S, i % 2, D:D + 1], SLOT_EPS, None, ALU.add).then_inc(d_u.sem, 1)
                dve.wait_ge(*at(d_u, K, 3 * k - 2))
                dve.reciprocal(uk[:, i % 2, 1:2], uk[:, i % 2, 0:1]).then_inc(d_u.sem, 1)
                dve.wait_ge(*at(d_u, K, 3 * k - 1))
                dve.wait_ge(*at(pe_x, K, k - 2))
                dve.tensor_scalar(un[:, i % 2, :], pu[:S, i % 2, 0:D], uk[:, i % 2, 1:2], None, ALU.mult).then_inc(d_u.sem, 1)
            elif what == "X":
                dve.wait_ge(*at(pe_x, K, k))
                if i == 0:
                    dve.wait_ge(*at(pe_g, K, 8 * (n - 1)))
                full = pu[:, i % 2, 0:DC * S].rearrange("p (c s) -> p c s", c=DC)
                hi, lo = (part[:, :, i * S:(i + 1) * S] for part in us[g])
                dve.tensor_copy(hi, full).then_inc(d_xh.sem, 1)
                dve.wait_ge(*at(d_xh, K, k))
                dve.tensor_tensor(lo, full, hi.bitcast(F32), ALU.subtract).then_inc(d_x.sem, 1)
            elif what == "g":
                kind, c = STEP[i]
                ps = pg[:, i % 2, 0:GN]
                if kind == "hn":
                    dve.wait_ge(*at(pe_g, K, 8 * n + i + 1))
                    dve.tensor_scalar(hh[:, c, :], ps, bhh[:, 4 + c:5 + c], 0.5, ALU.add, ALU.mult).then_inc(d_g.sem, 1)
                elif kind == "xn":
                    dve.wait_ge(*at(pe_g, K, 8 * n + i + 1))
                    dve.wait_ge(*at(d_g, K, 8 * n + 3 + c))
                    dve.wait_ge(*at(a_g, K, 6 * n))
                    dve.tensor_tensor(hh[:, c, :], ps, hh[:, c, :], ALU.add).then_inc(d_g.sem, 1)
            elif what == "R":
                dve.wait_ge(*at(d_g, K, 8 * n + i + 1))
                dve.wait_ge(*at(a_g, K, 6 * n + 1 + i))
                dve.scalar_tensor_tensor(out=hh[:, i, :], in0=tr[:, i, :], scalar=1.0, in1=hh[:, i, :],
                                         op0=ALU.add, op1=ALU.mult).then_inc(d_g.sem, 1)
            elif what == "H":
                state(n, i, K, hT[g])
            elif what == "fin":
                for j in range(GB):
                    x = x_all[:, (2 * K + g) * GB + j, :]
                    dve.wait_ge(*at(pe_f, K, g * GB + j + 1))
                    dve.tensor_tensor(x, pu[:S, j % 2, 0:D], x, ALU.add).then_inc(d_f.sem, 1)
                for j in range(GB):
                    dve.wait_ge(*at(d_f, K, g * GB + j + 1))
                    dve.sem_inc(apart.sem, 1)
                    dve.bn_stats(st[:, j, :], x_all[:, (2 * K + g) * GB + j, :]).then_inc(d_l.sem, 1)
                dve.wait_ge(*at(p_l, K, 7 * g))
                for j in range(GB):
                    dve.wait_ge(*at(d_l, K, g * 2 * GB + j + 1))
                    dve.sem_inc(apart.sem, 1)
                    dve.bn_aggr(mv[:, j, :], st[:, j, :]).then_inc(d_l.sem, 1)

        def state(n, c, K, new):
            dve.wait_ge(*at(p_d, K, 2 * n + c + 1))
            dve.wait_ge(*at(a_g, K, 6 * n + 4 + 2 * c))
            dve.scalar_tensor_tensor(out=tz[:, c, :], in0=tz[:, c, :], scalar=1.0, in1=df[:, c, :],
                                     op0=ALU.add, op1=ALU.mult).then_inc(d_g.sem, 1)
            dve.wait_ge(*at(d_g, K, 8 * n + 7 + c))
            dve.wait_ge(*at(p_lo, K, DC * (n + 1)))
            dve.scalar_tensor_tensor(out=new[:, c, :], in0=tz[:, c, :], scalar=0.5, in1=nn[:, c, :],
                                     op0=ALU.mult, op1=ALU.add).then_inc(d_h.sem, 1)

        iterations(dve, "dve", do)

    @block.gpsimd
    def _(pool):
        def do(what, i, n, K):
            g, r = n % 2, n // 2
            old = hT[g]
            if what == "fin":
                pool.wait_ge(*at(d_l, K, (g + 1) * 2 * GB))
                norm_roots(pool, p_l, lambda k: at(p_l, K, 7 * g + k), apart, mv, mhalf[:S, 0:1].to_broadcast([S, GB]), tmp,
                           mean, roots, bass.ds((2 * K + g) * GB, GB))
            elif what == "slots":
                for c in range(DC):
                    low(g, c, K)
            elif what == "H" and n + 2 < UNITS:
                low(n + 2, i, K)
            elif what == "rms":
                pool.wait_ge(*at(pe_u, K, -(1 - g) * GB))
                at_g = bass.ds((2 * K + g) * GB * KT, GB * KT)
                pool.sem_inc(apart.sem, 1)
                pool.tensor_copy(kr[g][:], row_root[:, at_g])
                pool.tensor_copy(cx[g][:, :, :, D], row_rms[:, at_g]
                                 .rearrange("p (i t) -> p i t", i=GB)).then_inc(p_k.sem, 1)
            elif what == "SS":
                pool.wait_ge(*at(d_ss, K, n - 1))
                pool.wait_ge(*at(a_q, K, n * GB))
                pool.tensor_tensor(rinv[:], ms[:], mhalf[:S, 0:1].to_broadcast([S, GB]), ALU.pow).then_inc(p_r.sem, 1)
            elif what == "g" and i in (5, 7):
                c = (i - 5) // 2
                pool.wait_ge(*at(a_g, K, 6 * n + 3 + 2 * c))
                pool.wait_ge(*at(d_g, K, 8 * n - 1 + c))
                pool.tensor_tensor(df[:, c, :], old[:, c, :], nn[:, c, :], ALU.subtract).then_inc(p_d.sem, 1)

        def low(n, c, K):
            pool.wait_ge(*at(a_hi, K, DC * n + c + 1))
            hi, lo = hs[n % 2]
            pool.tensor_tensor(lo[:, c, :], hT[n % 2][:, c, :], hi[:, c, :].bitcast(F32), ALU.subtract).then_inc(p_lo.sem, 1)

        pool.memset(zeros[:], 0.0).then_inc(blank.sem, 1)
        pool.memset(mhalf[:], -0.5)
        pool.memset(ones[:], 1.0).then_inc(made.sem, 1)
        pool.wait_ge(made.sem, 1)
        iterations(pool, "pool", do)



def phase_4(nc, ctx, a, t, out):
    def sb(name, shape, dt=F32):
        return ctx.enter_context(nc.sbuf_tensor("e_" + name, shape, dt))

    def psum(name, shape):
        return ctx.enter_context(nc.psum_tensor("e_" + name, shape, F32))

    def sem(name, per=1):
        return Sig(ctx.enter_context(nc.semaphore("e_" + name)), per)

    x_all, ident = t["x_all"], t["ident"]
    HID2 = 2 * F1
    FC = F1 // P
    BE = B * E1

    up = sb("up", [P, E1, DC, HID2])
    down, mean, roots = t["down"], t["mean"], t["roots"]
    scale = sb("scale4", [S, D])
    cT1 = sb("cT1", [P, DC, E1])
    ny, csq = sb("ny", [S, E1]), sb("csq4", [P, DC, E1])
    onesf, onesb = sb("onesf", [P, S]), sb("onesb", [S, S], BF16)
    before = sb("before", [S, S], BF16)
    rank_e = sb("rank_e", [S, E1])
    less = sb("less", [S, E1, E1])
    kk = sb("kk", [S, E1, B * S // P])
    tj = sb("tj", [S, MT, E1])
    xl, xn = sb("xl", [S, 2, D]), sb("xn4", [S, 2, D])
    xn_all = sb("xn_all", [S, B, D])
    sq = sb("sq4", [S, D])
    nx = sb("nx", [S, B])
    xnT = sb("xnT4", [P, 2, DC, S])
    dots = sb("dots", [S, B, E1])
    dist, cand, oh = sb("dist", [S, B, E1]), sb("cand", [S, B, E1]), sb("oh", [S, B, E1])
    best = sb("best", [S, 2, B])
    ohb = sb("ohb", [S, B, E1], BF16)
    cum = sb("cum", [S, 2, B, E1])
    cnt = sb("cnt", [S, B, E1])
    rank = sb("rank4", [S, B, E1])
    more = sb("more", [S, E1, B * S // P])
    tiles, start, end = sb("tiles", [S, E1]), sb("start", [S, E1]), sb("end", [S, E1])
    lt = sb("lt", [S, E1, E1])
    passed = sb("passed", [S, MT, E1])
    texp = sb("texp", [S, MT])
    texp_i = sb("texp_i", [S, MT], I32)
    place, place_i = sb("place", [S, B]), sb("place_i", [S, B], U32)
    xt, xT = sb("xt", [P, 2, D]), sb("xT", [P, 2, DC, P])
    th, u = sb("th", [P, 2, F1]), sb("u", [P, 2, F1])
    uT, ysb = sb("uT4", [P, 2, FC, P]), sb("ysb", [P, 2, D])
    yg = sb("yg", [S, B, D])
    xs = t["rows_by_place"]
    ys = nc.dram_tensor("results_by_place", [MT * P, D], F32).ap()

    pt, pd = psum("pt4", [P, 512]), psum("pd4", [P, 512])
    ph = psum("ph4", [P, 2, 2, 512])
    pz, py = psum("pz4", [P, 512]), psum("py4", [P, 512])
    xbank = [pt, py]

    s_in, u_in = sem("s_in"), sem("u_in")
    made = sem("made")
    apart = sem("apart")
    chosen = sem("chosen")
    lnd, nrm = sem("lnd"), sem("nrm")
    kept, nxd, xnk = sem("kept"), sem("nxd"), sem("xnk")
    tpd, tup, dotd, dup = sem("tpd"), sem("tup"), sem("dotd"), sem("dup")
    v = sem("v")
    routed_pe = sem("routed_pe")
    scattered, stored = sem("scattered"), sem("stored")
    gathered = [sem(f"gathered{g}") for g in range(NG)]
    x_in = [sem("x_in0"), sem("x_in1")]
    y_out = [sem("y_out0"), sem("y_out1")]
    t_pe, t_up, up_a, up_g, thd, gated, z_pe, z_up, y_pe, y_up = (
        sem(n) for n in ("t_pe", "t_up", "up_a", "up_g", "thd", "gated", "z_pe", "z_up", "y_pe", "y_up"))
    added = sem("added")

    block = ctx.enter_context(nc.Block())

    def tiles_loop(eng, body):
        body(0, 0, True, False)
        body(1, 1, False, False)
        with eng.Fori(1, (MT - 1) // 2) as j:
            body(2 * j, 0, False, True)
            body(2 * j + 1, 1, False, True)
        body(MT - 1, 0, False, True)

    @block.sync
    def _(sp):
        sp.dma_start(scale[:], a["scale"].to_broadcast([S, D])).then_inc(s_in.sem, 16)
        sp.dma_start(cT1[:], a["centT"].rearrange("(c p) e -> p c e", p=P)).then_inc(s_in.sem, 16)
        for e in range(E1):
            sp.dma_start(up[:, e], a["up"][e].rearrange("(c p) n -> p c n", p=P)).then_inc(u_in.sem, 16)
        sp.wait_ge(scattered.sem, 16 * B)

        def load(j, par):
            sp.dma_start(xt[:, par, :], xs[bass.ts(j, P), :]).then_inc(x_in[par].sem, 16)

        load(0, 0)
        load(1, 1)

        def body(j, par, first, full):
            if not (isinstance(j, int) and j + 2 >= MT):
                sp.wait_ge(t_pe.sem, j + 1)
                sp.sem_inc(apart.sem, 1)
                load(j + 2, par)
            sp.wait_ge(y_up.sem, j + 1)
            sp.sem_inc(apart.sem, 1)
            sp.dma_start(ys[bass.ts(j, P), :], ysb[:, par, :]).then_inc(y_out[par].sem, 16)

        body(0, 0, True, False)
        body(1, 1, False, False)
        with sp.Fori(1, (MT - 1) // 2 - 1) as j:
            body(2 * j, 0, False, True)
            body(2 * j + 1, 1, False, True)
        body(MT - 3, 0, False, True)
        body(MT - 2, 1, False, True)
        body(MT - 1, 0, False, True)
        for b in range(B):
            sp.wait_ge(added.sem, b + 1)
            sp.dma_start(out[b], x_all[:, b, :]).then_inc(stored.sem, 16)
        sp.wait_ge(stored.sem, 16 * B)

    @block.tensor
    def _(pe):
        pe.wait_ge(v.sem, 1)
        pe.wait_ge(made.sem, 10)
        for c in range(DC):
            m = pe.matmul(pz[:S, 0:E1], onesf[:, :], csq[:, c, :], start=(c == 0), stop=(c == DC - 1))
        m.then_inc(routed_pe.sem, 1)

        def turn_x(b, par):
            pe.wait_ge(nrm.sem, b + 3)
            pe.wait_ge(tup.sem, b + 1)
            for c in range(DC):
                m = pe.transpose(xbank[par][:, c * S:(c + 1) * S], xn[:, par, c * P:(c + 1) * P], ident[:S, :S])
            m.then_inc(tpd.sem, 1)

        def dot(b, par):
            pe.wait_ge(tup.sem, b + 3)
            pe.wait_ge(dup.sem, b + 2)
            for c in range(DC):
                m = pe.matmul(pd[:S, 0:E1], xnT[:, par, c, :], cT1[:, c, :], start=(c == 0), stop=(c == DC - 1))
            m.then_inc(dotd.sem, 1)

        turn_x(0, 0)
        turn_x(1, 1)
        dot(0, 0)
        with pe.Fori(1, B // 2) as j:
            turn_x(2 * j, 0)
            dot(2 * j - 1, 1)
            turn_x(2 * j + 1, 1)
            dot(2 * j, 0)
        dot(B - 1, 1)
        pe.wait_ge(v.sem, 8)
        pe.wait_ge(dup.sem, B + 2)
        pe.matmul(pd[:S, 0:BE], before[:, :], ohb[:, :, :].rearrange("s b e -> s (b e)"), start=True, stop=True)
        pe.matmul(pz[:S, 0:BE], onesb[:, :], ohb[:, :, :].rearrange("s b e -> s (b e)"), start=True, stop=True).then_inc(routed_pe.sem, 1)

        def turn(j, par, first):
            pe.wait_ge(x_in[par].sem, 8 * (j - par) + 16)
            if not first:
                pe.wait_ge(t_up.sem, j)
            else:
                pe.wait_ge(dotd.sem, B)
            for c in range(DC):
                m = pe.transpose(pt[:, c * P:(c + 1) * P], xt[:, par, c * P:(c + 1) * P], ident[:, :])
            m.then_inc(t_pe.sem, 1)

        def half(j, par, h, e, sig):
            for c in range(DC):
                m = pe.matmul(ph[:, par, h, :], xT[:, par, c, :], up[:, e, c, h * F1:(h + 1) * F1],
                              start=(c == 0), stop=(c == DC - 1))
            m.then_inc(sig.sem, 1)

        def turn_u(j, par, first):
            pe.wait_ge(gated.sem, j + 1)
            if not first:
                pe.wait_ge(z_up.sem, j)
            for f in range(FC):
                m = pe.transpose(pz[:, f * P:(f + 1) * P], u[:, par, f * P:(f + 1) * P], ident[:, :])
            m.then_inc(z_pe.sem, 1)

        def second(j, par, first, e):
            pe.wait_ge(z_up.sem, j + 1)
            if not first:
                pe.wait_ge(y_up.sem, j)
            for f in range(FC):
                m = pe.matmul(py[:, 0:D], uT[:, par, f, :], down[:, e, f, :], start=(f == 0), stop=(f == FC - 1))
            m.then_inc(y_pe.sem, 1)

        def expert(j):
            return pe.value_load(texp_i[0:1, bass.ds(j, 1)], min_val=0, max_val=E1 - 1)

        pe.wait_ge(v.sem, 23)
        turn(0, 0, True)
        pe.wait_ge(u_in.sem, 16 * E1)
        pe.wait_ge(t["down_in"].sem, 16 * E1)

        def body(j, par, first, full):
            e = expert(j)
            pe.wait_ge(t_up.sem, j + 1)
            if full:
                pe.wait_ge(gated.sem, j - 1)
            half(j, par, 1, e, up_g)
            if not first:
                turn_u(j - 1, 1 - par, isinstance(j, int) and j == 1)
            half(j, par, 0, e, up_a)
            if not (isinstance(j, int) and j == MT - 1):
                turn(j + 1, 1 - par, False)
            if not first:
                second(j - 1, 1 - par, isinstance(j, int) and j == 1, expert(j - 1))

        tiles_loop(pe, body)
        turn_u(MT - 1, 0, False)
        second(MT - 1, 0, False, expert(MT - 1))

    @block.scalar
    def _(act):
        act.sem_inc(tup.sem, 2)
        act.sem_inc(nxd.sem, 2)
        act.sem_inc(xnk.sem, 2)

        def turned_x(b, par, early):
            act.wait_ge(nrm.sem, b + 3)
            act.wait_ge(nxd.sem, b + 2)
            act.activation(sq[:], xn[:, par, :], ACT.Square, accum_out=nx[:, bass.ds(b, 1)]).then_inc(nxd.sem, 1)
            act.wait_ge(tpd.sem, b + 1)
            if not early:
                act.wait_ge(dotd.sem, b - 1)
            act.activation(xnT[:, par].rearrange("p c s -> p (c s)"), xbank[par][:, 0:DC * S], ACT.Copy).then_inc(tup.sem, 1)
            act.activation(xn_all[:, b, :], xn[:, par, :], ACT.Copy).then_inc(xnk.sem, 1)

        turned_x(0, 0, True)
        turned_x(1, 1, True)
        with act.Fori(1, B // 2) as j:
            turned_x(2 * j, 0, False)
            turned_x(2 * j + 1, 1, False)

        def body(j, par, first, full):
            act.wait_ge(up_g.sem, j + 1)
            if full:
                act.wait_ge(gated.sem, j - 1)
            act.activation(th[:, par, :], ph[:, par, 1, :], ACT.Tanh, scale=0.5).then_inc(thd.sem, 1)
            if not first:
                up_z(j - 1, 1 - par)

        def up_z(j, par):
            act.wait_ge(z_pe.sem, j + 1)
            act.activation(uT[:, par].rearrange("p f s -> p (f s)"), pz[:, :], ACT.Copy).then_inc(z_up.sem, 1)

        tiles_loop(act, body)
        up_z(MT - 1, 0)

    @block.vector
    def _(dve):
        dve.wait_ge(s_in.sem, 32)
        dve.tensor_tensor(csq[:], cT1[:], cT1[:], ALU.mult).then_inc(v.sem, 1)
        dve.sem_inc(lnd.sem, 2)
        dve.sem_inc(nrm.sem, 2)
        dve.sem_inc(dup.sem, 2)

        def dot_up(b):
            dve.wait_ge(dotd.sem, b + 1)
            dve.tensor_copy(dots[:, b, :], pd[:S, 0:E1]).then_inc(dup.sem, 1)

        def norm(b, par):
            dve.wait_ge(kept.sem, b + 1)
            dve.tensor_scalar(xl[:, par, :], x_all[:, b, :], mean[:, bass.ds(b, 1)], roots[:, 0, bass.ds(b, 1)],
                              ALU.subtract, ALU.mult).then_inc(lnd.sem, 1)
            dve.wait_ge(lnd.sem, b + 3)
            dve.wait_ge(xnk.sem, b + 1)
            dve.scalar_tensor_tensor(out=xn[:, par, :], in0=xl[:, par, :], scalar=roots[:, 1, bass.ds(b, 1)], in1=scale[:],
                                     op0=ALU.mult, op1=ALU.mult).then_inc(nrm.sem, 1)

        norm(0, 0)
        norm(1, 1)
        with dve.Fori(1, B // 2) as j:
            for par in range(2):
                b = 2 * j + par
                norm(b, par)
                dot_up(b - 2)
        dot_up(B - 2)
        dot_up(B - 1)

        n = [1]

        def chain(ins):
            n[0] += 1
            ins.then_inc(v.sem, 1)
            dve.wait_ge(v.sem, n[0])

        dve.wait_ge(routed_pe.sem, 1)
        chain(dve.tensor_copy(ny[:], pz[:S, 0:E1]))
        dve.wait_ge(nxd.sem, B + 2)
        dve.wait_ge(dup.sem, B + 2)
        chain(dve.tensor_tensor(dist[:], nx[:, :].unsqueeze(2).to_broadcast([S, B, E1]),
                                ny[:, :].unsqueeze(1).to_broadcast([S, B, E1]), ALU.add))
        chain(dve.scalar_tensor_tensor(out=dist[:], in0=dots[:], scalar=2.0, in1=dist[:], op0=ALU.mult, op1=ALU.subtract))
        chain(dve.tensor_reduce(best[:, 0, :], dist[:], AX.X, ALU.max))
        chain(dve.tensor_tensor(cand[:], dist[:], best[:, 0, :].unsqueeze(2).to_broadcast([S, B, E1]), ALU.is_ge))
        chain(dve.tensor_tensor(cand[:], cand[:], rank_e[:, :].unsqueeze(1).to_broadcast([S, B, E1]), ALU.mult))
        dve.tensor_reduce(best[:, 1, :], cand[:], AX.X, ALU.max).then_inc(chosen.sem, 1)
        dve.wait_ge(chosen.sem, 1)
        chain(dve.tensor_tensor(ohb[:], cand[:], best[:, 1, :].unsqueeze(2).to_broadcast([S, B, E1]), ALU.is_equal))
        chain(dve.tensor_copy(oh[:], ohb[:]))
        dve.wait_ge(routed_pe.sem, 2)
        chain(dve.tensor_copy(cnt[:], pz[:S, 0:BE].rearrange("s (b e) -> s b e", b=B)))
        src = cnt
        for k in range(4):
            w, dst = 1 << k, cum[:, k % 2]
            prev = src[:, :, :] if k == 0 else src
            dve.tensor_copy(dst[:, 0:w, :], prev[:, 0:w, :])
            chain(dve.tensor_tensor(dst[:, w:B, :], prev[:, w:B, :], prev[:, 0:B - w, :], ALU.add))
            src = dst
        total = src[:, B - 1, :]
        chain(dve.tensor_tensor(more[:], total.unsqueeze(2).to_broadcast([S, E1, B * S // P]), kk[:], ALU.is_gt))
        chain(dve.tensor_reduce(tiles[:], more[:], AX.X, ALU.add))
        chain(dve.tensor_tensor(lt[:], tiles[:, :].unsqueeze(1).to_broadcast([S, E1, E1]), less[:], ALU.mult))
        chain(dve.tensor_reduce(start[:], lt[:], AX.X, ALU.add))
        chain(dve.tensor_tensor(end[:], start[:], tiles[:], ALU.add))
        chain(dve.tensor_tensor(passed[:], end[:, :].unsqueeze(1).to_broadcast([S, MT, E1]), tj[:], ALU.is_le))
        chain(dve.tensor_reduce(texp[:], passed[:], AX.X, ALU.add))
        chain(dve.tensor_scalar(texp_i[:], texp[:], float(E1 - 1), None, ALU.min))
        dve.tensor_tensor(rank[:], src, cnt[:], ALU.subtract).then_inc(chosen.sem, 1)
        dve.wait_ge(chosen.sem, 2)
        dve.tensor_tensor(rank[:], pd[:S, 0:BE].rearrange("s (b e) -> s b e", b=B), rank[:], ALU.add).then_inc(chosen.sem, 1)
        dve.wait_ge(chosen.sem, 3)
        dve.tensor_scalar(start[:], start[:], float(P), None, ALU.mult).then_inc(chosen.sem, 1)
        dve.wait_ge(chosen.sem, 4)
        dve.tensor_tensor(rank[:], rank[:], start[:, :].unsqueeze(1).to_broadcast([S, B, E1]), ALU.add).then_inc(chosen.sem, 1)
        dve.wait_ge(chosen.sem, 5)
        dve.tensor_tensor(rank[:], rank[:], oh[:], ALU.mult).then_inc(chosen.sem, 1)
        dve.wait_ge(chosen.sem, 6)
        dve.tensor_reduce(place[:], rank[:], AX.X, ALU.add).then_inc(chosen.sem, 1)
        dve.wait_ge(chosen.sem, 7)
        chain(dve.tensor_copy(place_i[:], place[:]))

        def turned(j, par, first):
            dve.wait_ge(t_pe.sem, j + 1)
            if not first:
                dve.wait_ge(up_a.sem, j - 1)
            dve.tensor_copy(xT[:, par].rearrange("p c s -> p (c s)"), pt[:, 0:DC * P]).then_inc(t_up.sem, 1)

        def results(j, par, early):
            dve.wait_ge(y_pe.sem, j + 1)
            if not early:
                dve.wait_ge(y_out[par].sem, 8 * (j - par))
            dve.tensor_copy(ysb[:, par, :], py[:, 0:D]).then_inc(y_up.sem, 1)

        def body(j, par, first, full):
            dve.wait_ge(thd.sem, j + 1)
            if full:
                dve.wait_ge(z_pe.sem, j - 1)
            dve.scalar_tensor_tensor(out=u[:, par, :], in0=th[:, par, :], scalar=1.0, in1=ph[:, par, 1, :],
                                     op0=ALU.add, op1=ALU.mult).then_inc(lnd.sem, 1)
            dve.wait_ge(lnd.sem, j + B + 3)
            dve.wait_ge(up_a.sem, j + 1)
            dve.scalar_tensor_tensor(out=u[:, par, :], in0=u[:, par, :], scalar=0.5, in1=ph[:, par, 0, :],
                                     op0=ALU.mult, op1=ALU.mult).then_inc(gated.sem, 1)
            if not (isinstance(j, int) and j == MT - 1):
                turned(j + 1, 1 - par, isinstance(j, int) and j == 0)
            if not first:
                results(j - 1, 1 - par, isinstance(j, int) and j <= 2)

        turned(0, 0, True)
        tiles_loop(dve, body)
        results(MT - 1, 0, False)
        dve.wait_ge(kept.sem, B + 2)
        for b in range(B):
            if b % GB == 0:
                dve.wait_ge(gathered[b // GB].sem, 16 * GB)
            dve.tensor_tensor(x_all[:, b, :], x_all[:, b, :], yg[:, b, :], ALU.add).then_inc(added.sem, 1)

    @block.gpsimd
    def _(pool):
        pool.memset(onesf[:], 1.0).then_inc(made.sem, 1)
        pool.memset(onesb[:], 1.0).then_inc(made.sem, 1)
        pool.memset(before[:], 1.0).then_inc(made.sem, 1)
        pool.memset(less[:], 1.0).then_inc(made.sem, 1)
        pool.wait_ge(made.sem, 4)
        pool.affine_select(out=before[:], in_=before[:], compare_op=ALU.is_gt, fill=0.0, base=0,
                           pattern=[[1, S]], channel_multiplier=-1).then_inc(made.sem, 1)
        pool.affine_select(out=less[:], in_=less[:], compare_op=ALU.is_gt, fill=0.0, base=0,
                           pattern=[[1, E1], [-1, E1]], channel_multiplier=0).then_inc(made.sem, 1)
        pool.iota(rank_e[:], [[-1, E1]], base=E1, channel_multiplier=0, allow_small_or_imprecise_dtypes=True).then_inc(made.sem, 1)
        pool.iota(kk[:], [[0, E1], [P, B * S // P]], base=0, channel_multiplier=0, allow_small_or_imprecise_dtypes=True).then_inc(made.sem, 1)
        pool.iota(tj[:], [[1, MT], [0, E1]], base=0, channel_multiplier=0, allow_small_or_imprecise_dtypes=True).then_inc(made.sem, 1)
        pool.engine_nop().then_inc(made.sem, 1)
        pool.sem_inc(kept.sem, 2)
        with pool.Fori(0, B // 2) as j:
            for par in range(2):
                b = 2 * j + par
                pool.wait_ge(lnd.sem, b + 3)
                pool.sem_inc(apart.sem, 1)
                pool.tensor_tensor(x_all[:, b, :], x_all[:, b, :], xl[:, par, :], ALU.add).then_inc(kept.sem, 1)
        pool.wait_ge(t["zeroed"].sem, 16)
        pool.wait_ge(v.sem, 23)
        pool.wait_ge(xnk.sem, B + 2)
        for b in range(B):
            pool.indirect_dma_start(out=xs, out_offset=bass.IndirectOffsetOnAxis(ap=place_i[:, b:b + 1], axis=0),
                                    in_=xn_all[:, b, :], in_offset=None).then_inc(scattered.sem, 16)
        pool.wait_ge(y_out[0].sem, 16 * ((MT + 1) // 2))
        pool.wait_ge(y_out[1].sem, 16 * (MT // 2))
        for b in range(B):
            pool.indirect_dma_start(out=yg[:, b, :], out_offset=None, in_=ys,
                                    in_offset=bass.IndirectOffsetOnAxis(ap=place_i[:, b:b + 1], axis=0)).then_inc(gathered[b // GB].sem, 16)


def program(nc, a, out):
    with ExitStack() as ctx:
        def sb(c, name, shape, dt=F32):
            return c.enter_context(nc.sbuf_tensor(name, shape, dt))

        def sig(name, per=1):
            return Sig(ctx.enter_context(nc.semaphore(name)), per)

        down = sb(ctx, "down", [P, E1, F1 // P, D])
        place, w = down[:, :, :, :].rearrange("p e f d -> p (e f d)"), DC * E0 * F0
        t = {"x_all": sb(ctx, "x_all", [S, B, D]), "ident": sb(ctx, "ident", [P, P]), "down": down,
             "w1": place[:, 0:w].rearrange("p (c n) -> p c n", c=DC),
             "w2": place[:, w:w + E0 * D].rearrange("p (e d) -> p e d", e=E0),
             "xnT_all": place[:, w + E0 * D:w + E0 * D + DC * B * S].rearrange("p (c s) -> p c s", c=DC),
             "mean": sb(ctx, "mean", [S, B]), "roots": sb(ctx, "roots", [S, 2, B]),
             "rows_by_place": nc.dram_tensor("rows_by_place", [MT * P, D], F32).ap(),
             "slot_w_in": sig("slot_w_in"), "c_in0": sig("c_in0", 16 * (KT + 1) * GB),
             "down_in": sig("down_in"), "zeroed": sig("zeroed")}
        with ExitStack() as slots:
            t.update({name: sb(slots, name, shape) for name, shape in SLOT_WEIGHTS.items()})
            t.update({"wqk": sb(slots, "wqk", [P, DC, D]), "brz": sb(slots, "brz", [P, 4])})
            t.update({name: [sb(slots, f"{name}_{part}", [P, DC, 3 * D], F32R) for part in ("hi", "lo")] for name in ("wg", "wh")})
            t.update({name: sb(slots, name, [KP, B * KT]) for name in ("row_root", "row_rms")})
            t.update({"cx0": sb(slots, "cx0", [KP, GB, KT, D + 1]), "cT0": sb(slots, "cT0", [P, GB, DC, KEYS])})
            with ExitStack() as dense:
                t.update({"gates": sb(dense, "gates", [S, B, E0]), "b1": sb(dense, "b1", [P, E0])})
                for phase in (phase_1, phase_2):
                    with ExitStack() as own:
                        phase(nc, own, a, t)
                    nc.all_engine_barrier()
            with ExitStack() as own:
                phase_3(nc, own, a, t)
            nc.all_engine_barrier()
        with ExitStack() as own:
            phase_4(nc, own, a, t, out)


def lay_out(**x):
    import numpy as np
    x = {k: np.asarray(v) for k, v in x.items()}
    c = np.ascontiguousarray

    def heads(w):
        return c(w.transpose(1, 0, 2).reshape(D, H * DK))

    def padded(w):
        w = w.reshape(H, DK, -1)
        return c(np.concatenate([w, np.zeros((H, HP - DK, w.shape[2]), w.dtype)], 1).reshape(H * HP, -1))

    def columns(v):
        return c(v.reshape(-1, P).T)

    return {
        "x": c(x["x"]),
        "ctx": c(x["ctx_1024"]),
        "ctxT": c(x["ctx_1024"].transpose(0, 2, 1)),
        "mask": c(x["mask_BxSxS2_bk1"]),
        "wq": heads(x["L0_xattn_Wq"]), "wk": heads(x["L0_xattn_Wk"]), "wv": heads(x["L0_xattn_Wv"]),
        "bq": columns(x["L0_xattn_bq"].reshape(-1)), "bk": columns(x["L0_xattn_bk"].reshape(-1)),
        "bv": columns(padded(x["L0_xattn_bv"].reshape(-1, 1)).reshape(-1)),
        "wo": padded(x["L0_xattn_Wo"]), "bo": c(x["L0_xattn_bo"]),
        "w1": c(x["L0_ffn_w1"].transpose(1, 0, 2).reshape(D, E0 * F0)), "b1": c(x["L0_ffn_b1"].T),
        "w2": c(x["L0_ffn_w2"]), "b2": c(x["L0_ffn_b2"]), "cent": c(x["L0_ffn_centroids"]),
        "w_routeT": c(x["L0_ffn_w_route"].T),
        "xwq": c(x["L1_xattn_Wq"]), "xwk": c(x["L1_xattn_Wk"]), "xwv": c(x["L1_xattn_Wv"]),
        "wihT": c(x["L1_xattn_gru_wih"].T), "whhT": c(x["L1_xattn_gru_whh"].T),
        "bih": columns(x["L1_xattn_gru_bih"]), "bhh": columns(x["L1_xattn_gru_bhh"]),
        "slot_w": columns(x["L1_xattn_slot_norm_w"]), "in_w": columns(x["L1_xattn_input_norm_w"]), 
        "in_w_row": c(x["L1_xattn_input_norm_w"].reshape(1, D)),
        "scale": c(x["L1_ffn_scale"].reshape(1, D)), "centT": c(x["L1_ffn_centroids"].T), "cent1": c(x["L1_ffn_centroids"]),
        "up": c(x["L1_ffn_up_w"]), "down": c(x["L1_ffn_down_w"]),
    }


def kernel(**inputs):
    import numpy as np
    import concourse.bacc as bacc
    from concourse import mybir as _mybir
    from concourse.bass_utils import run_bass_kernel_spmd

    nc = bacc.Bacc("TRN2", target_bir_lowering=False, num_devices=1)
    arrays, aps = {}, {}
    for name, array in lay_out(**inputs).items():
        arrays[f"in_{name}_dram"] = array
        aps[name] = nc.dram_tensor(f"in_{name}_dram", array.shape, _mybir.dt.from_np(array.dtype), kind="ExternalInput").ap()
    out = nc.dram_tensor("out_0_dram", (B, S, D), _mybir.dt.from_np(np.dtype("float32")), kind="ExternalOutput").ap()
    program(nc, aps, out)
    result = run_bass_kernel_spmd(nc, [arrays], core_ids=[0])
    return result.results[0]["out_0_dram"]
```

```python
from contextlib import ExitStack

import concourse.bass as bass
from concourse import mybir

F32 = mybir.dt.float32
F32R = mybir.dt.float32r
BF16 = mybir.dt.bfloat16
U8 = mybir.dt.uint8
U32 = mybir.dt.uint32
I32 = mybir.dt.int32
ALU = mybir.AluOpType
ACT = mybir.ActivationFunctionType
AX = mybir.AxisListType

B, S, D, KEYS = 16, 112, 256, 375
P = 128
DC = D // P
H, DK = 16, 16
HC = P // DK
KT = 3
KP = KEYS // KT
HP = 32
HG = H // 4
E0, F0 = 8, 128
E1, F1 = 8, 512
GB = 4
NG = B // GB
GN = GB * S
LN_EPS, RMS_EPS, SLOT_EPS = 1e-5, 1e-6, 1e-6
NORM_EPS = 1e-12
ROUNDS = 3
MASKED = -1e-6
PLACE_ROW = 2 * D + 1
MT = (B * S) // P + E1 - 1


class Sig:

    def __init__(self, sem, per=1):
        self.sem, self.per = sem, per

    def __call__(self, i, k):
        return self.sem, i * self.per + k


def norm_roots(pool, sig, wait, apart, mv, half, tmp, mean, roots, at):
    var = mv[:, :, 1]
    pool.sem_inc(apart.sem, 1)
    pool.tensor_scalar(tmp[:, 0, :], var, LN_EPS, None, ALU.add).then_inc(sig.sem, 1)
    pool.wait_ge(*wait(1))
    pool.sem_inc(apart.sem, 1)
    pool.tensor_tensor(roots[:, 0, at], tmp[:, 0, :], half, ALU.pow).then_inc(sig.sem, 1)
    pool.wait_ge(*wait(2))
    pool.sem_inc(apart.sem, 1)
    pool.tensor_tensor(tmp[:, 1, :], var, roots[:, 0, at], ALU.mult).then_inc(sig.sem, 1)
    pool.wait_ge(*wait(3))
    pool.sem_inc(apart.sem, 1)
    pool.tensor_tensor(tmp[:, 2, :], tmp[:, 1, :], roots[:, 0, at], ALU.mult).then_inc(sig.sem, 1)
    pool.wait_ge(*wait(4))
    pool.sem_inc(apart.sem, 1)
    pool.tensor_scalar(tmp[:, 3, :], tmp[:, 2, :], RMS_EPS, None, ALU.add).then_inc(sig.sem, 1)
    pool.wait_ge(*wait(5))
    pool.sem_inc(apart.sem, 1)
    pool.tensor_tensor(roots[:, 1, at], tmp[:, 3, :], half, ALU.pow).then_inc(sig.sem, 1)
    pool.sem_inc(apart.sem, 1)
    pool.tensor_copy(mean[:, at], mv[:, :, 0]).then_inc(sig.sem, 1)


def phase_1(nc, ctx, a, t):
    def sb(name, shape, dt=F32):
        return ctx.enter_context(nc.sbuf_tensor(name, shape, dt))

    def psum(name, shape):
        return ctx.enter_context(nc.psum_tensor(name, shape, F32))

    def sem(name, per=1):
        return Sig(ctx.enter_context(nc.semaphore(name)), per)

    x_all, ident, xnT_all, gates_all = t["x_all"], t["ident"], t["xnT_all"], t["gates"]
    R = 4
    LT, LA = 3, 4

    wq = sb("wq", [P, DC, D])
    wk = sb("wk", [P, DC, D])
    wv = sb("wv", [P, DC, D])
    wo = sb("wo", [P, HG, D])
    bq = sb("bq", [P, DC])
    bk = sb("bk", [P, DC])
    bv = sb("bv", [P, HG])
    bo = sb("bo", [1, D])
    bvb = sb("bvb", [P, HG, P])
    bvo = sb("bvo", [P, D])
    b2 = sb("b2", [E0, D])
    cent = sb("cent", [E0, D])
    csq = sb("csq", [E0, D])
    cn = sb("cn", [E0, 3])
    cr = sb("cr", [P, DC, 2 * E0])
    hmask = sb("hmask", [P, HC])
    ones = sb("ones", [P, P])
    mhalf = sb("mhalf", [P, 1])
    ctxT = [sb(f"ctxT{i}", [P, DC, KEYS]) for i in range(2)]
    passes = ((0, 0), (0, 1), (1, 0))
    KW = KEYS + KEYS % 2
    ctxs = [sb(f"ctx_{part}", [P, DC, KW], F32R) for part in ("hi", "lo")]
    wks = [sb(f"wk_{part}", [P, DC, D], F32R) for part in ("hi", "lo")]
    wvs = [sb(f"wv_{part}", [P, DC, D], F32R) for part in ("hi", "lo")]
    mask8 = [sb(f"mask8_{i}", [S, KEYS], U8) for i in range(2)]
    maskf = [sb(f"maskf{i}", [S, KEYS]) for i in range(2)]
    kT = [sb(f"kT{i}", [P, DC, KEYS]) for i in range(2)]
    v = [sb(f"v{i}", [KP, KT, H, HP]) for i in range(2)]
    qm = [sb(f"qm{i}", [P, H, S]) for i in range(2)]
    nmax = [sb(f"nmax{i}", [S, H]) for i in range(2)]
    esum = [sb(f"esum{i}", [S, H]) for i in range(2)]
    st, mv, rstd = sb("st", [S, 6]), sb("mv", [S, 2]), sb("rstd", [S, 2])
    xn, xnT, qT = sb("xn", [S, D]), sb("xnT", [P, DC, S]), sb("qT", [P, DC, S])
    rec, recx = sb("rec", [S, H]), sb("recx", [S, H, HP])
    oT, oTn = sb("oT", [P, HG, S]), sb("oTn", [P, HG, S])
    st2, mv2, rs2 = sb("st2", [S, 6]), sb("mv2", [S, 2]), sb("rs2", [S, 6])
    xn2, xnT2 = sb("xn2", [S, D]), sb("xnT2", [P, DC, S])
    lg, lgt, top, keep = sb("lg", [S, 2 * E0]), sb("lgt", [S, E0]), sb("top", [S, 8]), sb("keep", [S, E0])
    ntop, eg, ek = sb("ntop", [S, 1]), sb("eg", [S, E0]), sb("ek", [S, E0])
    gs, gr, gate, gT = sb("gs", [S, 1]), sb("gr", [S, 1]), sb("gate", [S, E0]), sb("gT", [E0, S])
    rows, cols = t["cx0"][:].rearrange("p i t d -> p (i t d)"), t["cT0"][:].rearrange("p i c m -> p (i c m)")
    sm = rows[:S, 0:R * KEYS].rearrange("p (r m) -> p r m", r=R)
    ex = rows[:S, R * KEYS:2 * R * KEYS].rearrange("p (r m) -> p r m", r=R)
    eT = cols[:KP, 0:R * KT * S].rearrange("p (r t s) -> p r t s", r=R, t=KT)

    ps = psum("ps", [P, 2, 512])
    pt = psum("pt", [P, 2, 512])
    po = psum("po", [P, 2, 512])
    pf = psum("pf", [P, 2, 512])

    NW, NS = 5, 6
    NF, NT = 6, 6
    w_in, s_in, x_in, rest_in, w2_in = (sem(n) for n in ("w_in", "s_in", "x_in", "rest_in", "w2_in"))
    apart = sem("apart")
    made = sem("made")
    su_d, su_p, su_pe = sem("su_d"), sem("su_p"), sem("su_pe")
    loaded = [sem("loaded0", 32), sem("loaded1", 32)]
    c_split = sem("c_split", 2)
    w_split = sem("w_split")
    conv = sem("conv")
    scored = sem("scored", H)
    masked = sem("masked", H)
    maxed = sem("maxed", H)
    exped = sem("exped", H)
    turned = sem("turned", H)
    eT_up = sem("eT_up", H)
    times_v = sem("times_v", H)
    f_pe, f_ev = sem("f_pe", NF), sem("f_ev", NF)
    t_pe, t_ev = sem("t_pe", NT), sem("t_ev", NT)
    f_d, f_p = sem("f_d", 3), sem("f_p", 3)
    qm_up = sem("qm_up", DC)
    t_d, t_p = sem("t_d", 13), sem("t_p", 8)
    recd = sem("recd", 1)
    t_a = sem("t_a", 1)
    oT_up = sem("oT_up", 1)

    PF = [("f", 0, 2), ("t", 0, 3), ("f", 1, 4), ("t", 1, 5), ("f", 2, 6), ("f", 3, 7), ("t", 2, 8),
          ("t", 3, 10), ("f", 4, 11), ("f", 5, 13), ("t", 4, 13), ("t", 5, 15)]
    BANK = {(k, n): i % 2 for i, (k, n, _) in enumerate(PF)}

    def last_use(k, n, b, prev, nxt):
        i = [u[:2] for u in PF].index((k, n))
        here = [u for j, u in enumerate(PF[:i]) if j % 2 == i % 2 and (nxt if u[0] == "f" else prev)]
        if here:
            kk, m, _ = here[-1]
            return f_ev(b + 1, m + 1) if kk == "f" else t_ev(b - 1, m + 1)
        static = isinstance(b, int)
        before = [u for j, u in enumerate(PF) if j % 2 == i % 2 and (u[0] == "f" or not (static and b <= 1))]
        kk, m, _ = before[-1]
        return f_ev(b, m + 1) if kk == "f" else t_ev(b - 2, m + 1)

    def fbank(k, n):
        return pf[:, BANK[(k, n)], :]

    def bodies(eng, body):
        body(0, 0, False, True)
        body(1, 1, True, True)
        with eng.Fori(1, B // 2 - 1) as j:
            body(2 * j, 0, True, True)
            body(2 * j + 1, 1, True, True)
        body(B - 2, 0, True, True)
        body(B - 1, 1, True, False)

    block = ctx.enter_context(nc.Block())

    @block.sync
    def _(sp):
        def load(b, par):
            sp.dma_start(ctxT[par][:], a["ctxT"][b].rearrange("(c p) m -> p c m", p=P)).then_inc(loaded[par].sem, 16)
            sp.dma_start(mask8[par][:], a["mask"][b]).then_inc(loaded[par].sem, 16)

        x = a["x"].rearrange("b s d -> s b d")
        sp.dma_start(x_all[:, 0:2, :], x[:, 0:2, :]).then_inc(x_in.sem, 16)
        for dst, src in ((wq[:], a["wq"].rearrange("(c p) n -> p c n", p=P)),
                         (bq[:], a["bq"]),
                         (wk[:], a["wk"].rearrange("(c p) n -> p c n", p=P)),
                         (bk[:], a["bk"])):
            sp.dma_start(dst, src).then_inc(w_in.sem, 16)
        load(0, 0)
        sp.dma_start(wv[:], a["wv"].rearrange("(c p) n -> p c n", p=P)).then_inc(w_in.sem, 16)
        for dst, src in ((cent[:], a["cent"]),
                         (cr[:, :, E0:2 * E0], a["w_routeT"].rearrange("(c p) e -> p c e", p=P)),
                         (wo[:], a["wo"].rearrange("(c p) n -> p c n", p=P)),
                         (bv[:], a["bv"]),
                         (bo[:], a["bo"].rearrange("(o n) -> o n", o=1)),
                         (b2[:], a["b2"])):
            sp.dma_start(dst, src).then_inc(s_in.sem, 16)
        sp.dma_start(x_all[:, 2:B, :], x[:, 2:B, :]).then_inc(rest_in.sem, 16)
        load(1, 1)
        sp.dma_start(t["w1"], a["w1"].rearrange("(c p) n -> p c n", p=P)).then_inc(w2_in.sem, 16)
        sp.dma_start(t["w2"], a["w2"].rearrange("e p n -> p e n")).then_inc(w2_in.sem, 16)
        sp.dma_start(t["b1"][:], a["b1"]).then_inc(w2_in.sem, 16)

        slot_weight_loads(sp, a, t)

        with sp.Fori(0, B // 2 - 1) as j:
            for par in range(2):
                sp.wait_ge(*conv(2 * j + par, 1))
                sp.sem_inc(apart.sem, 1)
                load(2 * j + par + 2, par)
        sp.wait_ge(w2_in.sem, 48)

    @block.tensor
    def _(pe):
        def front(b, n, par):
            out = fbank("f", n)
            if n == 0:
                pe.wait_ge(*f_d(b, 3))
                for c in range(DC):
                    m = pe.transpose(out[:, c * S:(c + 1) * S], xn[:, c * P:(c + 1) * P], ident[:S, :S])
            elif n == 1:
                pe.wait_ge(*f_ev(b, 1))
                for o in range(DC):
                    for c in range(DC):
                        m = pe.matmul(out[:, o * S:(o + 1) * S], wq[:, c, o * P:(o + 1) * P], xnT[:, c, :],
                                      start=(c == 0), stop=(c == DC - 1))
            elif n in (2, 3):
                o = n - 2
                if n == 2:
                    pe.wait_ge(*c_split(b, 2))
                terms = [(c, *p) for c in range(DC) for p in passes]
                for i, (c, x, y) in enumerate(terms):
                    m = pe.matmul(out[:, 0:KW], wks[x][:, c, o * P:(o + 1) * P], ctxs[y][:, c, :],
                                  start=(i == 0), stop=(i == len(terms) - 1))
            else:
                for kt in ((0, 1) if n == 4 else (2,)):
                    terms = [(c, *p) for c in range(DC) for p in passes]
                    for i, (c, x, y) in enumerate(terms):
                        m = pe.matmul(out[:KP, kt % 2 * D:(kt % 2 + 1) * D], ctxs[x][:, c, kt * KP:(kt + 1) * KP],
                                      wvs[y][:, c, :], start=(i == 0), stop=(i == len(terms) - 1))
            m.then_inc(f_pe.sem, 1)

        def tail(b, n):
            out = fbank("t", n)
            if n == 0:
                pe.wait_ge(*t_d(b, 1))
                for g in range(HG):
                    m = pe.transpose(out[:, g * S:(g + 1) * S],
                                     recx[:, 4 * g:4 * g + 4, :].rearrange("s h p -> s (h p)"), ident[:S, :S])
            elif n == 1:
                pe.wait_ge(*t_ev(b, 1))
                for g in range(HG):
                    m = pe.matmul(out[:S, 0:D], oTn[:, g, :], wo[:, g, :], start=(g == 0), stop=(g == HG - 1))
            elif n == 2:
                pe.wait_ge(*t_d(b, 4))
                for c in range(DC):
                    m = pe.transpose(out[:, c * S:(c + 1) * S], xn2[:, c * P:(c + 1) * P], ident[:S, :S])
            elif n == 3:
                pe.wait_ge(*t_ev(b, 3))
                for c in range(DC):
                    m = pe.matmul(out[:S, 0:2 * E0], xnT2[:, c, :], cr[:, c, :], start=(c == 0), stop=(c == DC - 1))
            elif n == 4:
                pe.wait_ge(*t_d(b, 13))
                m = pe.transpose(out[:E0, 0:S], gate[:, :], ident[:S, :S])
            else:
                pe.wait_ge(*t_ev(b, 5))
                m = pe.matmul(out[:S, 0:D], gT[:, :], b2[:, :], start=True, stop=True)
            m.then_inc(t_pe.sem, 1)

        def score(b, s, par, ring_full):
            if ring_full:
                pe.wait_ge(*masked(b, s - 1))
            pe.matmul(ps[:S, s % 2, 0:KEYS], qm[par][:, s, :], kT[par][:, s // HC, :],
                      start=True, stop=True).then_inc(scored.sem, 1)

        def turn(b, s, ring_full):
            pe.wait_ge(*exped(b, s + 1))
            if ring_full:
                pe.wait_ge(*eT_up(b, s - 1))
            for kt in range(KT):
                m = pe.transpose(pt[:KP, s % 2, kt * S:(kt + 1) * S], ex[:, s % R, kt * KP:(kt + 1) * KP], ident[:S, :S])
            m.then_inc(turned.sem, 1)

        def attend(b, s, par, wait_out):
            hh = s % H
            g, j = hh // 4, hh % 4
            pe.wait_ge(*eT_up(b, s + 1))
            if wait_out:
                pe.wait_ge(*oT_up(b - 2, 1))
            for kt in range(KT):
                m = pe.matmul(po[j * HP:(j + 1) * HP, par, g * S:(g + 1) * S], v[par][:, kt, hh, :],
                              eT[:, s % R, kt, :], start=(kt == 0), stop=(kt == KT - 1))
            m.then_inc(times_v.sem, 1)

        def body(b, par, prev, nxt):
            pe.wait_ge(*qm_up(b, DC))
            pe.wait_ge(*f_ev(b, NF))
            for s in range(H):
                score(b, s, par, prev or s >= 2)
                if prev or s >= LT:
                    turn(b, s - LT, prev or s >= LT + 2)
                if prev or s >= LA:
                    mine = s >= LA
                    attend(b, s - LA, par if mine else 1 - par, s == LA and not (isinstance(b, int) and b < 2))
                for k, n, at in PF:
                    if at == s and (nxt if k == "f" else prev):
                        pe.wait_ge(*last_use(k, n, b, prev, nxt))
                        if k == "f":
                            front(b + 1, n, 1 - par)
                        else:
                            tail(b - 1, n)

        pe.wait_ge(made.sem, 8)
        pe.wait_ge(w_in.sem, 16 * NW)
        pe.wait_ge(w_split.sem, 4)
        for n in range(NF):
            if n == 3:
                pe.wait_ge(*f_ev(0, 2))
            elif n == 2:
                pass
            elif n == 4:
                pe.wait_ge(*f_ev(0, 3))
            elif n == 5:
                pe.wait_ge(*f_ev(0, 4))
            if n:
                pe.wait_ge(*f_ev(0, n))
            front(0, n, 0)
        pe.wait_ge(s_in.sem, 16 * NS)
        pe.wait_ge(*f_ev(0, NF))
        pe.wait_ge(su_d.sem, 2)
        for g in range(HG):
            pe.matmul(pf[:, 0, 0:D], bvb[:, g, :], wo[:, g, :], start=(g == 0), stop=False)
        pe.matmul(pf[:, 0, 0:D], ones[0:1, :], bo[:, :], start=False, stop=True)
        pe.wait_ge(su_d.sem, 3)
        for c in range(DC):
            m = pe.transpose(pf[:, 1, c * E0:(c + 1) * E0], csq[:, c * P:(c + 1) * P], ident[:E0, :E0])
        m.then_inc(su_pe.sem, 1)
        pe.wait_ge(su_d.sem, 5)
        bodies(pe, body)
        last = B - 1
        for s in range(H - LT, H):
            turn(last, s, True)
            attend(last, s - LA + LT, 1, False)
        for s in range(H - LA + LT, H):
            attend(last, s, 1, False)
        for n in range(NT):
            pe.wait_ge(*(t_ev(last, n) if n else t_ev(last - 1, NT)))
            tail(last, n)

    @block.scalar
    def _(act):
        def exp(b, s, par, ring_full):
            act.wait_ge(*maxed(b, s + 1))
            if ring_full:
                act.wait_ge(*turned(b, s - R + 1))
            act.activation(ex[:, s % R, :], sm[:, s % R, :], ACT.Exp, bias=nmax[par][:, s % H:s % H + 1],
                           accum_out=esum[par][:, s % H:s % H + 1]).then_inc(exped.sem, 1)

        def up(b, s, ring_full):
            act.wait_ge(*turned(b, s + 1))
            if ring_full:
                act.wait_ge(*times_v(b, s - R + 1))
            act.activation(eT[:, s % R, :, :].rearrange("p t s -> p (t s)"), pt[:KP, s % 2, 0:KT * S],
                           ACT.Copy).then_inc(eT_up.sem, 1)

        def o_up(b, par, first):
            act.wait_ge(*times_v(b, H))
            if not first:
                act.wait_ge(*t_ev(b - 1, 1))
            act.activation(oT[:, :, :].rearrange("p g s -> p (g s)"), po[:, par, 0:HG * S], ACT.Copy).then_inc(oT_up.sem, 1)

        def gate_exp(b):
            act.wait_ge(*t_d(b, 9))
            act.activation(eg[:], lgt[:], ACT.Exp, bias=ntop[:]).then_inc(t_a.sem, 1)

        def body(b, par, prev, nxt):
            for s in range(H):
                if prev or s >= 1:
                    exp(b, s - 1, par if s >= 1 else 1 - par, prev or s >= R + 1)
                if prev or s >= LT:
                    up(b, s - LT, prev or s >= R + LT)
                if prev and s == LA:
                    o_up(b - 1, 1 - par, isinstance(b, int) and b == 1)
                if prev and s == 11:
                    gate_exp(b - 1)

        bodies(act, body)
        last = B - 1
        exp(last, H - 1, 1, True)
        for s in range(H - LT, H):
            up(last, s, True)
        o_up(last, 1, False)
        gate_exp(last)

    @block.vector
    def _(dve):
        def mask_max(b, s, par, ring_full):
            if s == 0:
                dve.wait_ge(*conv(b, 1))
            dve.wait_ge(*scored(b, s + 1))
            if ring_full:
                dve.wait_ge(*exped(b, s - R + 1))
            dve.scalar_tensor_tensor(out=sm[:, s % R, :], in0=ps[:S, s % 2, 0:KEYS], scalar=-MASKED,
                                     in1=maskf[par][:], op0=ALU.add, op1=ALU.mult).then_inc(masked.sem, 1)
            dve.wait_ge(*masked(b, s + 1))
            dve.tensor_reduce(nmax[par][:, s:s + 1], sm[:, s % R, :], AX.X, ALU.max, negate=True).then_inc(maxed.sem, 1)

        def stats(b):
            dve.sem_inc(apart.sem, 1)
            dve.bn_stats(st[:], x_all[:, b, :]).then_inc(f_d.sem, 1)
            dve.wait_ge(*f_d(b, 1))
            dve.sem_inc(apart.sem, 1)
            dve.bn_aggr(mv[:], st[:]).then_inc(f_d.sem, 1)

        def normalise(b, first):
            dve.wait_ge(*f_p(b, 2))
            if not first:
                dve.wait_ge(*f_pe(b - 1, 1))
            dve.tensor_scalar(xn[:], x_all[:, b, :], mv[:, 0:1], rstd[:, 1:2], ALU.subtract, ALU.mult).then_inc(f_d.sem, 1)

        def front(b, n, par, first):
            src = fbank("f", n)
            dve.wait_ge(*f_pe(b, n + 1))
            if n == 0:
                m = dve.tensor_copy(xnT[:, :, :].rearrange("p c s -> p (c s)"), src[:, 0:DC * S])
            elif n == 1:
                if not first:
                    dve.wait_ge(*qm_up(b - 1, DC))
                for c in range(DC):
                    m = dve.tensor_scalar(qT[:, c, :], src[:, c * S:(c + 1) * S], bq[:, c:c + 1], DK ** -0.5,
                                          ALU.add, ALU.mult)
            elif n in (2, 3):
                m = dve.tensor_scalar(kT[par][:, n - 2, :], src[:, 0:KEYS], bk[:, n - 2:n - 1], None, ALU.add)
            elif n == 4:
                m = dve.tensor_copy(v[par][:, 0:2, :, 0:DK], src[:KP, 0:2 * D].rearrange("p (t h d) -> p t h d", t=2, h=H))
            else:
                m = dve.tensor_copy(v[par][:, 2, :, 0:DK], src[:KP, 0:D].rearrange("p (h d) -> p h d", h=H))
            m.then_inc(f_ev.sem, 1)

        def recip(b, par, first):
            dve.wait_ge(*exped(b, H))
            dve.reciprocal(rec[:], esum[par][:]).then_inc(recd.sem, 1)
            dve.wait_ge(*recd(b, 1))
            if not first:
                dve.wait_ge(*t_pe(b - 1, 1))
            dve.tensor_copy(recx[:], rec[:, :].unsqueeze(2).to_broadcast([S, H, HP])).then_inc(t_d.sem, 1)

        def tail(b, n, first):
            src = fbank("t", n)
            dve.wait_ge(*t_pe(b, n + 1))
            if n == 0:
                dve.wait_ge(*oT_up(b, 1))
                if not first:
                    dve.wait_ge(*t_pe(b - 1, 2))
                dve.tensor_tensor(oTn[:, :, :].rearrange("p g s -> p (g s)"), src[:, 0:HG * S],
                                  oT[:, :, :].rearrange("p g s -> p (g s)"), ALU.mult).then_inc(t_ev.sem, 1)
            elif n == 1:
                dve.wait_ge(*f_p(b, 3))
                dve.tensor_tensor(x_all[:, b, :], src[:S, 0:D], x_all[:, b, :], ALU.add).then_inc(t_ev.sem, 1)
                dve.wait_ge(*t_ev(b, 2))
                dve.sem_inc(apart.sem, 1)
                dve.bn_stats(st2[:], x_all[:, b, :]).then_inc(t_d.sem, 1)
                dve.wait_ge(*t_d(b, 2))
                if not first:
                    dve.wait_ge(*t_p(b - 1, 6))
                dve.sem_inc(apart.sem, 1)
                dve.bn_aggr(mv2[:], st2[:]).then_inc(t_d.sem, 1)
            elif n == 2:
                if not first:
                    dve.wait_ge(*t_p(b - 1, 7))
                dve.tensor_copy(xnT2[:, :, :].rearrange("p c s -> p (c s)"), src[:, 0:DC * S]).then_inc(t_ev.sem, 1)
            elif n == 3:
                dve.tensor_copy(lg[:], src[:S, 0:2 * E0]).then_inc(t_ev.sem, 1)
                dve.wait_ge(*t_ev(b, 4))
                dve.wait_ge(*t_p(b, 6))
                dve.scalar_tensor_tensor(out=lgt[:], in0=lg[:, 0:E0], scalar=rs2[:, 5:6], in1=lg[:, E0:2 * E0],
                                         op0=ALU.mult, op1=ALU.add).then_inc(t_d.sem, 1)
                dve.wait_ge(*t_d(b, 5))
                dve.sem_inc(apart.sem, 1)
                dve.max(top[:], lgt[:]).then_inc(t_d.sem, 1)
                dve.wait_ge(*t_d(b, 6))
                dve.tensor_scalar(keep[:], lgt[:], top[:, 1:2], None, ALU.is_ge).then_inc(t_d.sem, 1)
                dve.tensor_scalar(ntop[:], top[:, 0:1], -1.0, None, ALU.mult).then_inc(t_d.sem, 1)
                dve.engine_nop().then_inc(t_d.sem, 1)
            elif n == 4:
                dve.tensor_copy(gT[:], src[:E0, 0:S]).then_inc(t_ev.sem, 1)
            else:
                dve.tensor_tensor(x_all[:, b, :], src[:S, 0:D], x_all[:, b, :], ALU.add).then_inc(t_ev.sem, 1)

        def normalise2(b):
            dve.wait_ge(*t_p(b, 2))
            dve.tensor_scalar(xn2[:], x_all[:, b, :], mv2[:, 0:1], rs2[:, 1:2], ALU.subtract, ALU.mult).then_inc(t_d.sem, 1)

        def gates(b, first):
            dve.wait_ge(*t_a(b, 1))
            dve.wait_ge(*t_d(b, 9))
            dve.tensor_tensor(ek[:], eg[:], keep[:], ALU.mult).then_inc(t_d.sem, 1)
            dve.wait_ge(*t_d(b, 10))
            dve.tensor_reduce(gs[:], ek[:], AX.X, ALU.add).then_inc(t_d.sem, 1)
            dve.wait_ge(*t_d(b, 11))
            dve.reciprocal(gr[:], gs[:]).then_inc(t_d.sem, 1)
            dve.wait_ge(*t_d(b, 12))
            if not first:
                dve.wait_ge(*t_p(b - 1, 8))
            dve.tensor_scalar(gate[:], ek[:], gr[:], None, ALU.mult).then_inc(t_d.sem, 1)

        def body(b, par, prev, nxt):
            first_t = isinstance(b, int) and b == 1
            for s in range(H):
                mask_max(b, s, par, prev or s >= R)
                if s == H - 1 and not (isinstance(b, int) and b >= B - 2):
                    if isinstance(b, int) and b == 0:
                        dve.wait_ge(rest_in.sem, 16)
                    stats(b + 2)
                if nxt and s == 1:
                    normalise(b + 1, False)
                if prev and s == 1:
                    recip(b - 1, 1 - par, first_t)
                for k, n, at in PF:
                    if at != s - 1 or not (nxt if k == "f" else prev):
                        continue
                    if k == "f":
                        front(b + 1, n, 1 - par, False)
                    else:
                        tail(b - 1, n, first_t)
                if prev and s == 7:
                    normalise2(b - 1)
                if prev and s == 12:
                    gates(b - 1, first_t)
            if prev:
                tail(b - 1, 5, first_t)

        dve.wait_ge(x_in.sem, 16)
        stats(0)
        normalise(0, True)
        stats(1)
        dve.wait_ge(made.sem, 8)
        dve.wait_ge(w_in.sem, 16 * NW)
        for parts, whole in ((wks, wk), (wvs, wv)):
            dve.tensor_copy(parts[0][:], whole[:]).then_inc(w_split.sem, 1)
        dve.wait_ge(w_split.sem, 2)
        for parts, whole in ((wks, wk), (wvs, wv)):
            dve.tensor_tensor(parts[1][:], whole[:], parts[0][:].bitcast(F32), ALU.subtract).then_inc(w_split.sem, 1)
        for n in range(NF):
            front(0, n, 0, True)
        dve.wait_ge(s_in.sem, 16 * NS)
        dve.tensor_copy(bvb[:], bv[:, :].unsqueeze(2).to_broadcast([P, HG, P])).then_inc(su_d.sem, 1)
        dve.tensor_tensor_reduce(csq[:], cent[:], cent[:], 1.0, 0.0, ALU.mult, ALU.add, cn[:, 0:1]).then_inc(su_d.sem, 1)
        dve.wait_ge(su_p.sem, 2)
        dve.tensor_scalar(csq[:], cent[:], cn[:, 2:3], None, ALU.mult).then_inc(su_d.sem, 1)
        dve.wait_ge(su_pe.sem, 1)
        dve.tensor_copy(bvo[:], pf[:, 0, 0:D]).then_inc(su_d.sem, 1)
        dve.tensor_copy(cr[:, :, 0:E0], pf[:, 1, 0:DC * E0].rearrange("p (c e) -> p c e", c=DC)).then_inc(su_d.sem, 1)
        bodies(dve, body)
        last = B - 1
        recip(last, 1, False)
        for n in range(NT):
            tail(last, n, False)
            if n == 1:
                normalise2(last)
            if n == 3:
                gates(last, False)

    @block.gpsimd
    def _(pool):
        def root(b, sig, k, var, tmp, out):
            pool.sem_inc(apart.sem, 1)
            pool.tensor_scalar(tmp, var, LN_EPS, None, ALU.add).then_inc(sig.sem, 1)
            pool.wait_ge(*sig(b, k))
            pool.tensor_tensor(out, tmp, mhalf[:S, :], ALU.pow).then_inc(sig.sem, 1)

        def front(b, par, early):
            pool.wait_ge(*f_d(b, 2))
            root(b, f_p, 1, mv[:, 1:2], rstd[:, 0:1], rstd[:, 1:2])
            pool.wait_ge(loaded[par].sem, 16 * (b - par) + 32)
            if not (isinstance(b, int) and b == 0):
                pool.wait_ge(*f_pe(b - 1, NF))
            hi, lo = (part[:, :, 0:KEYS] for part in ctxs)
            pool.sem_inc(apart.sem, 1)
            pool.tensor_copy(hi, ctxT[par][:]).then_inc(c_split.sem, 1)
            pool.wait_ge(*c_split(b, 1))
            pool.sem_inc(apart.sem, 1)
            pool.tensor_tensor(lo, ctxT[par][:], hi.bitcast(F32), ALU.subtract).then_inc(c_split.sem, 1)
            if not early:
                pool.wait_ge(*masked(b - 2, H))
            pool.sem_inc(apart.sem, 1)
            pool.tensor_copy(maskf[par][:], mask8[par][:]).then_inc(conv.sem, 1)
            if not (isinstance(b, int) and b == 0):
                add_bias(b)

        def add_bias(b):
            pool.wait_ge(*f_d(b, 3))
            pool.tensor_tensor(x_all[:, b, :], x_all[:, b, :], bvo[:S, :], ALU.add).then_inc(f_p.sem, 1)

        def mask_q(b, par, early):
            pool.wait_ge(*f_ev(b, 2))
            if not early:
                pool.wait_ge(*scored(b - 2, H))
            for c in range(DC):
                pool.tensor_tensor(qm[par][:, c * HC:(c + 1) * HC, :],
                                   qT[:, c, :].unsqueeze(1).to_broadcast([P, HC, S]),
                                   hmask[:, :].unsqueeze(2).to_broadcast([P, HC, S]), ALU.mult).then_inc(qm_up.sem, 1)

        def tail_2(b):
            pool.wait_ge(*t_d(b, 3))
            root(b, t_p, 1, mv2[:, 1:2], rs2[:, 0:1], rs2[:, 1:2])
            pool.wait_ge(*t_p(b, 2))
            pool.tensor_tensor(rs2[:, 2:3], mv2[:, 1:2], rs2[:, 1:2], ALU.mult).then_inc(t_p.sem, 1)
            pool.wait_ge(*t_p(b, 3))
            pool.tensor_tensor(rs2[:, 3:4], rs2[:, 2:3], rs2[:, 1:2], ALU.mult).then_inc(t_p.sem, 1)
            pool.wait_ge(*t_p(b, 4))
            pool.sem_inc(apart.sem, 1)
            pool.tensor_scalar(rs2[:, 4:5], rs2[:, 3:4], float(D), NORM_EPS ** 2, ALU.mult, ALU.max).then_inc(t_p.sem, 1)
            pool.wait_ge(*t_p(b, 5))
            pool.tensor_tensor(rs2[:, 5:6], rs2[:, 4:5], mhalf[:S, :], ALU.pow).then_inc(t_p.sem, 1)

        def tail_3(b):
            pool.wait_ge(*t_ev(b, 3))
            pool.sem_inc(apart.sem, 1)
            pool.tensor_copy(xnT_all[:, :, bass.ts(b, S)], xnT2[:]).then_inc(t_p.sem, 1)
            pool.wait_ge(*t_d(b, 13))
            pool.sem_inc(apart.sem, 1)
            pool.tensor_copy(gates_all[:, b, :], gate[:]).then_inc(t_p.sem, 1)

        def body(b, par, prev, nxt):
            static = isinstance(b, int)
            if nxt:
                front(b + 1, 1 - par, static and b == 0)
            if nxt:
                mask_q(b + 1, 1 - par, static and b == 0)
            if prev:
                tail_2(b - 1)
                tail_3(b - 1)

        pool.memset(ident[:], 0.0).then_inc(made.sem, 1)
        pool.memset(hmask[:], 1.0).then_inc(made.sem, 1)
        pool.memset(ones[:], 1.0).then_inc(made.sem, 1)
        pool.memset(mhalf[:], -0.5).then_inc(made.sem, 1)
        pool.wait_ge(made.sem, 4)
        pool.affine_select(out=ident[:], in_=ident[:], compare_op=ALU.not_equal, fill=1.0, base=0,
                           pattern=[[-1, P]], channel_multiplier=1).then_inc(made.sem, 1)
        pool.affine_select(out=hmask[:], in_=hmask[:], compare_op=ALU.is_ge, fill=0.0, base=0,
                           pattern=[[-DK, HC]], channel_multiplier=1).then_inc(made.sem, 1)
        pool.wait_ge(made.sem, 6)
        pool.affine_select(out=hmask[:], in_=hmask[:], compare_op=ALU.is_ge, fill=0.0, base=DK - 1,
                           pattern=[[DK, HC]], channel_multiplier=-1).then_inc(made.sem, 1)
        for part in ctxs:
            pool.memset(part[:, :, KEYS:KW].bitcast(F32), 0.0)
        for par in range(2):
            m = pool.memset(v[par][:], 0.0)
        m.then_inc(made.sem, 1)
        pool.wait_ge(made.sem, 8)
        front(0, 0, True)
        mask_q(0, 0, True)
        pool.wait_ge(su_d.sem, 2)
        pool.sem_inc(apart.sem, 1)
        pool.tensor_scalar(cn[:, 1:2], cn[:, 0:1], NORM_EPS ** 2, None, ALU.max).then_inc(su_p.sem, 1)
        pool.wait_ge(su_p.sem, 1)
        pool.tensor_tensor(cn[:, 2:3], cn[:, 1:2], mhalf[:E0, :], ALU.pow).then_inc(su_p.sem, 1)
        pool.wait_ge(su_d.sem, 4)
        add_bias(0)
        bodies(pool, body)
        last = B - 1
        tail_2(last)
        tail_3(last)



def phase_2(nc, ctx, a, t):
    def sb(name, shape, dt=F32):
        return ctx.enter_context(nc.sbuf_tensor(name, shape, dt))

    def sem(name, per=1):
        return Sig(ctx.enter_context(nc.semaphore(name)), per)

    x_all, xnT_all, gates_all, w1, b1, w2 = (t[k] for k in ("x_all", "xnT_all", "gates", "w1", "b1", "w2"))
    LAG, RING = 2, 4
    passes = ((0, 0), (0, 1), (1, 0))
    w1s = [sb(f"w1_{part}", [P, DC, E0 * F0], F32R) for part in ("hi", "lo")]
    w2s = [sb(f"w2_{part}", [P, E0, D], F32R) for part in ("hi", "lo")]
    xs = [sb(f"xnT_{part}", [P, DC, B * S], F32R) for part in ("hi", "lo")]
    hid = sb("hid", [P, 2, GN])
    hs = [sb(f"hid_{part}", [P, RING, GN], F32R) for part in ("hi", "lo")]
    ph = ctx.enter_context(nc.psum_tensor("ph", [P, 2, 512], F32))
    py = ctx.enter_context(nc.psum_tensor("py", [P, 2, GB, D], F32))
    hidden = sem("hidden", E0)
    gelud = sem("gelud", E0)
    hid_hi, hid_lo = sem("hid_hi", E0), sem("hid_lo", E0)
    x_hi, x_lo = sem("x_hi", 1), sem("x_lo", 1)
    w_hi, w_lo = sem("w_hi"), sem("w_lo")
    expert = sem("expert", E0)
    added = sem("added", E0 * GB)
    st, mv, mhalf = sb("p2_st", [S, GB, 6]), sb("p2_mv", [S, GB, 2]), sb("mhalf2", [S, 1])
    tmp = sb("tmp2", [S, 4, GB])
    stat = sem("stat", 2 * GB)
    root = sem("root", 7)
    apart, halved = sem("apart2"), sem("halved")
    wq, wk, wv, wih, whh, bih, bhh, slot_w, in_w, in_row = (t[k] for k in SLOT_WEIGHTS)
    wqk, wg, wh = t["wqk"], t["wg"], t["wh"]
    fact = sb("fact", [P, DC, D])
    pw = ctx.enter_context(nc.psum_tensor("pw", [P, DC * D], F32))
    rows = sb("rows", [KP, 2, KT, D])
    sqr = sb("sqr", [KP, D])
    rsq, rms = sb("rsq", [KP, GB * KT]), sb("rms", [KP, GB * KT])
    half_k = sb("half_k", [KP, 1])
    folded = sem("folded")
    su = sem("su2")
    rows_in = [sem("rows_in0"), sem("rows_in1")]
    squared = sem("squared", GB * KT)
    rooted = sem("rooted", 3)
    EXPERT_HALVES = (slice(0, E0 // 2), slice(E0 // 2, E0))
    block = ctx.enter_context(nc.Block())

    def groups(eng, body):
        body(0, True)
        with eng.Fori(1, NG - 1) as g:
            body(g, False)
        body(NG - 1, False)

    @block.sync
    def _(sp):
        def load(b, par):
            sp.dma_start(rows[:, par], a["ctx"][b].rearrange("(t p) d -> p t d", p=KP)).then_inc(rows_in[par].sem, 16)

        load(0, 0)
        load(1, 1)
        for i in range(GB):
            context_loads(sp, a, i, t["cx0"], t["cT0"], i, t["c_in0"])
        with sp.Fori(1, B // 2) as j:
            for par in range(2):
                sp.wait_ge(squared.sem, (2 * j + par - 1) * KT)
                sp.sem_inc(apart.sem, 1)
                load(2 * j + par, par)

    @block.tensor
    def _(pe):
        def second(g, e, first):
            pe.wait_ge(*hid_lo(g, e + 1))
            if first and e < 2:
                pe.wait_ge(su.sem, 2 * e + 2)
            if first and e in (0, E0 // 2):
                pe.wait_ge(w_lo.sem, 2 if e == 0 else 4)
            if not (first and e < 2):
                pe.wait_ge(*added(g, (e - 1) * GB))
            for i in range(GB):
                for n, (x, y) in enumerate(passes):
                    m = pe.matmul(py[:S, e % 2, i, :], hs[x][:, e % RING, i * S:(i + 1) * S], w2s[y][:, e % E0, :],
                                  start=(n == 0), stop=(n == len(passes) - 1))
            m.then_inc(expert.sem, 1)

        def body(g, first):
            pe.wait_ge(*x_lo(g, 1))
            for e in range(E0):
                if not (first and e < 2):
                    pe.wait_ge(*gelud(g, e - 1))
                if first and e in (0, E0 // 2):
                    pe.wait_ge(w_lo.sem, 1 if e == 0 else 3)
                terms = [(c, *p) for c in range(DC) for p in passes]
                for n, (c, x, y) in enumerate(terms):
                    m = pe.matmul(ph[:, e % 2, 0:GN], w1s[x][:, c, e * F0:(e + 1) * F0], xs[y][:, c, bass.ts(g, GN)],
                                  start=(n == 0), stop=(n == len(terms) - 1))
                m.then_inc(hidden.sem, 1)
                if not (first and e < LAG):
                    second(g, e - LAG, first)
        pe.wait_ge(t["slot_w_in"].sem, 160)
        for c in range(DC):
            for lo in (0, 512):
                for o in range(DC):
                    m = pe.matmul(py[:, c].rearrange("p i d -> p (i d)")[:, lo:min(lo + 512, 3 * D)], wv[:, o, c * P:(c + 1) * P],
                                  wih[:, o, lo:min(lo + 512, 3 * D)], start=(o == 0), stop=(o == DC - 1))
            m.then_inc(folded.sem, 1)
        for c in range(DC):
            for o in range(DC):
                m = pe.matmul(pw[:, c * D:(c + 1) * D], wq[:, o, c * P:(c + 1) * P], wk[:, o, :], start=(o == 0), stop=(o == DC - 1))
        m.then_inc(folded.sem, 1)
        groups(pe, body)
        for e in range(E0 - LAG, E0):
            second(NG - 1, e, False)

    @block.scalar
    def _(act):
        def body(g, first):
            for e in range(E0):
                act.wait_ge(*hidden(g, e + 1))
                if not (first and e < 2):
                    act.wait_ge(*hid_lo(g, e - 1))
                act.activation(hid[:, e % 2, :], ph[:, e % 2, 0:GN], ACT.Gelu, bias=b1[:, e:e + 1]).then_inc(gelud.sem, 1)
                act.wait_ge(*gelud(g, e + 1))
                if not (first and e < RING):
                    act.wait_ge(*expert(g, e - RING + 1))
                act.activation(hs[0][:, e % RING, :], hid[:, e % 2, :], ACT.Copy).then_inc(hid_hi.sem, 1)
                if e == E0 - 4 and not (isinstance(g, int) and g == NG - 1):
                    x_part(g + 1)
                for j in (2 * e - 4, 2 * e - 3):
                    if 0 <= j < GB * KT:
                        square(g, j, first)

        def square(g, j, first):
            i, kt = j // KT, j % KT
            if kt == 0:
                act.wait_ge(rows_in[i % 2].sem, 16 * (2 * g + i // 2 + 1))
            if j == 0 and not first:
                act.wait_ge(*rooted(g - 1, 1))
            if not (first and j == 0):
                act.wait_ge(*squared(g, j))
            act.activation(sqr[:], rows[:, i % 2, kt, :], ACT.Square, accum_out=rsq[:, j:j + 1]).then_inc(squared.sem, 1)

        def x_part(g):
            act.activation(xs[0][:, :, bass.ts(g, GN)], xnT_all[:, :, bass.ts(g, GN)], ACT.Copy).then_inc(x_hi.sem, 1)

        x_part(0)
        for es in EXPERT_HALVES:
            cols = slice(es.start * F0, es.stop * F0)
            act.activation(w1s[0][:, :, cols], w1[:, :, cols], ACT.Copy).then_inc(w_hi.sem, 1)
            act.activation(w2s[0][:, es, :], w2[:, es, :], ACT.Copy).then_inc(w_hi.sem, 1)
        groups(act, body)

    @block.vector
    def _(dve):
        def body(g, first):
            for e in range(E0):
                dve.wait_ge(*expert(g, e + 1))
                for i in range(GB):
                    if e:
                        dve.wait_ge(*added(g, (e - 1) * GB + i + 1))
                    x = x_all[:, g * GB + i, :]
                    dve.scalar_tensor_tensor(out=x, in0=py[:S, e % 2, i, :], scalar=gates_all[:, g * GB + i, e:e + 1],
                                             in1=x, op0=ALU.mult, op1=ALU.add).then_inc(added.sem, 1)
            for i in range(GB):
                dve.wait_ge(*added(g, (E0 - 1) * GB + i + 1))
                dve.sem_inc(apart.sem, 1)
                dve.bn_stats(st[:, i, :], x_all[:, g * GB + i, :]).then_inc(stat.sem, 1)
            if not first:
                dve.wait_ge(*root(g - 1, 7))
            for i in range(GB):
                dve.wait_ge(*stat(g, i + 1))
                dve.sem_inc(apart.sem, 1)
                dve.bn_aggr(mv[:, i, :], st[:, i, :]).then_inc(stat.sem, 1)
        hi, lo = wg
        for c in range(DC):
            full = py[:, c].rearrange("p i d -> p (i d)")
            dve.wait_ge(folded.sem, c + 1)
            for at in (slice(0, 512), slice(512, 3 * D)):
                m = dve.tensor_scalar(hi[:, c, at], full[:, at], in_w[:, c:c + 1], None, ALU.mult)
            m.then_inc(su.sem, 1)
            dve.wait_ge(su.sem, 2 * c + 1)
            for at in (slice(0, 512), slice(512, 3 * D)):
                m = dve.scalar_tensor_tensor(out=lo[:, c, at], in0=full[:, at], scalar=in_w[:, c:c + 1],
                                             in1=hi[:, c, at].bitcast(F32), op0=ALU.mult, op1=ALU.subtract)
            m.then_inc(su.sem, 1)
        for c in range(DC):
            m = dve.tensor_scalar(fact[:, c, :], in_row[:], slot_w[:, c:c + 1], D ** -0.5, ALU.mult, ALU.mult)
        m.then_inc(su.sem, 1)
        dve.tensor_copy(wh[0][:], whh[:])
        dve.tensor_tensor(t["brz"][:], bih[:, 0:4], bhh[:, 0:4], ALU.add).then_inc(su.sem, 1)
        dve.wait_ge(su.sem, 6)
        dve.tensor_scalar(t["brz"][:], t["brz"][:], 0.5, None, ALU.mult)
        dve.wait_ge(folded.sem, 3)
        dve.tensor_tensor(wqk[:, :, :].rearrange("p c d -> p (c d)"), pw[:, :], fact[:, :, :].rearrange("p c d -> p (c d)"), ALU.mult)
        dve.tensor_tensor(wh[1][:], whh[:], wh[0][:].bitcast(F32), ALU.subtract)
        groups(dve, body)

    @block.gpsimd
    def _(pool):
        def x_part(g):
            pool.wait_ge(*x_hi(g, 1))
            pool.sem_inc(apart.sem, 1)
            at = bass.ts(g, GN)
            pool.tensor_tensor(xs[1][:, :, at], xnT_all[:, :, at], xs[0][:, :, at].bitcast(F32), ALU.subtract).then_inc(x_lo.sem, 1)

        def body(g, first):
            for e in range(E0):
                pool.wait_ge(*hid_hi(g, e + 1))
                if not (first and e < RING):
                    pool.wait_ge(*expert(g, e - RING + 1))
                pool.tensor_tensor(hs[1][:, e % RING, :], hid[:, e % 2, :], hs[0][:, e % RING, :].bitcast(F32),
                                   ALU.subtract).then_inc(hid_lo.sem, 1)
                if e == E0 - 3 and not (isinstance(g, int) and g == NG - 1):
                    x_part(g + 1)
                if e == 1 and not first:
                    row_roots(g - 1)
                if e == 3 and not first:
                    slot_roots(g - 1)

        def row_roots(g):
            at = bass.ds(g * GB * KT, GB * KT)
            pool.wait_ge(*squared(g, GB * KT))
            pool.sem_inc(apart.sem, 1)
            pool.tensor_scalar(rms[:], rsq[:], 1.0 / D, RMS_EPS, ALU.mult, ALU.add).then_inc(rooted.sem, 1)
            pool.wait_ge(*rooted(g, 1))
            pool.sem_inc(apart.sem, 1)
            pool.tensor_tensor(t["row_root"][:, at], rms[:], half_k[:, 0:1].to_broadcast([KP, GB * KT]), ALU.pow).then_inc(rooted.sem, 1)
            pool.wait_ge(*rooted(g, 2))
            pool.sem_inc(apart.sem, 1)
            pool.tensor_tensor(t["row_rms"][:, at], rms[:], t["row_root"][:, at], ALU.mult).then_inc(rooted.sem, 1)

        def slot_roots(g):
            pool.wait_ge(*stat(g, 2 * GB))
            norm_roots(pool, root, lambda k: root(g, k), apart, mv, mhalf[:, 0:1].to_broadcast([S, GB]), tmp,
                       t["mean"], t["roots"], bass.ds(g * GB, GB))

        pool.memset(half_k[:], -0.5)
        pool.memset(mhalf[:], -0.5).then_inc(halved.sem, 1)
        pool.wait_ge(halved.sem, 1)
        x_part(0)
        for n, es in enumerate(EXPERT_HALVES):
            cols = slice(es.start * F0, es.stop * F0)
            pool.wait_ge(w_hi.sem, 2 * n + 1)
            pool.tensor_tensor(w1s[1][:, :, cols], w1[:, :, cols], w1s[0][:, :, cols].bitcast(F32), ALU.subtract).then_inc(w_lo.sem, 1)
            pool.wait_ge(w_hi.sem, 2 * n + 2)
            pool.tensor_tensor(w2s[1][:, es, :], w2[:, es, :], w2s[0][:, es, :].bitcast(F32), ALU.subtract).then_inc(w_lo.sem, 1)
        groups(pool, body)
        row_roots(NG - 1)
        slot_roots(NG - 1)



SLOT_WEIGHTS = {"xwq": [P, DC, D], "xwk": [P, DC, D], "xwv": [P, DC, D], "wihT": [P, DC, 3 * D], "whhT": [P, DC, 3 * D],
                "bih": [P, 6], "bhh": [P, 6], "slot_w": [P, DC], "in_w": [P, DC], "in_w_row": [P, D]}


def slot_weight_loads(sp, a, t):
    for name, shape in SLOT_WEIGHTS.items():
        src = a[name]
        if name == "in_w_row":
            src = src.to_broadcast(shape)
        elif len(shape) == 3:
            src = src.rearrange("(c p) n -> p c n", p=P)
        sp.dma_start(t[name][:], src).then_inc(t["slot_w_in"].sem, 16)


def context_loads(sp, a, b, cx, cT, i, c_in):
    for kt in range(KT):
        sp.dma_start(cx[:, i, kt, 0:D], a["ctx"][b, kt * KP:(kt + 1) * KP, :]).then_inc(c_in.sem, 16)
    sp.dma_start(cT[:, i], a["ctxT"][b].rearrange("(c p) m -> p c m", p=P)).then_inc(c_in.sem, 16)


def phase_3(nc, ctx, a, t):
    def sb(name, shape, dt=F32):
        return ctx.enter_context(nc.sbuf_tensor(name, shape, dt))

    def psum(name, shape):
        return ctx.enter_context(nc.psum_tensor(name, shape, F32))

    sigs = {}

    def sem(name, per, owner):
        s = Sig(ctx.enter_context(nc.semaphore("r_" + name)), per)
        sigs.setdefault(owner, []).append(s)
        return s

    def at(s, K, k):
        return s.sem, (K + 1) * s.per + k

    def prime(eng, owner):
        for s in sigs[owner]:
            eng.sem_inc(s.sem, s.per)

    x_all, ident = t["x_all"], t["ident"]
    UNITS = 2 * ROUNDS
    G3 = 3 * D

    wq, wk, wv, wih, whh, bih, bhh, slot_w, in_w, in_row = (t[k] for k in SLOT_WEIGHTS)
    wqk, brz, wg, wh, row_root, row_rms = (t[k] for k in ("wqk", "brz", "wg", "wh", "row_root", "row_rms"))
    ones = sb("ones3", [P, 1])
    mhalf = sb("mhalf3", [P, 1])
    cx = [t["cx0"], sb("cx1", [KP, GB, KT, D + 1])]
    cT = [t["cT0"], sb("cT1", [P, GB, DC, KEYS])]
    hT = [sb(f"hT{g}", [P, DC, GN]) for g in range(2)]
    hs = [[sb(f"h_{part}{g}", [P, DC, GN], F32R) for part in ("hi", "lo")] for g in range(2)]
    us = [[sb(f"u_{part}{g}", [P, DC, GN], F32R) for part in ("hi", "lo")] for g in range(2)]
    kr = [sb(f"kr{g}", [KP, GB * KT]) for g in range(2)]
    mean, roots = t["mean"], t["roots"]
    sl = sb("sl", [S, 2, D])
    st, mv, tmp = sb("st3", [S, GB, 6]), sb("mv3", [S, GB, 2]), sb("tmp3", [S, 4, GB])
    blank = sb("blank", [P, PLACE_ROW])
    hsq = sb("hsq", [P, DC, GN])
    ms, rinv = sb("ms", [S, GB]), sb("rinv", [S, GB])
    qs, qT = sb("qs", [S, 2, D]), sb("qT3", [P, 2, DC, S])
    nm, nb = sb("nm3", [KP, GB, KT]), sb("nb3", [KP, GB, KT])
    e = sb("e3", [KP, GB, KT, S])
    es, er = sb("es3", [KP, GB, KT]), sb("er3", [KP, GB, KT])
    uk, un = sb("uk", [S, 2, 2]), sb("un", [S, 2, D])
    tr, tz = sb("tr", [P, DC, GN]), sb("tz", [P, DC, GN])
    hh, nn = whh[:, :, 0:GN], wih[:, :, 0:GN]
    df = tr

    pa, pg, pc, pu = (psum(n, [P, 2, 512]) for n in ("pa", "pg", "pc", "pu"))

    made = Sig(ctx.enter_context(nc.semaphore("x_made")))
    blanked = Sig(ctx.enter_context(nc.semaphore("x_blank")))
    apart = Sig(ctx.enter_context(nc.semaphore("x_apart")))
    c_in = [t["c_in0"], sem("c_in1", 16 * (KT + 1) * GB, "sp")]
    sigs["sp"].append(c_in[0])
    U4 = UNITS * GB
    pe_i = sem("pe_i", 2 * GB, "pe")
    pe_ss = sem("pe_ss", UNITS - 2, "pe")
    pe_q = sem("pe_q", U4, "pe")
    pe_t = sem("pe_t", U4, "pe")
    pe_s = sem("pe_s", U4, "pe")
    pe_u = sem("pe_u", U4, "pe")
    pe_x = sem("pe_x", U4, "pe")
    pe_g = sem("pe_g", UNITS * 8, "pe")
    pe_f = sem("pe_f", 2 * GB, "pe")
    a_i = sem("a_i", 2 * GB, "act")
    a_q = sem("a_q", U4, "act")
    a_e = sem("a_e", U4, "act")
    a_g = sem("a_g", UNITS * 6, "act")
    a_h = sem("a_h", (UNITS - 2) * 2, "act")
    a_hi = sem("a_hi", UNITS * DC, "act")
    d_n = sem("d_n", 2 * GB, "dve")
    d_ss = sem("d_ss", UNITS - 2, "dve")
    d_t = sem("d_t3", U4, "dve")
    d_m = sem("d_m3", 2 * U4, "dve")
    d_e = sem("d_e", 3 * U4, "dve")
    d_u = sem("d_u", 3 * U4, "dve")
    d_xh, d_x = sem("d_xh", U4, "dve"), sem("d_x", U4, "dve")
    d_g = sem("d_g", UNITS * 8, "dve")
    d_h = sem("d_h", UNITS * 2, "dve")
    d_f = sem("d_f3", 2 * GB, "dve")
    d_l = sem("d_l", 2 * (2 * GB), "dve")
    p_l = sem("p_l", 2 * 7, "pool")
    p_lo = sem("p_lo", UNITS * DC, "pool")
    p_k = sem("p_k", 2, "pool")
    p_r = sem("p_r", UNITS - 2, "pool")
    p_d = sem("p_d", UNITS * 2, "pool")

    ATT = [("q", 0), ("q", 1), ("SS", 0), "g", ("T", 0), ("T", 1), ("R", 0), ("q", 2), ("q", 3), "g", ("T", 2), ("S", 0),
           ("R", 1), ("T", 3), ("S", 1), "g", ("S", 2), ("N", 0), "g", ("S", 3), ("N", 1), ("U", 0), "g", ("N", 2), ("X", 0),
           ("U", 1), "g", ("N", 3), ("X", 1), ("U", 2), ("H", 0), ("U", 3), ("H", 1), ("X", 2), ("h", 0), ("X", 3), ("h", 1)]
    LAST = ["g", ("R", 0), "g", ("R", 1), "g", "g", "g", "g", ("H", 0), ("H", 1)]
    STEP = [("hn", 0), ("hn", 1), ("r", 0), ("r", 1), ("xn", 0), ("z", 0), ("xn", 1), ("z", 1)]
    AT_A = {("r", 0): 1, ("r", 1): 2, ("xn", 0): 3, ("z", 0): 4, ("xn", 1): 5, ("z", 1): 6}

    ONCE = {("S", 1): [("slots", 1, 1)]}

    def schedule():
        out = [("rms", 0, 0), ("slots", 0, 0), ("rms", 1, 1)]
        for n in range(UNITS + 1):
            gru = list(range(2, len(STEP)))
            for s in (ATT if n < UNITS else LAST):
                if s == "g":
                    if n:
                        out.append(("g", gru.pop(0), n - 1))
                elif s[0] in ("H", "R"):
                    if n:
                        out.append((*s, n - 1))
                elif s[0] == "SS":
                    if n >= 2:
                        out.append((*s, n))
                elif s[0] == "h":
                    out.append(("g", s[1], n))
                else:
                    out.append((*s, n))
                if n == 0:
                    out += ONCE.get(s, [])
            if n >= UNITS - 1:
                out.append(("fin", (n - 1) % 2, n - 1))
        return out
    SCHEDULE = schedule()

    def iterations(eng, owner, do):
        prime(eng, owner)
        with eng.Fori(0, NG // 2) as K:
            for what, i, n in SCHEDULE:
                do(what, i, n, K)

    block = ctx.enter_context(nc.Block())

    @block.sync
    def _(sp):
        prime(sp, "sp")

        def load(K, g):
            for i in range(GB):
                context_loads(sp, a, (2 * K + g) * GB + i, cx[g], cT[g], i, c_in[g])

        load(0, 1)
        for e in range(E1):
            sp.dma_start(t["down"][:, e], a["down"][e].rearrange("(c p) n -> p c n", p=P)).then_inc(t["down_in"].sem, 16)
        sp.wait_ge(blanked.sem, 2)
        sp.dma_start(t["rows_by_place"].rearrange("(t p) d -> p t d", p=P),
                     blank[:, :].unsqueeze(1).to_broadcast([P, MT, PLACE_ROW])).then_inc(t["zeroed"].sem, 16)
        with sp.Fori(1, NG // 2) as K:
            for g in range(2):
                sp.wait_ge(*at(pe_u, K, -(1 - g) * GB))
                sp.sem_inc(apart.sem, 1)
                load(K, g)

    @block.tensor
    def _(pe):
        def do(what, i, n, K):
            g, r = n % 2, n // 2
            k = n * GB + i + 1
            if what == "slots":
                for j in range(GB):
                    b = g * GB + j
                    pe.wait_ge(*at(d_n, K, b + 1))
                    if b >= 2:
                        pe.wait_ge(*at(a_i, K, b - 1))
                    else:
                        pe.wait_ge(*at(d_f, K, 0))
                    for c in range(DC):
                        m = pe.transpose(pu[:, b % 2, c * S:(c + 1) * S], sl[:, b % 2, c * P:(c + 1) * P], ident[:S, :S])
                    m.then_inc(pe_i.sem, 1)
            elif what == "SS":
                pe.wait_ge(*at(a_h, K, 2 * n - 2))
                pe.wait_ge(*at(d_t, K, n * GB))
                for j in range(GB):
                    for c in range(DC):
                        m = pe.matmul(pa[:S, 0, D + DC * S + j:D + DC * S + j + 1], hsq[:, c, j * S:(j + 1) * S], ones[:, 0:1],
                                      start=(c == 0), stop=(c == DC - 1))
                m.then_inc(pe_ss.sem, 1)
            elif what == "q":
                if i == 0:
                    pe.wait_ge(*at(d_t, K, n * GB - 1))
                    if r == 0:
                        pe.wait_ge(*at(a_i, K, (g + 1) * GB))
                    else:
                        pe.wait_ge(*at(d_h, K, 2 * (n - 1)))
                elif i == 1:
                    pe.wait_ge(*at(d_t, K, n * GB))
                else:
                    pe.wait_ge(*at(d_t, K, k - 2))
                for c in range(DC):
                    m = pe.matmul(pa[:S, i % 2, 0:D], hT[g][:, c, i * S:(i + 1) * S], wqk[:, c, :],
                                  start=(c == 0), stop=(c == DC - 1))
                m.then_inc(pe_q.sem, 1)
            elif what == "T":
                pe.wait_ge(*at(a_q, K, k))
                for c in range(DC):
                    m = pe.transpose(pa[:, i % 2, D + c * S:D + (c + 1) * S], qs[:, i % 2, c * P:(c + 1) * P], ident[:S, :S])
                m.then_inc(pe_t.sem, 1)
            elif what == "S":
                if i == 0 and r == 0:
                    pe.wait_ge(*at(c_in[g], K, c_in[g].per))
                pe.wait_ge(*at(d_t, K, k))
                pe.wait_ge(*at(a_e, K, k - 2))
                for kt in range(KT):
                    for c in range(DC):
                        m = pe.matmul(pc[:KP, i % 2, kt * S:(kt + 1) * S], cT[g][:, i, c, kt * KP:(kt + 1) * KP],
                                      qT[:, i % 2, c, :], start=(c == 0), stop=(c == DC - 1))
                m.then_inc(pe_s.sem, 1)
            elif what == "U":
                pe.wait_ge(*at(d_e, K, 3 * k))
                if i == 0 and r == 0:
                    pe.wait_ge(*at(p_k, K, g + 1))
                if n == 0 and i == 0:
                    pe.wait_ge(*at(a_i, K, 2 * GB))
                pe.wait_ge(*at(d_x, K, k - 2))
                for kt in range(KT):
                    m = pe.matmul(pu[:S, i % 2, 0:D + 1], e[:, i, kt, :], cx[g][:, i, kt, :],
                                  start=(kt == 0), stop=(kt == KT - 1))
                m.then_inc(pe_u.sem, 1)
            elif what == "X":
                pe.wait_ge(*at(d_u, K, 3 * k))
                for c in range(DC):
                    m = pe.transpose(pu[:, i % 2, c * S:(c + 1) * S],
                                     un[:, i % 2, c * P:(c + 1) * P], ident[:S, :S])
                m.then_inc(pe_x.sem, 1)
            elif what == "g":
                kind, c = STEP[i]
                out = pg[:, i % 2, 0:GN]
                if i == 0:
                    pe.wait_ge(*at(d_g, K, 8 * n - 2))
                elif i == 1:
                    pe.wait_ge(*at(a_g, K, 6 * n))
                elif i == 2:
                    pe.wait_ge(*at(d_g, K, 8 * n + 1))
                    pe.wait_ge(*at(d_x, K, (n + 1) * GB))
                elif i == 3:
                    pe.wait_ge(*at(d_g, K, 8 * n + 2))
                elif i == 4:
                    pe.wait_ge(*at(a_g, K, 6 * n + 1))
                elif i == 5:
                    pe.wait_ge(*at(a_g, K, 6 * n + 2))
                elif i == 6:
                    pe.wait_ge(*at(d_g, K, 8 * n + 5))
                else:
                    pe.wait_ge(*at(a_g, K, 6 * n + 4))
                col = {"r": 0, "z": D, "hn": 2 * D, "xn": 2 * D}[kind] + c * P
                if i == 0:
                    pe.wait_ge(*at(p_lo, K, DC * (n + 1)))
                sums = ([(wg, us[g])] if kind != "hn" else []) + ([(wh, hs[g])] if kind != "xn" else [])
                terms = [(w[x], s[y], q) for w, s in sums for q in range(DC) for x, y in ((0, 0), (0, 1), (1, 0))]
                for j, (w, s, q) in enumerate(terms):
                    m = pe.matmul(out, w[:, q, col:col + P], s[:, q, :], start=(j == 0), stop=(j == len(terms) - 1))
                m.then_inc(pe_g.sem, 1)
            elif what == "fin":
                for j in range(GB):
                    b = g * GB + j
                    pe.wait_ge(*at(d_h, K, 2 * (n + 1)))
                    if b < 2:
                        pe.wait_ge(*at(a_e, K, U4))
                    else:
                        pe.wait_ge(*at(d_f, K, b - 1))
                    if g == 0 and j < 2:
                        pe.wait_ge(*at(d_u, K, 3 * U4))
                        pe.wait_ge(*at(d_x, K, U4))
                    for c in range(DC):
                        m = pe.transpose(pu[:S, b % 2, c * P:(c + 1) * P], hT[g][:, c, j * S:(j + 1) * S], ident[:, :])
                    m.then_inc(pe_f.sem, 1)

        pe.wait_ge(made.sem, 1)
        iterations(pe, "pe", do)

    @block.scalar
    def _(act):
        def do(what, i, n, K):
            g, r = n % 2, n // 2
            k = n * GB + i + 1
            if what == "slots":
                for j in range(GB):
                    act.wait_ge(*at(pe_i, K, g * GB + j + 1))
                    act.wait_ge(*at(pe_f, K, 0))
                    act.activation(hT[g][:, :, j * S:(j + 1) * S],
                                   pu[:, j % 2, 0:DC * S].rearrange("p (c s) -> p c s", c=DC), ACT.Copy).then_inc(a_i.sem, 1)
                act.wait_ge(*at(a_i, K, (g + 1) * GB))
                for c in range(DC):
                    high(g, c, K)
            elif what == "q":
                act.wait_ge(*at(pe_q, K, k))
                if r:
                    act.wait_ge(*at(p_r, K, n - 1))
                    scale = rinv[:, i:i + 1]
                else:
                    scale = roots[:, 1, bass.ds((2 * K + g) * GB + i, 1)]
                act.wait_ge(*at(pe_t, K, k - 2))
                act.activation(qs[:, i % 2, :], pa[:S, i % 2, 0:D], ACT.Copy, scale=scale).then_inc(a_q.sem, 1)
            elif what == "S":
                act.wait_ge(*at(d_m, K, 2 * k))
                act.wait_ge(*at(pe_u, K, k - GB))
                for kt in range(KT):
                    m = act.activation(e[:, i, kt, :], pc[:KP, i % 2, kt * S:(kt + 1) * S], ACT.Exp,
                                       scale=kr[g][:, i * KT + kt:i * KT + kt + 1], bias=nb[:, i, kt:kt + 1],
                                       accum_out=es[:, i, kt:kt + 1])
                m.then_inc(a_e.sem, 1)
            elif what == "g" and STEP[i] in AT_A:
                kind, c = STEP[i]
                ps = pg[:, i % 2, 0:GN]
                if kind == "xn":
                    act.wait_ge(*at(d_g, K, 8 * n + 5 + c))
                    act.wait_ge(*at(d_h, K, 2 * n))
                    act.activation(nn[:, c, :], hh[:, c, :], ACT.Tanh, bias=bih[:, 4 + c:5 + c]).then_inc(a_g.sem, 1)
                else:
                    act.wait_ge(*at(pe_g, K, 8 * n + i + 1))
                    dst, col = (tr, c) if kind == "r" else (tz, 2 + c)
                    act.wait_ge(*at(d_h, K, 2 * n))
                    act.activation(dst[:, c, :], ps, ACT.Tanh, scale=0.5, bias=brz[:, col:col + 1]).then_inc(a_g.sem, 1)
            elif what == "H" and n + 2 < UNITS:
                act.wait_ge(*at(d_h, K, 2 * n + i + 1))
                square(n + 2, i, K)
                high(n + 2, i, K)

        def high(n, c, K):
            act.wait_ge(*at(pe_g, K, 8 * (n - 1)))
            act.activation(hs[n % 2][0][:, c, :], hT[n % 2][:, c, :], ACT.Copy).then_inc(a_hi.sem, 1)

        def square(n, c, K):
            act.wait_ge(*at(pe_ss, K, n - 2))
            act.activation(hsq[:, c, :], hT[n % 2][:, c, :], ACT.Square).then_inc(a_h.sem, 1)

        iterations(act, "act", do)

    @block.vector
    def _(dve):
        def do(what, i, n, K):
            g, r = n % 2, n // 2
            k = n * GB + i + 1
            if what == "slots":
                for j in range(GB):
                    b, xb = g * GB + j, (2 * K + g) * GB + j
                    dve.wait_ge(*at(pe_i, K, b - 1))
                    dve.tensor_scalar(sl[:, b % 2, :], x_all[:, xb, :], mean[:, bass.ds(xb, 1)], roots[:, 0, bass.ds(xb, 1)],
                                      ALU.subtract, ALU.mult).then_inc(d_n.sem, 1)
            elif what == "SS":
                dve.wait_ge(*at(pe_ss, K, n - 1))
                dve.wait_ge(*at(p_r, K, n - 2))
                dve.tensor_scalar(ms[:], pa[:S, 0, D + DC * S:D + DC * S + GB], 1.0 / D, RMS_EPS, ALU.mult, ALU.add).then_inc(d_ss.sem, 1)
            elif what == "T":
                dve.wait_ge(*at(pe_t, K, k))
                dve.wait_ge(*at(pe_s, K, k - 2))
                dve.tensor_copy(qT[:, i % 2].rearrange("p c s -> p (c s)"), pa[:, i % 2, D:D + DC * S]).then_inc(d_t.sem, 1)
            elif what == "S":
                dve.wait_ge(*at(pe_s, K, k))
                if i == 0 and r == 0:
                    dve.wait_ge(*at(p_k, K, g + 1))
                dve.wait_ge(*at(a_e, K, k - GB))
                dve.tensor_reduce(nm[:, i, :], pc[:KP, i % 2, 0:KT * S].rearrange("p (t s) -> p t s", t=KT),
                                  AX.X, ALU.max, negate=True).then_inc(d_m.sem, 1)
                dve.wait_ge(*at(d_m, K, 2 * k - 1))
                dve.tensor_tensor(nb[:, i, :], nm[:, i, :], kr[g][:, i * KT:(i + 1) * KT], ALU.mult).then_inc(d_m.sem, 1)
            elif what == "N":
                dve.wait_ge(*at(a_e, K, k))
                dve.reciprocal(er[:, i, :], es[:, i, :]).then_inc(d_e.sem, 1)
                dve.wait_ge(*at(d_e, K, 3 * k - 2))
                dve.tensor_tensor(er[:, i, :], er[:, i, :], kr[g][:, i * KT:(i + 1) * KT], ALU.mult).then_inc(d_e.sem, 1)
                dve.wait_ge(*at(d_e, K, 3 * k - 1))
                dve.tensor_tensor(e[:, i], e[:, i], er[:, i, :].unsqueeze(2).to_broadcast([KP, KT, S]),
                                  ALU.mult).then_inc(d_e.sem, 1)
            elif what == "U":
                dve.wait_ge(*at(pe_u, K, k))
                dve.tensor_scalar(uk[:, i % 2, 0:1], pu[:S, i % 2, D:D + 1], SLOT_EPS, None, ALU.add).then_inc(d_u.sem, 1)
                dve.wait_ge(*at(d_u, K, 3 * k - 2))
                dve.reciprocal(uk[:, i % 2, 1:2], uk[:, i % 2, 0:1]).then_inc(d_u.sem, 1)
                dve.wait_ge(*at(d_u, K, 3 * k - 1))
                dve.wait_ge(*at(pe_x, K, k - 2))
                dve.tensor_scalar(un[:, i % 2, :], pu[:S, i % 2, 0:D], uk[:, i % 2, 1:2], None, ALU.mult).then_inc(d_u.sem, 1)
            elif what == "X":
                dve.wait_ge(*at(pe_x, K, k))
                if i == 0:
                    dve.wait_ge(*at(pe_g, K, 8 * (n - 1)))
                full = pu[:, i % 2, 0:DC * S].rearrange("p (c s) -> p c s", c=DC)
                hi, lo = (part[:, :, i * S:(i + 1) * S] for part in us[g])
                dve.tensor_copy(hi, full).then_inc(d_xh.sem, 1)
                dve.wait_ge(*at(d_xh, K, k))
                dve.tensor_tensor(lo, full, hi.bitcast(F32), ALU.subtract).then_inc(d_x.sem, 1)
            elif what == "g":
                kind, c = STEP[i]
                ps = pg[:, i % 2, 0:GN]
                if kind == "hn":
                    dve.wait_ge(*at(pe_g, K, 8 * n + i + 1))
                    dve.tensor_scalar(hh[:, c, :], ps, bhh[:, 4 + c:5 + c], 0.5, ALU.add, ALU.mult).then_inc(d_g.sem, 1)
                elif kind == "xn":
                    dve.wait_ge(*at(pe_g, K, 8 * n + i + 1))
                    dve.wait_ge(*at(d_g, K, 8 * n + 3 + c))
                    dve.wait_ge(*at(a_g, K, 6 * n))
                    dve.tensor_tensor(hh[:, c, :], ps, hh[:, c, :], ALU.add).then_inc(d_g.sem, 1)
            elif what == "R":
                dve.wait_ge(*at(d_g, K, 8 * n + i + 1))
                dve.wait_ge(*at(a_g, K, 6 * n + 1 + i))
                dve.scalar_tensor_tensor(out=hh[:, i, :], in0=tr[:, i, :], scalar=1.0, in1=hh[:, i, :],
                                         op0=ALU.add, op1=ALU.mult).then_inc(d_g.sem, 1)
            elif what == "H":
                state(n, i, K, hT[g])
            elif what == "fin":
                for j in range(GB):
                    x = x_all[:, (2 * K + g) * GB + j, :]
                    dve.wait_ge(*at(pe_f, K, g * GB + j + 1))
                    dve.tensor_tensor(x, pu[:S, j % 2, 0:D], x, ALU.add).then_inc(d_f.sem, 1)
                for j in range(GB):
                    dve.wait_ge(*at(d_f, K, g * GB + j + 1))
                    dve.sem_inc(apart.sem, 1)
                    dve.bn_stats(st[:, j, :], x_all[:, (2 * K + g) * GB + j, :]).then_inc(d_l.sem, 1)
                dve.wait_ge(*at(p_l, K, 7 * g))
                for j in range(GB):
                    dve.wait_ge(*at(d_l, K, g * 2 * GB + j + 1))
                    dve.sem_inc(apart.sem, 1)
                    dve.bn_aggr(mv[:, j, :], st[:, j, :]).then_inc(d_l.sem, 1)

        def state(n, c, K, new):
            dve.wait_ge(*at(p_d, K, 2 * n + c + 1))
            dve.wait_ge(*at(a_g, K, 6 * n + 4 + 2 * c))
            dve.scalar_tensor_tensor(out=tz[:, c, :], in0=tz[:, c, :], scalar=1.0, in1=df[:, c, :],
                                     op0=ALU.add, op1=ALU.mult).then_inc(d_g.sem, 1)
            dve.wait_ge(*at(d_g, K, 8 * n + 7 + c))
            dve.wait_ge(*at(p_lo, K, DC * (n + 1)))
            dve.scalar_tensor_tensor(out=new[:, c, :], in0=tz[:, c, :], scalar=0.5, in1=nn[:, c, :],
                                     op0=ALU.mult, op1=ALU.add).then_inc(d_h.sem, 1)

        iterations(dve, "dve", do)

    @block.gpsimd
    def _(pool):
        def do(what, i, n, K):
            g, r = n % 2, n // 2
            old = hT[g]
            if what == "fin":
                pool.wait_ge(*at(d_l, K, (g + 1) * 2 * GB))
                norm_roots(pool, p_l, lambda k: at(p_l, K, 7 * g + k), apart, mv, mhalf[:S, 0:1].to_broadcast([S, GB]), tmp,
                           mean, roots, bass.ds((2 * K + g) * GB, GB))
            elif what == "slots":
                for c in range(DC):
                    low(g, c, K)
            elif what == "H" and n + 2 < UNITS:
                low(n + 2, i, K)
            elif what == "rms":
                pool.wait_ge(*at(pe_u, K, -(1 - g) * GB))
                at_g = bass.ds((2 * K + g) * GB * KT, GB * KT)
                pool.sem_inc(apart.sem, 1)
                pool.tensor_copy(kr[g][:], row_root[:, at_g])
                pool.tensor_copy(cx[g][:, :, :, D], row_rms[:, at_g]
                                 .rearrange("p (i t) -> p i t", i=GB)).then_inc(p_k.sem, 1)
            elif what == "SS":
                pool.wait_ge(*at(d_ss, K, n - 1))
                pool.wait_ge(*at(a_q, K, n * GB))
                pool.tensor_tensor(rinv[:], ms[:], mhalf[:S, 0:1].to_broadcast([S, GB]), ALU.pow).then_inc(p_r.sem, 1)
            elif what == "g" and i in (5, 7):
                c = (i - 5) // 2
                pool.wait_ge(*at(a_g, K, 6 * n + 3 + 2 * c))
                pool.wait_ge(*at(d_g, K, 8 * n - 1 + c))
                pool.tensor_tensor(df[:, c, :], old[:, c, :], nn[:, c, :], ALU.subtract).then_inc(p_d.sem, 1)

        def low(n, c, K):
            pool.wait_ge(*at(a_hi, K, DC * n + c + 1))
            hi, lo = hs[n % 2]
            pool.tensor_tensor(lo[:, c, :], hT[n % 2][:, c, :], hi[:, c, :].bitcast(F32), ALU.subtract).then_inc(p_lo.sem, 1)

        pool.memset(blank[:, 0:2 * D], 0.0).then_inc(blanked.sem, 1)
        pool.memset(blank[:, 2 * D:], 1.0).then_inc(blanked.sem, 1)
        pool.memset(mhalf[:], -0.5)
        pool.memset(ones[:], 1.0).then_inc(made.sem, 1)
        pool.wait_ge(made.sem, 1)
        iterations(pool, "pool", do)



def phase_4(nc, ctx, a, t, out):
    def sb(name, shape, dt=F32):
        return ctx.enter_context(nc.sbuf_tensor("e_" + name, shape, dt))

    def psum(name, shape):
        return ctx.enter_context(nc.psum_tensor("e_" + name, shape, F32))

    def sem(name, per=1):
        return Sig(ctx.enter_context(nc.semaphore("e_" + name)), per)

    x_all, ident = t["x_all"], t["ident"]
    HID2 = 2 * F1
    FC = F1 // P
    BE = B * E1
    RW = PLACE_ROW
    RING = 4

    up = sb("up", [P, E1, DC, HID2])
    down, mean, roots = t["down"], t["mean"], t["roots"]
    scale = sb("scale4", [S, D])
    cT1 = sb("cT1", [P, DC, E1])
    ny, csq = sb("ny", [S, E1]), sb("csq4", [P, DC, E1])
    onesf, onesb = sb("onesf", [P, S]), sb("onesb", [S, S], BF16)
    before = sb("before", [S, S], BF16)
    rank_e = sb("rank_e", [S, E1])
    less = sb("less", [S, E1, E1])
    kk = sb("kk", [S, E1, B * S // P])
    tj = sb("tj", [S, MT, E1])
    xl, xn = sb("xl", [S, 2, D]), sb("xn4", [S, 2, D])
    rows = sb("e_rows", [S, B, RW])
    sq = sb("sq4", [S, D])
    nx = sb("nx", [S, B])
    xnT = sb("xnT4", [P, 2, DC, S])
    dots = sb("dots", [S, B, E1])
    dist, cand, oh = sb("dist", [S, B, E1]), sb("cand", [S, B, E1]), sb("oh", [S, B, E1])
    best = sb("best", [S, 2, B])
    ohb = sb("ohb", [S, B, E1], BF16)
    cum = sb("cum", [S, 2, B, E1])
    cnt = sb("cnt", [S, B, E1])
    rank = sb("rank4", [S, B, E1])
    more = sb("more", [S, E1, B * S // P])
    tiles, start, end, first = (sb(n, [S, E1]) for n in ("tiles", "start", "end", "first"))
    lt = sb("lt", [S, E1, E1])
    passed = sb("passed", [S, MT, E1])
    texp = sb("texp", [S, MT])
    texp_i = sb("texp_i", [S, MT], I32)
    place, place_i = sb("place", [S, B]), sb("place_i", [S, B], U32)
    xt, xT = sb("xt", [P, RING, RW]), sb("xT", [P, 2, DC, P])
    th, u = sb("th", [P, 2, F1]), sb("u", [P, 2, F1])
    uT, ysb = sb("uT4", [P, 2, FC, P]), sb("ysb", [P, 2, D])
    xs = t["rows_by_place"]

    pt, pd = psum("pt4", [P, 512]), psum("pd4", [P, 512])
    ph = psum("ph4", [P, 2, 2, 512])
    pz, py = psum("pz4", [P, 512]), psum("py4", [P, 512])
    xbank = [pt, py]

    s_in, u_in = sem("s_in"), sem("u_in")
    made = sem("made")
    apart = sem("apart")
    chosen = sem("chosen")
    lnd, nrm = sem("lnd"), sem("nrm")
    kept, nxd, xnk = sem("kept"), sem("nxd"), sem("xnk")
    tpd, tup, dotd, dup = sem("tpd"), sem("tup"), sem("dotd"), sem("dup")
    v = sem("v")
    routed_pe = sem("routed_pe")
    scattered = sem("scattered")
    x_in = [sem(f"x_in{q}") for q in range(RING)]
    y_out = [sem(f"y_out{q}") for q in range(RING)]
    t_pe, t_up, up_a, up_g, thd, gated, z_pe, z_up, y_pe, y_up = (
        sem(n) for n in ("t_pe", "t_up", "up_a", "up_g", "thd", "gated", "z_pe", "z_up", "y_pe", "y_up"))

    block = ctx.enter_context(nc.Block())

    def tiles_loop(eng, body):
        for q in range(RING):
            body(q, 0, q)
        with eng.Fori(1, (MT - 1) // RING) as i:
            for q in range(RING):
                body(RING * i + q, i, q)
        body(MT - 1, (MT - 1) // RING, 0)

    def is_early(j, n):
        return isinstance(j, int) and j < n

    def is_last(j, n=1):
        return isinstance(j, int) and j >= MT - n

    @block.sync
    def _(sp):
        sp.dma_start(scale[:], a["scale"].to_broadcast([S, D])).then_inc(s_in.sem, 16)
        sp.dma_start(cT1[:], a["centT"].rearrange("(c p) e -> p c e", p=P)).then_inc(s_in.sem, 16)
        for e in range(E1):
            sp.dma_start(up[:, e], a["up"][e].rearrange("(c p) n -> p c n", p=P)).then_inc(u_in.sem, 16)
        sp.wait_ge(scattered.sem, 16 * B)

        def load(j, q):
            sp.dma_start(xt[:, q, :], xs[bass.ts(j, P), :]).then_inc(x_in[q].sem, 16)

        for q in range(RING):
            load(q, q)

        def body(j, i, q):
            if not is_last(j, RING):
                sp.wait_ge(y_out[q].sem, 16 * (i + 1))
                sp.sem_inc(apart.sem, 1)
                load(j + RING, q)

        for q in range(RING):
            body(q, 0, q)
        with sp.Fori(1, (MT - 1) // RING - 1) as i:
            for q in range(RING):
                body(RING * i + q, i, q)
        body(MT - 1 - RING, (MT - 1) // RING - 1, 0)
        for q in range(RING):
            sp.wait_ge(y_out[q].sem, 16 * ((MT - 1 - q) // RING + 1))

    @block.tensor
    def _(pe):
        pe.wait_ge(v.sem, 1)
        pe.wait_ge(made.sem, 10)
        for c in range(DC):
            m = pe.matmul(pz[:S, 0:E1], onesf[:, :], csq[:, c, :], start=(c == 0), stop=(c == DC - 1))
        m.then_inc(routed_pe.sem, 1)

        def turn_x(b, par):
            pe.wait_ge(nrm.sem, b + 3)
            pe.wait_ge(tup.sem, b + 1)
            for c in range(DC):
                m = pe.transpose(xbank[par][:, c * S:(c + 1) * S], xn[:, par, c * P:(c + 1) * P], ident[:S, :S])
            m.then_inc(tpd.sem, 1)

        def dot(b, par):
            pe.wait_ge(tup.sem, b + 3)
            pe.wait_ge(dup.sem, b + 2)
            for c in range(DC):
                m = pe.matmul(pd[:S, 0:E1], xnT[:, par, c, :], cT1[:, c, :], start=(c == 0), stop=(c == DC - 1))
            m.then_inc(dotd.sem, 1)

        turn_x(0, 0)
        turn_x(1, 1)
        dot(0, 0)
        with pe.Fori(1, B // 2) as j:
            turn_x(2 * j, 0)
            dot(2 * j - 1, 1)
            turn_x(2 * j + 1, 1)
            dot(2 * j, 0)
        dot(B - 1, 1)
        pe.wait_ge(v.sem, 8)
        pe.wait_ge(dup.sem, B + 2)
        pe.matmul(pd[:S, 0:BE], before[:, :], ohb[:, :, :].rearrange("s b e -> s (b e)"), start=True, stop=True)
        pe.matmul(pz[:S, 0:BE], onesb[:, :], ohb[:, :, :].rearrange("s b e -> s (b e)"), start=True, stop=True).then_inc(routed_pe.sem, 1)

        def turn(j, i, q, first):
            pe.wait_ge(x_in[q].sem, 16 * (i + 1))
            if not first:
                pe.wait_ge(t_up.sem, j)
            else:
                pe.wait_ge(dotd.sem, B)
            for c in range(DC):
                m = pe.transpose(pt[:, c * P:(c + 1) * P], xt[:, q, c * P:(c + 1) * P], ident[:, :])
            m.then_inc(t_pe.sem, 1)

        def half(j, par, h, e, sig):
            for c in range(DC):
                m = pe.matmul(ph[:, par, h, :], xT[:, par, c, :], up[:, e, c, h * F1:(h + 1) * F1],
                              start=(c == 0), stop=(c == DC - 1))
            m.then_inc(sig.sem, 1)

        def turn_u(j, par, first):
            pe.wait_ge(gated.sem, j + 1)
            if not first:
                pe.wait_ge(z_up.sem, j)
            for f in range(FC):
                m = pe.transpose(pz[:, f * P:(f + 1) * P], u[:, par, f * P:(f + 1) * P], ident[:, :])
            m.then_inc(z_pe.sem, 1)

        def second(j, par, first, e):
            pe.wait_ge(z_up.sem, j + 1)
            if not first:
                pe.wait_ge(y_up.sem, j)
            for f in range(FC):
                m = pe.matmul(py[:, 0:D], uT[:, par, f, :], down[:, e, f, :], start=(f == 0), stop=(f == FC - 1))
            m.then_inc(y_pe.sem, 1)

        def expert(j):
            return pe.value_load(texp_i[0:1, bass.ds(j, 1)], min_val=0, max_val=E1 - 1)

        pe.wait_ge(v.sem, 23)
        turn(0, 0, 0, True)
        pe.wait_ge(u_in.sem, 16 * E1)
        pe.wait_ge(t["down_in"].sem, 16 * E1)

        def body(j, i, q):
            par = q % 2
            e = expert(j)
            pe.wait_ge(t_up.sem, j + 1)
            if not is_early(j, 2):
                pe.wait_ge(gated.sem, j - 1)
            half(j, par, 1, e, up_g)
            if not is_early(j, 1):
                turn_u(j - 1, 1 - par, is_early(j, 2))
            half(j, par, 0, e, up_a)
            if not is_last(j):
                turn(j + 1, i + (q + 1) // RING, (q + 1) % RING, False)
            if not is_early(j, 1):
                second(j - 1, 1 - par, is_early(j, 2), expert(j - 1))

        tiles_loop(pe, body)
        turn_u(MT - 1, 0, False)
        second(MT - 1, 0, False, expert(MT - 1))

    @block.scalar
    def _(act):
        act.sem_inc(tup.sem, 2)
        act.sem_inc(nxd.sem, 2)
        act.sem_inc(xnk.sem, 2)

        def turned_x(b, par, early):
            act.wait_ge(nrm.sem, b + 3)
            act.wait_ge(nxd.sem, b + 2)
            act.activation(sq[:], xn[:, par, :], ACT.Square, accum_out=nx[:, bass.ds(b, 1)]).then_inc(nxd.sem, 1)
            act.wait_ge(tpd.sem, b + 1)
            if not early:
                act.wait_ge(dotd.sem, b - 1)
            act.activation(xnT[:, par].rearrange("p c s -> p (c s)"), xbank[par][:, 0:DC * S], ACT.Copy).then_inc(tup.sem, 1)
            act.activation(rows[:, b, 0:D], xn[:, par, :], ACT.Copy).then_inc(xnk.sem, 1)

        turned_x(0, 0, True)
        turned_x(1, 1, True)
        with act.Fori(1, B // 2) as j:
            turned_x(2 * j, 0, False)
            turned_x(2 * j + 1, 1, False)

        def body(j, i, q):
            par = q % 2
            act.wait_ge(up_g.sem, j + 1)
            if not is_early(j, 2):
                act.wait_ge(gated.sem, j - 1)
            act.activation(th[:, par, :], ph[:, par, 1, :], ACT.Tanh, scale=0.5).then_inc(thd.sem, 1)
            if not is_early(j, 1):
                up_z(j - 1, 1 - par)

        def up_z(j, par):
            act.wait_ge(z_pe.sem, j + 1)
            act.activation(uT[:, par].rearrange("p f s -> p (f s)"), pz[:, :], ACT.Copy).then_inc(z_up.sem, 1)

        tiles_loop(act, body)
        up_z(MT - 1, 0)

    @block.vector
    def _(dve):
        dve.wait_ge(s_in.sem, 32)
        dve.tensor_tensor(csq[:], cT1[:], cT1[:], ALU.mult).then_inc(v.sem, 1)
        dve.sem_inc(lnd.sem, 2)
        dve.sem_inc(nrm.sem, 2)
        dve.sem_inc(dup.sem, 2)

        def dot_up(b):
            dve.wait_ge(dotd.sem, b + 1)
            dve.tensor_copy(dots[:, b, :], pd[:S, 0:E1]).then_inc(dup.sem, 1)

        def norm(b, par):
            dve.wait_ge(kept.sem, b + 1)
            dve.tensor_scalar(xl[:, par, :], x_all[:, b, :], mean[:, bass.ds(b, 1)], roots[:, 0, bass.ds(b, 1)],
                              ALU.subtract, ALU.mult).then_inc(lnd.sem, 1)
            dve.wait_ge(lnd.sem, b + 3)
            dve.wait_ge(xnk.sem, b + 1)
            dve.scalar_tensor_tensor(out=xn[:, par, :], in0=xl[:, par, :], scalar=roots[:, 1, bass.ds(b, 1)], in1=scale[:],
                                     op0=ALU.mult, op1=ALU.mult).then_inc(nrm.sem, 1)

        norm(0, 0)
        norm(1, 1)
        with dve.Fori(1, B // 2) as j:
            for par in range(2):
                b = 2 * j + par
                norm(b, par)
                dot_up(b - 2)
        dot_up(B - 2)
        dot_up(B - 1)

        n = [1]

        def chain(ins):
            n[0] += 1
            ins.then_inc(v.sem, 1)
            dve.wait_ge(v.sem, n[0])

        dve.wait_ge(routed_pe.sem, 1)
        chain(dve.tensor_copy(ny[:], pz[:S, 0:E1]))
        dve.wait_ge(nxd.sem, B + 2)
        dve.wait_ge(dup.sem, B + 2)
        chain(dve.tensor_tensor(dist[:], nx[:, :].unsqueeze(2).to_broadcast([S, B, E1]),
                                ny[:, :].unsqueeze(1).to_broadcast([S, B, E1]), ALU.add))
        chain(dve.scalar_tensor_tensor(out=dist[:], in0=dots[:], scalar=2.0, in1=dist[:], op0=ALU.mult, op1=ALU.subtract))
        chain(dve.tensor_reduce(best[:, 0, :], dist[:], AX.X, ALU.max))
        chain(dve.tensor_tensor(cand[:], dist[:], best[:, 0, :].unsqueeze(2).to_broadcast([S, B, E1]), ALU.is_ge))
        chain(dve.tensor_tensor(cand[:], cand[:], rank_e[:, :].unsqueeze(1).to_broadcast([S, B, E1]), ALU.mult))
        dve.tensor_reduce(best[:, 1, :], cand[:], AX.X, ALU.max).then_inc(chosen.sem, 1)
        dve.wait_ge(chosen.sem, 1)
        chain(dve.tensor_tensor(ohb[:], cand[:], best[:, 1, :].unsqueeze(2).to_broadcast([S, B, E1]), ALU.is_equal))
        chain(dve.tensor_copy(oh[:], ohb[:]))
        dve.wait_ge(routed_pe.sem, 2)
        chain(dve.tensor_copy(cnt[:], pz[:S, 0:BE].rearrange("s (b e) -> s b e", b=B)))
        src = cnt
        for k in range(4):
            w, dst = 1 << k, cum[:, k % 2]
            prev = src[:, :, :] if k == 0 else src
            dve.tensor_copy(dst[:, 0:w, :], prev[:, 0:w, :])
            chain(dve.tensor_tensor(dst[:, w:B, :], prev[:, w:B, :], prev[:, 0:B - w, :], ALU.add))
            src = dst
        total = src[:, B - 1, :]
        chain(dve.tensor_tensor(more[:], total.unsqueeze(2).to_broadcast([S, E1, B * S // P]), kk[:], ALU.is_gt))
        chain(dve.tensor_reduce(tiles[:], more[:], AX.X, ALU.add))
        chain(dve.tensor_tensor(lt[:], tiles[:, :].unsqueeze(1).to_broadcast([S, E1, E1]), less[:], ALU.mult))
        chain(dve.tensor_reduce(start[:], lt[:], AX.X, ALU.add))
        dve.tensor_tensor(rank[:], src, cnt[:], ALU.subtract).then_inc(chosen.sem, 1)
        dve.wait_ge(chosen.sem, 2)
        dve.tensor_tensor(rank[:], pd[:S, 0:BE].rearrange("s (b e) -> s b e", b=B), rank[:], ALU.add).then_inc(chosen.sem, 1)
        dve.wait_ge(chosen.sem, 3)
        dve.tensor_scalar(first[:], start[:], float(P), None, ALU.mult).then_inc(chosen.sem, 1)
        dve.wait_ge(chosen.sem, 4)
        dve.tensor_tensor(rank[:], rank[:], first[:, :].unsqueeze(1).to_broadcast([S, B, E1]), ALU.add).then_inc(chosen.sem, 1)
        dve.wait_ge(chosen.sem, 5)
        dve.tensor_tensor(rank[:], rank[:], oh[:], ALU.mult).then_inc(chosen.sem, 1)
        dve.wait_ge(chosen.sem, 6)
        dve.tensor_reduce(place[:], rank[:], AX.X, ALU.add).then_inc(chosen.sem, 1)
        dve.wait_ge(chosen.sem, 7)
        chain(dve.tensor_copy(place_i[:], place[:]))
        chain(dve.tensor_tensor(end[:], start[:], tiles[:], ALU.add))
        chain(dve.tensor_tensor(passed[:], end[:, :].unsqueeze(1).to_broadcast([S, MT, E1]), tj[:], ALU.is_le))   
        chain(dve.tensor_reduce(texp[:], passed[:], AX.X, ALU.add))
        chain(dve.tensor_scalar(texp_i[:], texp[:], float(E1 - 1), None, ALU.min))

        def turned(j, par, first):
            dve.wait_ge(t_pe.sem, j + 1)
            if not first:
                dve.wait_ge(up_a.sem, j - 1)
            dve.tensor_copy(xT[:, par].rearrange("p c s -> p (c s)"), pt[:, 0:DC * P]).then_inc(t_up.sem, 1)

        def results(j, i, q):
            dve.wait_ge(y_pe.sem, j + 1)
            dve.wait_ge(x_in[q].sem, 16 * (i + 1))
            if not is_early(j, 2):
                dve.wait_ge(y_out[(q - 2) % RING].sem, 16 * (i + (q - 2) // RING + 1))
            dve.tensor_tensor(ysb[:, q % 2, :], py[:, 0:D], xt[:, q, D:2 * D], ALU.add).then_inc(y_up.sem, 1)

        def body(j, i, q):
            par = q % 2
            dve.wait_ge(thd.sem, j + 1)
            if not is_early(j, 2):
                dve.wait_ge(z_pe.sem, j - 1)
            dve.scalar_tensor_tensor(out=u[:, par, :], in0=th[:, par, :], scalar=1.0, in1=ph[:, par, 1, :],
                                     op0=ALU.add, op1=ALU.mult).then_inc(lnd.sem, 1)
            dve.wait_ge(lnd.sem, j + B + 3)
            dve.wait_ge(up_a.sem, j + 1)
            dve.scalar_tensor_tensor(out=u[:, par, :], in0=u[:, par, :], scalar=0.5, in1=ph[:, par, 0, :],
                                     op0=ALU.mult, op1=ALU.mult).then_inc(gated.sem, 1)
            if not is_last(j):
                turned(j + 1, 1 - par, is_early(j, 1))
            if not is_early(j, 1):
                results(j - 1, i + (q - 1) // RING, (q - 1) % RING)

        turned(0, 0, True)
        tiles_loop(dve, body)
        results(MT - 1, (MT - 1) // RING, 0)

    @block.gpsimd
    def _(pool):
        pool.memset(onesf[:], 1.0).then_inc(made.sem, 1)
        pool.memset(onesb[:], 1.0).then_inc(made.sem, 1)
        pool.memset(before[:], 1.0).then_inc(made.sem, 1)
        pool.memset(less[:], 1.0).then_inc(made.sem, 1)
        pool.wait_ge(made.sem, 4)
        pool.affine_select(out=before[:], in_=before[:], compare_op=ALU.is_gt, fill=0.0, base=0,
                           pattern=[[1, S]], channel_multiplier=-1).then_inc(made.sem, 1)
        pool.affine_select(out=less[:], in_=less[:], compare_op=ALU.is_gt, fill=0.0, base=0,
                           pattern=[[1, E1], [-1, E1]], channel_multiplier=0).then_inc(made.sem, 1)
        pool.iota(rank_e[:], [[-1, E1]], base=E1, channel_multiplier=0, allow_small_or_imprecise_dtypes=True).then_inc(made.sem, 1)
        pool.iota(kk[:], [[0, E1], [P, B * S // P]], base=0, channel_multiplier=0, allow_small_or_imprecise_dtypes=True).then_inc(made.sem, 1)
        pool.iota(tj[:], [[1, MT], [0, E1]], base=0, channel_multiplier=0, allow_small_or_imprecise_dtypes=True).then_inc(made.sem, 1)
        pool.iota(rows[:, :, 2 * D].bitcast(U32), [[S, B]], base=0, channel_multiplier=1).then_inc(made.sem, 1)
        pool.sem_inc(kept.sem, 2)
        with pool.Fori(0, B // 2) as j:
            for par in range(2):
                b = 2 * j + par
                pool.wait_ge(lnd.sem, b + 3)
                pool.sem_inc(apart.sem, 1)
                pool.tensor_tensor(rows[:, b, D:2 * D], x_all[:, b, :], xl[:, par, :], ALU.add).then_inc(kept.sem, 1)
        pool.wait_ge(t["zeroed"].sem, 16)
        pool.wait_ge(v.sem, 19)
        pool.wait_ge(made.sem, 10)
        pool.wait_ge(xnk.sem, B + 2)
        pool.wait_ge(kept.sem, B + 2)
        for b in range(B):
            pool.indirect_dma_start(out=xs, out_offset=bass.IndirectOffsetOnAxis(ap=place_i[:, b:b + 1], axis=0),
                                    in_=rows[:, b, :], in_offset=None).then_inc(scattered.sem, 16)

        def body(j, i, q):
            pool.wait_ge(y_up.sem, j + 1)
            pool.sem_inc(apart.sem, 1)
            pool.indirect_dma_start(out=out.rearrange("b s d -> (b s) d"),
                                    out_offset=bass.IndirectOffsetOnAxis(ap=xt[:, q, 2 * D:2 * D + 1].bitcast(U32), axis=0),
                                    in_=ysb[:, q % 2, :], in_offset=None, bounds_check=B * S - 1,
                                    oob_is_err=False).then_inc(y_out[q].sem, 16)
        tiles_loop(pool, body)


def program(nc, a, out):
    with ExitStack() as ctx:
        def sb(c, name, shape, dt=F32):
            return c.enter_context(nc.sbuf_tensor(name, shape, dt))

        def sig(name, per=1):
            return Sig(ctx.enter_context(nc.semaphore(name)), per)

        down = sb(ctx, "down", [P, E1, F1 // P, D])
        place, w = down[:, :, :, :].rearrange("p e f d -> p (e f d)"), DC * E0 * F0
        t = {"x_all": sb(ctx, "x_all", [S, B, D]), "ident": sb(ctx, "ident", [P, P]), "down": down,
             "w1": place[:, 0:w].rearrange("p (c n) -> p c n", c=DC),
             "w2": place[:, w:w + E0 * D].rearrange("p (e d) -> p e d", e=E0),
             "xnT_all": place[:, w + E0 * D:w + E0 * D + DC * B * S].rearrange("p (c s) -> p c s", c=DC),
             "mean": sb(ctx, "mean", [S, B]), "roots": sb(ctx, "roots", [S, 2, B]),
             "rows_by_place": nc.dram_tensor("rows_by_place", [MT * P, PLACE_ROW], F32).ap(),
             "slot_w_in": sig("slot_w_in"), "c_in0": sig("c_in0", 16 * (KT + 1) * GB),
             "down_in": sig("down_in"), "zeroed": sig("zeroed")}
        with ExitStack() as slots:
            t.update({name: sb(slots, name, shape) for name, shape in SLOT_WEIGHTS.items()})
            t.update({"wqk": sb(slots, "wqk", [P, DC, D]), "brz": sb(slots, "brz", [P, 4])})
            t.update({name: [sb(slots, f"{name}_{part}", [P, DC, 3 * D], F32R) for part in ("hi", "lo")] for name in ("wg", "wh")})
            t.update({name: sb(slots, name, [KP, B * KT]) for name in ("row_root", "row_rms")})
            t.update({"cx0": sb(slots, "cx0", [KP, GB, KT, D + 1]), "cT0": sb(slots, "cT0", [P, GB, DC, KEYS])})
            with ExitStack() as dense:
                t.update({"gates": sb(dense, "gates", [S, B, E0]), "b1": sb(dense, "b1", [P, E0])})
                for phase in (phase_1, phase_2):
                    with ExitStack() as own:
                        phase(nc, own, a, t)
                    nc.all_engine_barrier()
            with ExitStack() as own:
                phase_3(nc, own, a, t)
            nc.all_engine_barrier()
        with ExitStack() as own:
            phase_4(nc, own, a, t, out)


def lay_out(**x):
    import numpy as np
    x = {k: np.asarray(v) for k, v in x.items()}
    c = np.ascontiguousarray

    def heads(w):
        return c(w.transpose(1, 0, 2).reshape(D, H * DK))

    def padded(w):
        w = w.reshape(H, DK, -1)
        return c(np.concatenate([w, np.zeros((H, HP - DK, w.shape[2]), w.dtype)], 1).reshape(H * HP, -1))

    def columns(v):
        return c(v.reshape(-1, P).T)

    return {
        "x": c(x["x"]),
        "ctx": c(x["ctx_1024"]),
        "ctxT": c(x["ctx_1024"].transpose(0, 2, 1)),
        "mask": c(x["mask_BxSxS2_bk1"]),
        "wq": heads(x["L0_xattn_Wq"]), "wk": heads(x["L0_xattn_Wk"]), "wv": heads(x["L0_xattn_Wv"]),
        "bq": columns(x["L0_xattn_bq"].reshape(-1)), "bk": columns(x["L0_xattn_bk"].reshape(-1)),
        "bv": columns(padded(x["L0_xattn_bv"].reshape(-1, 1)).reshape(-1)),
        "wo": padded(x["L0_xattn_Wo"]), "bo": c(x["L0_xattn_bo"]),
        "w1": c(x["L0_ffn_w1"].transpose(1, 0, 2).reshape(D, E0 * F0)), "b1": c(x["L0_ffn_b1"].T),
        "w2": c(x["L0_ffn_w2"]), "b2": c(x["L0_ffn_b2"]), "cent": c(x["L0_ffn_centroids"]),
        "w_routeT": c(x["L0_ffn_w_route"].T),
        "xwq": c(x["L1_xattn_Wq"]), "xwk": c(x["L1_xattn_Wk"]), "xwv": c(x["L1_xattn_Wv"]),
        "wihT": c(x["L1_xattn_gru_wih"].T), "whhT": c(x["L1_xattn_gru_whh"].T),
        "bih": columns(x["L1_xattn_gru_bih"]), "bhh": columns(x["L1_xattn_gru_bhh"]),
        "slot_w": columns(x["L1_xattn_slot_norm_w"]), "in_w": columns(x["L1_xattn_input_norm_w"]), 
        "in_w_row": c(x["L1_xattn_input_norm_w"].reshape(1, D)),
        "scale": c(x["L1_ffn_scale"].reshape(1, D)), "centT": c(x["L1_ffn_centroids"].T), "cent1": c(x["L1_ffn_centroids"]),
        "up": c(x["L1_ffn_up_w"]), "down": c(x["L1_ffn_down_w"]),
    }


def kernel(**inputs):
    import numpy as np
    import concourse.bacc as bacc
    from concourse import mybir as _mybir
    from concourse.bass_utils import run_bass_kernel_spmd

    nc = bacc.Bacc("TRN2", target_bir_lowering=False, num_devices=1)
    arrays, aps = {}, {}
    for name, array in lay_out(**inputs).items():
        arrays[f"in_{name}_dram"] = array
        aps[name] = nc.dram_tensor(f"in_{name}_dram", array.shape, _mybir.dt.from_np(array.dtype), kind="ExternalInput").ap()
    out = nc.dram_tensor("out_0_dram", (B, S, D), _mybir.dt.from_np(np.dtype("float32")), kind="ExternalOutput").ap()
    program(nc, aps, out)
    result = run_bass_kernel_spmd(nc, [arrays], core_ids=[0])
    return result.results[0]["out_0_dram"]
```
